# Optimizing a Trainium2 kernel written in Bass

```python
import numpy as np
import jax
import jax.numpy as jnp

def _softmax(x, axis=-1):
    return jax.nn.softmax(x, axis=axis)

def _gelu(x):
    return jax.nn.gelu(x, approximate=True)

def _silu(x):
    return jax.nn.silu(x)

def _sigmoid(x):
    return jax.nn.sigmoid(x)

def _layernorm(x, axis=-1, eps=1e-05):
    m = jnp.mean(x, axis=axis, keepdims=True)
    v = jnp.var(x, axis=axis, keepdims=True)
    return (x - m) / jnp.sqrt(v + eps)

def _scatter_add(tgt, idx, src, axis=0):
    return tgt.at[idx].add(src)

def _segment_sum(src, seg, n):
    return jax.ops.segment_sum(src, seg, n)
kernel_name = 'mk_gnn_preln_d4_gnn_r8_5c6352'

def setup_inputs(seed: int=0):
    np.random.seed(seed)
    _w = jnp.asarray

    def _rec_inputs():
        import jax
        import jax.numpy as jnp
        _gk = jax.random.key(seed)
        x = -0.0001126 + 1 * jax.random.normal(jax.random.fold_in(_gk, 1), (3750, 256), jnp.float32)
        _s = jax.random.randint(jax.random.fold_in(_gk, 2), (30000,), 0, 3750, jnp.int32)
        _d = jax.random.randint(jax.random.fold_in(_gk, 3), (30000,), 0, 3750, jnp.int32)
        _loop = jnp.arange(3750, dtype=jnp.int32)
        src = jnp.concatenate([_s, _d, _loop])
        dst = jnp.concatenate([_d, _s, _loop])
        _o = jnp.argsort(dst, stable=True)
        src = src[_o]
        dst = dst[_o]
        edge_attr_64 = 0.000279952 + 1.00013 * jax.random.normal(jax.random.fold_in(_gk, 13), (63750, 64), jnp.float32)
        edge_type_8 = jax.random.randint(jax.random.fold_in(_gk, 15), (63750,), 0, 8, jnp.int32)
        return (x, src, dst, edge_attr_64, edge_type_8)
    x, src, dst, edge_attr_64, edge_type_8 = _rec_inputs()

    def _L0_gnn_setup():
        import jax, jax.numpy as jnp
        import numpy as np
        N_NODES = 3750
        N_EDGES = 60000
        IN_FEAT = 256
        OUT_FEAT = 256
        N_RELS = 8
        N_HEADS = 4
        HEAD_DIM = OUT_FEAT // N_HEADS
        LEAKY_SLOPE = 0.2
        key = jax.random.key(seed)
        ks = jax.random.split(key, 8)
        inputs = jax.random.normal(ks[0], (N_NODES, IN_FEAT), dtype=jnp.float32)
        conv_weights = jax.random.normal(ks[1], (N_RELS, N_HEADS, IN_FEAT, HEAD_DIM), dtype=jnp.float32) * (1.0 / np.sqrt(IN_FEAT))
        attn_l = jax.random.normal(ks[2], (N_RELS, N_HEADS, HEAD_DIM), dtype=jnp.float32) * 0.1
        attn_r = jax.random.normal(ks[3], (N_RELS, N_HEADS, HEAD_DIM), dtype=jnp.float32) * 0.1
        h_bias = jax.random.normal(ks[4], (OUT_FEAT,), dtype=jnp.float32) * 0.02
        edge_src = jax.random.randint(ks[5], (N_EDGES,), 0, N_NODES, dtype=jnp.int32)
        edge_dst = jax.random.randint(ks[6], (N_EDGES,), 0, N_NODES, dtype=jnp.int32)
        edge_type = jax.random.randint(ks[7], (N_EDGES,), 0, N_RELS, dtype=jnp.int32)
        return {'inputs': inputs, 'conv_weights': conv_weights, 'attn_l': attn_l, 'attn_r': attn_r, 'h_bias': h_bias, 'edge_src': edge_src, 'edge_dst': edge_dst, 'edge_type': edge_type}
    _L0_gnn_all = _L0_gnn_setup()
    _L0_gnn_in = {k: v for k, v in _L0_gnn_all.items() if k in ('conv_weights', 'attn_l', 'attn_r', 'h_bias')}
    del _L0_gnn_all

    def _L1_gnn_setup():
        import jax, jax.numpy as jnp
        import numpy as np
        N_NODES = 12500
        N_EDGES = 400000
        IN_CH = 256
        N_CLUSTERS = 10

        def _gcn_conv(h, W, bias, edge_index, n_nodes):
            h = h @ W
            loop = jnp.arange(n_nodes, dtype=edge_index.dtype)
            src = jnp.concatenate([edge_index[0], loop])
            dst = jnp.concatenate([edge_index[1], loop])
            deg = jax.ops.segment_sum(jnp.ones_like(dst, dtype=h.dtype), dst, num_segments=n_nodes)
            dinv = jnp.where(deg > 0, jax.lax.rsqrt(deg), 0.0)
            norm = dinv[src] * dinv[dst]
            msg = h[src] * norm[:, None]
            out = jax.ops.segment_sum(msg, dst, num_segments=n_nodes)
            return out + bias
        key = jax.random.key(seed)
        k1, k2, k3, k4 = jax.random.split(key, 4)
        x = jax.random.normal(k1, (N_NODES, IN_CH), dtype=jnp.float32)
        edge_index = jax.random.randint(k2, (2, N_EDGES), 0, N_NODES, dtype=jnp.int64)
        batch = jnp.zeros((N_NODES,), dtype=jnp.int64)
        W = jax.random.normal(k3, (IN_CH, N_CLUSTERS), dtype=jnp.float32) * (1.0 / np.sqrt(IN_CH))
        bias = jnp.zeros((N_CLUSTERS,), dtype=jnp.float32)
        cluster_emb = jax.random.normal(k4, (N_CLUSTERS, IN_CH), dtype=jnp.float32) * 0.1
        return {'x': x, 'edge_index': edge_index, 'batch': batch, 'W': W, 'bias': bias, 'cluster_emb': cluster_emb}
    _L1_gnn_all = _L1_gnn_setup()
    _L1_gnn_in = {k: v for k, v in _L1_gnn_all.items() if k in ('W', 'bias', 'cluster_emb')}
    del _L1_gnn_all

    def _L2_gnn_setup():
        import jax, jax.numpy as jnp
        import numpy as np
        N = 12500
        E = 40000
        CIN = 256
        EDIM = 64
        EEMB = 256
        H = 1024
        LN_EPS = 1e-05

        def _ln(x, g, b):
            m = jnp.mean(x, axis=-1, keepdims=True)
            v = jnp.var(x, axis=-1, keepdims=True)
            return (x - m) * jax.lax.rsqrt(v + LN_EPS) * g + b
        key = jax.random.key(seed)
        ks = jax.random.split(key, 16)

        def w(k, i, o):
            return (jax.random.normal(k, (i, o), jnp.float32) / np.sqrt(i)).astype(jnp.float32)
        return {'x': jax.random.normal(ks[0], (N, CIN), jnp.float32), 'edge_index': jax.random.randint(ks[1], (2, E), 0, N, dtype=jnp.int64), 'edge_attr': jax.random.normal(ks[2], (E, EDIM), jnp.float32), 'eps': jnp.float32(0.0), 'ee_w1': w(ks[3], EDIM, EEMB), 'ee_b1': jnp.zeros((EEMB,), jnp.float32), 'ee_w2': w(ks[4], EEMB, CIN), 'ee_b2': jnp.zeros((CIN,), jnp.float32), 'w1': w(ks[5], CIN, H), 'b1': jnp.zeros((H,), jnp.float32), 'g1': jnp.ones((H,), jnp.float32), 'be1': jnp.zeros((H,), jnp.float32), 'w2': w(ks[6], H, H), 'b2': jnp.zeros((H,), jnp.float32), 'g2': jnp.ones((H,), jnp.float32), 'be2': jnp.zeros((H,), jnp.float32), 'w3': w(ks[7], H, CIN), 'b3': jnp.zeros((CIN,), jnp.float32), 'bn_g': jnp.ones((CIN,), jnp.float32), 'bn_b': jnp.zeros((CIN,), jnp.float32)}
    _L2_gnn_all = _L2_gnn_setup()
    _L2_gnn_in = {k: v for k, v in _L2_gnn_all.items() if k in ('eps', 'ee_w1', 'ee_b1', 'ee_w2', 'ee_b2', 'w1', 'b1', 'g1', 'be1', 'w2', 'b2', 'g2', 'be2', 'w3', 'b3', 'bn_g', 'bn_b')}
    del _L2_gnn_all

    def _L3_gnn_setup():
        import jax, jax.numpy as jnp
        import numpy as np
        EPS = 1e-05
        N_NODES = 1250
        N_EDGES = 40000
        D_IN = 256
        D_OUT = 256
        key = jax.random.key(seed)
        k_x, k_e, k_wl, k_bl, k_wr = jax.random.split(key, 5)
        x = jax.random.normal(k_x, (N_NODES, D_IN), dtype=jnp.float32)
        edge_index = jax.random.randint(k_e, (2, N_EDGES), 0, N_NODES, dtype=jnp.int64)
        gamma = jnp.ones((D_IN,), dtype=jnp.float32)
        beta = jnp.zeros((D_IN,), dtype=jnp.float32)
        s = 1.0 / np.sqrt(D_IN)
        W_l = jax.random.uniform(k_wl, (D_OUT, D_IN), dtype=jnp.float32, minval=-s, maxval=s)
        b_l = jax.random.uniform(k_bl, (D_OUT,), dtype=jnp.float32, minval=-s, maxval=s)
        W_r = jax.random.uniform(k_wr, (D_OUT, D_IN), dtype=jnp.float32, minval=-s, maxval=s)
        return {'x': x, 'edge_index': edge_index, 'gamma': gamma, 'beta': beta, 'W_l': W_l, 'b_l': b_l, 'W_r': W_r}
    _L3_gnn_all = _L3_gnn_setup()
    _L3_gnn_in = {k: v for k, v in _L3_gnn_all.items() if k in ('gamma', 'beta', 'W_l', 'b_l', 'W_r')}
    del _L3_gnn_all
    return {'x': x, 'src': src, 'dst': dst, 'edge_attr_64': edge_attr_64, 'edge_type_8': edge_type_8, 'L0_gnn_conv_weights': _L0_gnn_in['conv_weights'], 'L0_gnn_attn_l': _L0_gnn_in['attn_l'], 'L0_gnn_attn_r': _L0_gnn_in['attn_r'], 'L0_gnn_h_bias': _L0_gnn_in['h_bias'], 'L1_gnn_W': _L1_gnn_in['W'], 'L1_gnn_bias': _L1_gnn_in['bias'], 'L1_gnn_cluster_emb': _L1_gnn_in['cluster_emb'], 'L2_gnn_eps': _L2_gnn_in['eps'], 'L2_gnn_ee_w1': _L2_gnn_in['ee_w1'], 'L2_gnn_ee_b1': _L2_gnn_in['ee_b1'], 'L2_gnn_ee_w2': _L2_gnn_in['ee_w2'], 'L2_gnn_ee_b2': _L2_gnn_in['ee_b2'], 'L2_gnn_w1': _L2_gnn_in['w1'], 'L2_gnn_b1': _L2_gnn_in['b1'], 'L2_gnn_g1': _L2_gnn_in['g1'], 'L2_gnn_be1': _L2_gnn_in['be1'], 'L2_gnn_w2': _L2_gnn_in['w2'], 'L2_gnn_b2': _L2_gnn_in['b2'], 'L2_gnn_g2': _L2_gnn_in['g2'], 'L2_gnn_be2': _L2_gnn_in['be2'], 'L2_gnn_w3': _L2_gnn_in['w3'], 'L2_gnn_b3': _L2_gnn_in['b3'], 'L2_gnn_bn_g': _L2_gnn_in['bn_g'], 'L2_gnn_bn_b': _L2_gnn_in['bn_b'], 'L3_gnn_gamma': _L3_gnn_in['gamma'], 'L3_gnn_beta': _L3_gnn_in['beta'], 'L3_gnn_W_l': _L3_gnn_in['W_l'], 'L3_gnn_b_l': _L3_gnn_in['b_l'], 'L3_gnn_W_r': _L3_gnn_in['W_r']}

def reference(x, src, dst, edge_attr_64, edge_type_8, L0_gnn_conv_weights, L0_gnn_attn_l, L0_gnn_attn_r, L0_gnn_h_bias, L1_gnn_W, L1_gnn_bias, L1_gnn_cluster_emb, L2_gnn_eps, L2_gnn_ee_w1, L2_gnn_ee_b1, L2_gnn_ee_w2, L2_gnn_ee_b2, L2_gnn_w1, L2_gnn_b1, L2_gnn_g1, L2_gnn_be1, L2_gnn_w2, L2_gnn_b2, L2_gnn_g2, L2_gnn_be2, L2_gnn_w3, L2_gnn_b3, L2_gnn_bn_g, L2_gnn_bn_b, L3_gnn_gamma, L3_gnn_beta, L3_gnn_W_l, L3_gnn_b_l, L3_gnn_W_r):
    import jax
    import jax.numpy as jnp

    def _L0_gnn_ref(inputs, conv_weights, attn_l, attn_r, h_bias, edge_src, edge_dst, edge_type):
        import jax, jax.numpy as jnp
        import numpy as np
        N_NODES = 3750
        N_EDGES = 60000
        IN_FEAT = 256
        OUT_FEAT = 256
        N_RELS = 8
        N_HEADS = 4
        HEAD_DIM = OUT_FEAT // N_HEADS
        LEAKY_SLOPE = 0.2
        feat_all = jnp.einsum('ni,rhid->rnhd', inputs, conv_weights)
        feat_src_e = feat_all[edge_type, edge_src]
        feat_dst_e = feat_all[edge_type, edge_dst]
        el = jnp.sum(feat_src_e * attn_l[edge_type], axis=-1)
        er = jnp.sum(feat_dst_e * attn_r[edge_type], axis=-1)
        e = jax.nn.leaky_relu(el + er, negative_slope=LEAKY_SLOPE)
        m = jax.ops.segment_max(e, edge_dst, num_segments=N_NODES)
        ex = jnp.exp(e - m[edge_dst])
        denom = jax.ops.segment_sum(ex, edge_dst, num_segments=N_NODES)
        alpha = ex / denom[edge_dst]
        h = jax.ops.segment_sum(alpha[..., None] * feat_src_e, edge_dst, num_segments=N_NODES)
        h = h.reshape(N_NODES, OUT_FEAT) + h_bias
        return h

    def _L1_gnn_ref(x, edge_index, batch, W, bias, cluster_emb):
        import jax, jax.numpy as jnp
        import numpy as np
        N_NODES = 12500
        N_EDGES = 400000
        IN_CH = 256
        N_CLUSTERS = 10

        def _gcn_conv(h, W, bias, edge_index, n_nodes):
            h = h @ W
            loop = jnp.arange(n_nodes, dtype=edge_index.dtype)
            src = jnp.concatenate([edge_index[0], loop])
            dst = jnp.concatenate([edge_index[1], loop])
            deg = jax.ops.segment_sum(jnp.ones_like(dst, dtype=h.dtype), dst, num_segments=n_nodes)
            dinv = jnp.where(deg > 0, jax.lax.rsqrt(deg), 0.0)
            norm = dinv[src] * dinv[dst]
            msg = h[src] * norm[:, None]
            out = jax.ops.segment_sum(msg, dst, num_segments=n_nodes)
            return out + bias
        n_nodes = x.shape[0]
        h = x + jnp.sum(cluster_emb, axis=0)
        logits = _gcn_conv(h, W, bias, edge_index, n_nodes)
        s = jax.nn.softmax(logits, axis=1)
        p = s @ cluster_emb
        return x + p

    def _L2_gnn_ref(x, edge_index, edge_attr, eps, ee_w1, ee_b1, ee_w2, ee_b2, w1, b1, g1, be1, w2, b2, g2, be2, w3, b3, bn_g, bn_b):
        import jax, jax.numpy as jnp
        import numpy as np
        N = 12500
        E = 40000
        CIN = 256
        EDIM = 64
        EEMB = 256
        H = 1024
        LN_EPS = 1e-05

        def _ln(x, g, b):
            m = jnp.mean(x, axis=-1, keepdims=True)
            v = jnp.var(x, axis=-1, keepdims=True)
            return (x - m) * jax.lax.rsqrt(v + LN_EPS) * g + b
        n = x.shape[0]
        sl = jnp.arange(n, dtype=edge_index.dtype)
        ei = jnp.concatenate([edge_index, jnp.stack([sl, sl], axis=0)], axis=1)
        ea = jnp.concatenate([edge_attr, jnp.zeros((n, edge_attr.shape[1]), edge_attr.dtype)], axis=0)
        src, dst = (ei[0], ei[1])
        e = jax.nn.relu(ea @ ee_w1 + ee_b1) @ ee_w2 + ee_b2
        msg = x[src] + e
        agg = jax.ops.segment_sum(msg, dst, num_segments=n)
        h = (1.0 + eps) * x + agg
        h = jax.nn.relu(_ln(h @ w1 + b1, g1, be1))
        h = jax.nn.relu(_ln(h @ w2 + b2, g2, be2))
        y = h @ w3 + b3
        out = x + y
        out = _ln(out, bn_g, bn_b)
        return jax.nn.relu(out)

    def _L3_gnn_ref(x, edge_index, gamma, beta, W_l, b_l, W_r):
        import jax, jax.numpy as jnp
        import numpy as np
        EPS = 1e-05
        N_NODES = 1250
        N_EDGES = 40000
        D_IN = 256
        D_OUT = 256
        mu = jnp.mean(x, axis=-1, keepdims=True)
        var = jnp.mean(jnp.square(x - mu), axis=-1, keepdims=True)
        h = (x - mu) * jax.lax.rsqrt(var + EPS) * gamma + beta
        h = jax.nn.relu(h)
        src, dst = (edge_index[0], edge_index[1])
        n = h.shape[0]
        msg = h[src]
        summed = jax.ops.segment_sum(msg, dst, num_segments=n)
        deg = jax.ops.segment_sum(jnp.ones((src.shape[0],), dtype=h.dtype), dst, num_segments=n)
        agg = summed / jnp.maximum(deg, 1.0)[:, None]
        return agg @ W_l.T + b_l + h @ W_r.T
    edge_index = jnp.stack([src, dst])
    batch0 = jnp.zeros((3750,), jnp.int32)
    h = jnp.maximum(_layernorm(x, axis=-1), 0.0)
    x = x + _L0_gnn_ref(h, L0_gnn_conv_weights, L0_gnn_attn_l, L0_gnn_attn_r, L0_gnn_h_bias, src, dst, edge_type_8)
    h = jnp.maximum(_layernorm(x, axis=-1), 0.0)
    x = x + _L1_gnn_ref(h, edge_index, batch0, L1_gnn_W, L1_gnn_bias, L1_gnn_cluster_emb)
    h = jnp.maximum(_layernorm(x, axis=-1), 0.0)
    x = x + _L2_gnn_ref(h, edge_index, edge_attr_64, L2_gnn_eps, L2_gnn_ee_w1, L2_gnn_ee_b1, L2_gnn_ee_w2, L2_gnn_ee_b2, L2_gnn_w1, L2_gnn_b1, L2_gnn_g1, L2_gnn_be1, L2_gnn_w2, L2_gnn_b2, L2_gnn_g2, L2_gnn_be2, L2_gnn_w3, L2_gnn_b3, L2_gnn_bn_g, L2_gnn_bn_b)
    h = jnp.maximum(_layernorm(x, axis=-1), 0.0)
    x = x + _L3_gnn_ref(h, edge_index, L3_gnn_gamma, L3_gnn_beta, L3_gnn_W_l, L3_gnn_b_l, L3_gnn_W_r)
    return x

_drawn_inputs = setup_inputs


def setup_inputs(seed=0):
    import zlib

    import numpy as np

    out = dict(_drawn_inputs(seed))
    spreads = {'L1_gnn_bias': (0.0, 2.0),
     'L2_gnn_ee_b1': (0.0, 0.468),
     'L2_gnn_ee_b2': (0.0, 0.293),
     'L2_gnn_b1': (0.0, 2.0),
     'L2_gnn_g1': (1.0, 0.2),
     'L2_gnn_be1': (0.0, 0.336),
     'L2_gnn_b2': (0.0, 0.304),
     'L2_gnn_g2': (1.0, 0.2),
     'L2_gnn_be2': (0.0, 0.375),
     'L2_gnn_b3': (0.0, 0.1),
     'L2_gnn_bn_g': (1.0, 0.2),
     'L2_gnn_bn_b': (0.0, 0.1),
     'L3_gnn_gamma': (1.0, 0.2),
     'L3_gnn_beta': (0.0, 0.52)}
    factors = {'L0_gnn_h_bias': 2.868,
     'L1_gnn_W': 7.094,
     'L1_gnn_cluster_emb': 3.139,
     'L3_gnn_b_l': 3.859}
    for name, (base, spread) in spreads.items():
        noise = np.random.default_rng([zlib.crc32(name.encode()), seed]).standard_normal(out[name].shape)
        drawn = base * np.exp(spread * noise) if base else spread * noise
        out[name] = jnp.asarray(drawn.astype(out[name].dtype))
    for name, factor in factors.items():
        out[name] = (out[name] * factor).astype(out[name].dtype)
    return out
```

```python
from contextlib import ExitStack

import concourse.bass as bass
from concourse import mybir

P = 128
F32 = mybir.dt.float32
BF16 = mybir.dt.bfloat16
I32 = mybir.dt.int32
ALU = mybir.AluOpType
ACT = mybir.ActivationFunctionType
AX = mybir.AxisListType.X
DVE = mybir.EngineType.DVE
PE = mybir.EngineType.PE
BIG = 1e30
LN_EPS = 1e-5


class Steps:

    def __init__(self, eng, sem):
        self.eng, self.sem, self.n, self.u, self.per = eng, sem, 0, None, 0

    def __call__(self, ins):
        self.n += 1
        ins.then_inc(self.sem, 1)
        self.eng.wait_ge(self.sem, self.n if self.u is None else self.u * self.per + self.n)

    def enter(self, u, per):
        self.u, self.per, self.first = u, per, self.n

    def leave(self, trips):
        assert self.n - self.first == self.per, (self.n - self.first, self.per)
        self.n, self.u = self.first + trips * self.per, None


def gnn(nc, x, src, dst, edge_attr, edge_type, conv_w, attn_l, attn_r, h_bias, gcn_w, gcn_b, cluster,
        eps, ee_w1, ee_b1, ee_w2, ee_b2, w1, b1, g1, be1, w2, b2, g2, be2, w3, b3, bn_g, bn_b,
        gamma, beta, w_l, b_l, w_r, out):
    N, D = x.shape
    E = src.shape[0]
    R, H, _, DH = conv_w.shape
    RH = R * H
    K = gcn_w.shape[1]
    HID = w1.shape[1]
    ED = edge_attr.shape[1]
    KH = HID // P
    NT = -(-N // P)
    NJ = NT // 2
    NTAIL = N - (NT - 1) * P
    NPAD = NT * P
    LB, LT = 4, 125
    T = LB * LT
    IT = T // 10
    EFULL = E // P
    ETAIL = E - EFULL * P
    AW = NPAD + 40
    assert D == 2 * P and R * D == 2048 and NT % 2 == 0 and AW >= N + P and T * P >= E and EFULL == T - 2
    PAD_DST = 8000.0

    feat_d = nc.dram_tensor("feat_d", (NPAD, R * D), F32).ap()
    el_d = nc.dram_tensor("el_d", (NPAD, RH), F32).ap()
    y_d = nc.dram_tensor("y_d", (NPAD, K), F32).ap()
    h2_d = nc.dram_tensor("h2_d", (NPAD, D), F32).ap()
    h3_d = nc.dram_tensor("h3_d", (NPAD, D), F32).ap()
    rel_d = nc.dram_tensor("rel_d", (T * P,), BF16).ap()

    with ExitStack() as ctx:
        def sb(name, shape, dt=F32):
            return ctx.enter_context(nc.sbuf_tensor(name, shape, dt))

        def sem(name):
            return ctx.enter_context(nc.semaphore(name))

        PS = ctx.enter_context(nc.psum_tensor("PS", [P, 8, 512], F32))

        X = sb("X", [P, NT, D])
        ACC = sb("ACC", [P, 3, AW])
        HS = sb("HS", [P, 2, AW])
        SL = sb("SL", [P, 10, D])
        OHB = sb("OHB", [P, 1280])
        AL = sb("AL", [P, 2048])
        BG = sb("BG", [P, 15872])
        DREL = sb("DREL", [P, T])
        IDXST = sb("IDXST", [P, T], I32)
        IDXS = sb("IDXS", [P, T], I32)
        BASE = sb("BASE", [1, T], I32)
        IX = sb("IX", [P, 2, 5], I32)
        IDENT = sb("IDENT", [P, P])
        IOTA = sb("IOTA", [P, P])
        IOTP = sb("IOTP", [P, 2])
        EPSC = sb("EPSC", [P, 1])
        W1A = sb("W1A", [ED + 1, D])
        EW2 = sb("EW2", [P, 2, D])
        GW = sb("GW", [P, 2, K])
        CE = sb("CE", [K, D])
        CW = sb("CW", [P, K])
        GB = sb("GB", [P, K])
        STAT = sb("STAT", [P, 2, 12])
        XST = sb("XST", [P, NT, 6])
        MV = sb("MV", [P, NT, 2])
        RS = sb("RS", [P, NT])
        NB = sb("NB", [P, NT])
        DG = sb("DG", [P, NT])
        COL = sb("COL", [P, 16])
        COL8 = sb("COL8", [P, 4, KH])
        SM = sb("SM", [P, 2, 8])
        REP = sb("REP", [LT, 2, LB, H])
        QEC = sb("QEC", [LT, 2, LB, H])
        QC = sb("QC", [LT, 4, LB])
        QI = sb("QI", [LT, 2, LB], I32)
        ALS = sb("ALS", [P, 2, 20])
        ONES = sb("ONES", [P, P])
        B2C, B1C, CSUM, CB2, SC2 = COL[:, 0:2], COL[:, 2:4], COL[:, 4:6], COL[:, 6:8], COL[:, 8:9]

        ACF = ACC[:, :, :].rearrange("p a n -> p (a n)")
        HSF = HS[:, :, :].rearrange("p a n -> p (a n)")
        SLF = SL[:, :, :].rearrange("p a n -> p (a n)")
        WALL = ACF[:, 0:4096].rearrange("p (c n) -> p c n", c=2)
        STAGE = ACF[:, 4096:8192].rearrange("p (i n) -> p i n", i=2)
        ATT = STAGE
        MF, MB, MFN, MBN = (ACF[0:LT, 8192 + 512 * i:8704 + 512 * i] for i in range(4))
        TF, STF = (ACF[0:LT, 10240 + 512 * i:10752 + 512 * i] for i in range(2))
        RELQ = ACF[0:LT, 11264:11520].bitcast(BF16)
        DI, SI, TI = (SLF[0:LT, 512 * i:512 * i + 512].bitcast(I32) for i in range(3))
        DF, SF = (SLF[0:LT, 1536 + 512 * i:2048 + 512 * i] for i in range(2))
        RELF = SLF[0:LT, 0:512]
        TM = HSF[:, 0:T * R].rearrange("p (t r) -> p t r", r=R)
        OHT = HSF[:, 4000:6560].rearrange("p (h q e) -> p h q e", h=2, q=2)
        ELS = HSF[:, 6560:6560 + NT * RH].rearrange("p (t r) -> p t r", r=RH)
        EF, EB, EX = (HSF[0:LT, 2048 * i:2048 * i + 2048].rearrange("p (h n) -> p h n", h=H) for i in range(3))
        HT = BG[:, 0:2 * NPAD].rearrange("p (c n) -> p c n", c=2)
        SA = BG[:, 2 * NPAD:15872]
        ELA = SA[:, 0:T * H]
        FS, BS = (SA[0:LT, 2048 * i + 2048:2048 * i + 4096].rearrange("p (h n) -> p h n", h=H) for i in range(2))
        RB = SA[:, 6144:6784].bitcast(BF16).rearrange("p (h e) -> p h e", h=2)
        QR = SA[0:1, 6784:6784 + T].bitcast(I32)
        TMP = SA[:, 7300:7620].rearrange("p (h n) -> p h n", h=2)
        ER = SA[:, 2048:2048 + (NT + 1) * RH]
        AW_ = SA[:, 3072:3200].rearrange("p (c n) -> p c n", c=2)
        QE = QEC[:, :, :, :]
        ROWS = [HT[0:H, 0, 512 * i:512 * i + T + 1] for i in range(7)] + \
               [HT[0:H, 1, 512 * i:512 * i + T + 1] for i in range(7)]

        CF, CBK = ROWS[11:13]

        AR = OHB[:, 0:768].rearrange("p (i n) -> p i n", i=2)
        HR = OHB[:, 768:1280].rearrange("p (i n) -> p i n", i=2)
        HTR = BG[:, 15360:15872].rearrange("p (i c n) -> p i c n", i=2, c=2)
        HB = AL[:, 0:D]
        OH = OHB[:, :].rearrange("p (k n) -> p k n", k=10)
        EA = AL[:, 0:384].rearrange("p (h k n) -> p h k n", h=2, k=3)
        HM = AL[:, 384:640]
        EAT = AL[0:ED + 1, 640:768]
        Y = AL[:, 1024:1024 + NT * K].rearrange("p (t k) -> p t k", k=K)
        Z = AL[:, 1344:1344 + NT * K].rearrange("p (t k) -> p t k", k=K)
        ZM = AL[:, 1664:1664 + NT]
        SR = AL[:, 1700:1720].rearrange("p (i k) -> p i k", i=2)
        STR = AL[0:K, 1724:1980].rearrange("p (i n) -> p i n", i=2)

        W1S = BG[:, 0:2048].rearrange("p (c n) -> p c n", c=2)
        W2S = BG[:, 2048:10240].rearrange("p (c n) -> p c n", c=KH)
        W3S = BG[:, 10240:12288].rearrange("p (c n) -> p c n", c=KH)
        BR = BG[:, 12288:14336].rearrange("p (i n) -> p i n", i=2)
        B3R, GNR, BNR = (BG[:, 14336 + D * i:14336 + D * (i + 1)] for i in range(3))
        ZR = AL[:, :].rearrange("p (i n) -> p i n", i=2)
        H1T = SLF[:, 0:2048].rearrange("p (i c n) -> p i c n", i=2, c=KH)
        HIN = OHB[:, 0:512].rearrange("p (i c n) -> p i c n", i=2, c=2)
        H2R = OHB[:, 512:1024].rearrange("p (i n) -> p i n", i=2)
        WRAW = HSF[:, 0:1024].rearrange("p (w o n) -> p w o n", w=2, o=2)
        WLR = HSF[:, 1024:2048].rearrange("p (w c n) -> p w c n", w=2, c=2)
        GMR, BTR, BLR = (HSF[:, 2048 + D * i:2048 + D * (i + 1)] for i in range(3))

        S = {}

        def s(name):
            if name not in S:
                S[name] = sem(name)
            return S[name]

        gath = [sem(f"gathered{k}") for k in range(10)]

        def mine(eng, ins, name, value):
            ins.then_inc(s(name), 1)
            eng.wait_ge(s(name), value)

        def bc(ap, shape):
            return ap.broadcast_to(shape)

        def rows(d, t):
            return d[bass.ds(t * P, P), :]

        block = ctx.enter_context(nc.Block())

        @block.sync
        def _(sp):
            def load(dst_ap, src_ap, name):
                sp.dma_start(dst_ap, src_ap).then_inc(s(name), 16)

            def row(ap, n):
                return ap.partition_broadcast(n)

            sp.wait_ge(s("edge_pads"), 3)
            for a, t in ((dst, DI), (src, SI), (edge_type, TI)):
                v = t.rearrange("t (b e) -> t b e", b=LB)
                load(v[:, 0:LB - 1, :], a[0:(LB - 1) * LT * P].rearrange("(b t e) -> t b e", b=LB - 1, e=P), "edges_in")
                n = EFULL - (LB - 1) * LT
                load(v[0:n, LB - 1, :], a[(LB - 1) * LT * P:EFULL * P].rearrange("(t e) -> t e", e=P), "edges_in")
                load(v[n:n + 1, LB - 1, 0:ETAIL], a[EFULL * P:E].rearrange("(o e) -> o e", o=1), "edges_in")
            load(X[:, 0:NT - 1, :], x[0:(NT - 1) * P, :].rearrange("(t p) d -> p t d", p=P), "x_in")
            sp.wait_ge(s("x_tail_zero"), 1)
            load(X[0:NTAIL, NT - 1, :], x[(NT - 1) * P:N, :], "x_in")
            for c in range(2):
                load(WALL[:, c, :].rearrange("p (r d) -> p r d", r=RH),
                     conv_w.rearrange("r h i d -> i (r h) d")[c * P:(c + 1) * P], "conv_in")
            load(ATT[:, 0, :], row(attn_l.rearrange("r h d -> (r h d)"), P), "attn_in")
            load(ATT[:, 1, :], row(attn_r.rearrange("r h d -> (r h d)"), P), "attn_in")
            with nc.allow_non_contiguous_dma(reason="small weight columns"):
                load(W1A[0:ED, :], ee_w1, "small_in")
                load(W1A[ED:ED + 1, :], ee_b1.rearrange("(o n) -> o n", o=1), "small_in")
                load(EW2[:, :, :], ee_w2.rearrange("(c p) n -> p c n", p=P), "small_in")
                load(GW[:, :, :], gcn_w.rearrange("(c p) n -> p c n", p=P), "small_in")
                load(CE[:, :], cluster, "small_in")
                load(GB[:, :], row(gcn_b, P), "small_in")
                load(B2C, ee_b2.rearrange("(c p) -> p c", p=P), "small_in")
                load(B1C, ee_b1.rearrange("(c p) -> p c", p=P), "small_in")
                load(SC2, eps.partition_broadcast(P), "small_in")
                for c in range(2):
                    load(ZR[:, 0, c * K:(c + 1) * K], cluster.rearrange("k (c p) -> c p k", p=P)[c], "small_in")
                for i, a in enumerate((g1, be1, g2, be2)):
                    load(COL8[:, i, :], a.rearrange("(c p) -> p c", p=P), "small_in")
            sp.wait_ge(s("relq_ready"), 1)
            load(rel_d.rearrange("(b t e) -> t b e", b=LB, e=P), RELQ.rearrange("t (b e) -> t b e", b=LB), "rel_out")
            sp.wait_ge(s("elr_done"), NT + 2)
            load(el_d.rearrange("(t p) r -> p t r", p=P), ELS, "el_out")
            for i in range(2):
                sp.sem_inc(s(f"stage_out{i}"), 16)
            with sp.Fori(0, NJ) as j:
                for i in range(2):
                    sp.wait_ge(s("tab_free"), (2 * j + i + 1) * 4 + 4)
                    load(rows(feat_d, 2 * j + i), STAGE[:, i, :], f"stage_out{i}")
            sp.wait_ge(s("rel_out"), 16)
            with sp.Fori(0, IT) as u:
                for h in range(2):
                    sp.wait_ge(s("oht_ready"), 2 * u + h + 1)
                    load(RB[:, h, :], rel_d[bass.ds((10 * u + 5 * h) * P, 5 * P)].partition_broadcast(P), f"rb_in{h}")
            sp.wait_ge(s("msg_ready"), T)
            load(HB, row(h_bias, P), "hb_in")
            sp.wait_ge(s("y_ready"), 1)
            load(y_d.rearrange("(t p) k -> p t k", p=P), Y, "y_out")
            load(W1S, w1.rearrange("(c p) n -> p c n", p=P), "mlp_in")
            load(W2S, w2.rearrange("(c p) n -> p c n", p=P), "mlp_in")
            load(W3S, w3.rearrange("(c p) n -> p c n", p=P), "mlp_in")
            for t, a in ((BR[:, 0, :], b1), (BR[:, 1, :], b2), (B3R, b3), (GNR, bn_g), (BNR, bn_b)):
                load(t, row(a, P), "mlp_in")

            ea_even = edge_attr[0:EFULL * P, :].rearrange("(v q p) f -> p v q f", q=2, p=P)

            def edge_rows(par, u, last):
                n0 = 3 - par
                sp.wait_ge(s("ea_used"), IT * 5 * par + 5 * u + n0)
                load(EA[:, 0, 0:n0, :], ea_even[:, bass.ds(5 * u, n0), par, :], "ea_in0")
                sp.wait_ge(s("ea_used"), IT * 5 * par + 5 * u + 5)
                n1 = 4 - n0
                load(EA[:, 1, 0:n1, :], ea_even[:, bass.ds(5 * u + n0, n1), par, :], "ea_in1")
                if not last:
                    load(EA[:, 1, n1, :], ea_even[:, bass.ds(5 * u + 4, 1), par, :], "ea_in1")
                elif par == 0:
                    load(EA[0:ETAIL, 1, n1, :], edge_attr[EFULL * P:E, :], "ea_in1")
                else:
                    load(EA[:, 1, n1, :], ea_even[:, 5 * u + 3, par, :], "ea_in1")

            sp.wait_ge(s("f0_done"), NT + 2)
            with sp.Fori(0, IT - 1) as u:
                edge_rows(0, u, False)
            edge_rows(0, IT - 1, True)
            for i in range(2):
                sp.sem_inc(s(f"h2_out{i}"), 16)
            with sp.Fori(0, NJ) as j:
                for i in range(2):
                    sp.wait_ge(s("n2_hr"), 2 * j + i + 1)
                    load(rows(h2_d, 2 * j + i), HR[:, i, :], f"h2_out{i}")
            with sp.Fori(0, IT - 1) as u:
                edge_rows(1, u, False)
            edge_rows(1, IT - 1, True)
            with sp.Fori(0, NJ) as j:
                for i in range(2):
                    sp.wait_ge(s("h2r_free"), 2 * j + i + 1)
                    load(H2R[:, i, :], rows(h2_d, 2 * j + i), f"h2r_in{i}")
            sp.wait_ge(s("m_out"), NT + 2)
            for w, a in ((0, w_l), (1, w_r)):
                load(WRAW[:, w, :, :], a.rearrange("(o p) n -> p o n", p=P), "l3_in")
            for t, a in ((GMR, gamma), (BTR, beta), (BLR, b_l)):
                load(t, row(a, P), "l3_in")
            for i in range(2):
                sp.sem_inc(s(f"h3_out{i}"), 16)
            with sp.Fori(0, NJ) as j:
                for i in range(2):
                    sp.wait_ge(s("n3_hr"), 2 * j + i + 1)
                    load(rows(h3_d, 2 * j + i), HR[:, i, :], f"h3_out{i}")
            for i in range(2):
                sp.sem_inc(s(f"out{i}"), 16)
            with sp.Fori(0, NJ - 1) as j:
                for i in range(2):
                    sp.wait_ge(s("o_ready"), 2 * j + i + 1)
                    load(rows(out, 2 * j + i), HR[:, i, :], f"out{i}")
            sp.wait_ge(s("o_ready"), NT - 1)
            load(out[(NT - 2) * P:(NT - 1) * P, :], HR[:, 0, :], "out0")
            sp.wait_ge(s("o_ready"), NT)
            load(out[(NT - 1) * P:N, :], HR[0:NTAIL, 1, :], "out1")
            for i in range(2):
                sp.wait_ge(s(f"out{i}"), 16 * (NJ + 1))
                sp.wait_ge(s(f"stage_out{i}"), 16 * (NJ + 1))
                sp.wait_ge(s(f"h2_out{i}"), 16 * (NJ + 1))
                sp.wait_ge(s(f"h3_out{i}"), 16 * (NJ + 1))
            sp.wait_ge(s("el_out"), 16)
            sp.wait_ge(s("y_out"), 16)

        @block.gpsimd
        def _(pool):
            step = Steps(pool, s("pool_steps"))
            step(pool.memset(IDENT[:, :], 0.0))
            pool.affine_select(out=IDENT[:, :], in_=IDENT[:, :], compare_op=ALU.not_equal, fill=1.0, base=0,
                               pattern=[[-1, P]], channel_multiplier=1).then_inc(s("const_ready"), 1)
            pool.iota(IOTA[:, :], pattern=[[1, P]], base=0, channel_multiplier=0,
                      allow_small_or_imprecise_dtypes=True).then_inc(s("const_ready"), 1)
            pool.iota(IOTP[:, :], pattern=[[P, 2]], base=0, channel_multiplier=1,
                      allow_small_or_imprecise_dtypes=True).then_inc(s("const_ready"), 1)

            def gather(g, table, width, idx):
                with pool.Fori(0, IT) as u:
                    step.enter(u, 2)
                    for h in range(2):
                        if g == 0:
                            pool.wait_ge(s("el_slots"), 2 * u + h + 1)
                        else:
                            pool.wait_ge(s("added"), T * (g - 1) + 10 * u + 5 * h + 5)
                        step(pool.tensor_copy(IX[:, h, :], idx[:, bass.ds(10 * u + 5 * h, 5)]))
                        pool.nop(nofuse=True)
                        for k in range(5):
                            pool.indirect_dma_start(
                                SL[:, 5 * h + k, 0:width], None, table,
                                bass.IndirectOffsetOnAxis(ap=IX[:, h, k:k + 1], axis=0),
                            ).then_inc(gath[5 * h + k], 16)
                    step.leave(IT)

            pool.wait_ge(s("idx_ready"), 2)
            pool.wait_ge(s("el_out"), 16)
            gather(0, el_d.rearrange("n (r h) -> (n r) h", r=R), H, IDXST)
            pool.wait_ge(s("el_slots"), 2 * IT + 2)
            for i in range(2):
                pool.wait_ge(s(f"stage_out{i}"), 16 * (NJ + 1))
            gather(1, feat_d.rearrange("n (r d) -> (n r) d", r=R), D, IDXST)
            pool.wait_ge(s("y_out"), 16)
            gather(2, y_d, K, IDXS)
            for i in range(2):
                pool.wait_ge(s(f"h2_out{i}"), 16 * (NJ + 1))
            gather(3, h2_d, D, IDXS)
            for i in range(2):
                pool.wait_ge(s(f"h3_out{i}"), 16 * (NJ + 1))
            pool.wait_ge(s("m_t"), 4 * NT)
            gather(4, h3_d, D, IDXS)

        @block.scalar
        def _(act):
            step = Steps(act, s("act_steps"))

            def rstd(name, var, to):
                act.wait_ge(s(name), 1)
                act.activation(to, var, ACT.Sqrt, bias=EPSC[:, 0:1]).then_inc(s(name + "_sqrt"), 1)

            def norm_rows(l, used):
                rstd(f"n{l}_stats", MV[:, :, 1], RS[:, :])
                act.wait_ge(s(f"n{l}_scale"), 1)
                with act.Fori(0, NJ) as j:
                    for i in range(2):
                        t = 2 * j + i
                        for name, k, c in used:
                            act.wait_ge(s(name.format(i=i)), k(j, t))
                        act.activation(HR[:, i, :], X[:, bass.ds(t, 1), :], ACT.Relu, scale=RS[:, bass.ds(t, 1)],
                                       bias=NB[:, bass.ds(t, 1)]).then_inc(s(f"n{l}_hr"), 1)

            act.wait_ge(s("ones_row"), 1)
            norm_rows(0, [("n0_tp", lambda j, t: t + 1, 0)])
            act.wait_ge(s("small_in"), 16 * 15)
            act.activation(B1C, B1C, ACT.Relu).then_inc(s("b1_relu"), 1)
            act.sem_inc(s("el_slots"), 2)
            with act.Fori(0, IT) as u:
                for h in range(2):
                    for k in range(5):
                        act.wait_ge(gath[5 * h + k], 16 * (u + 1))
                    act.activation(ELA[:, bass.ds((10 * u + 5 * h) * H, 5 * H)].rearrange("p (k h) -> p k h", h=H),
                                   SL[:, 5 * h:5 * h + 5, 0:H], ACT.Copy).then_inc(s("el_slots"), 1)
            act.wait_ge(s("e_ps"), 1)
            step(act.activation(EF, PS[0:LT, 0:H, 0:LB * P], ACT.Copy))
            act.activation(EB, PS[0:LT, 0:H, 0:LB * P], ACT.Copy).then_inc(s("e_sb"), 1)
            act.wait_ge(s("e_shift"), 1)
            act.activation(EX, EX, ACT.Exp).then_inc(s("e_exp"), 1)
            act.wait_ge(s("e_exp"), 1)
            act.activation(EF, EX, ACT.Copy).then_inc(s("x_sb"), 1)
            act.activation(EB, EX, ACT.Copy).then_inc(s("x_sb"), 1)
            act.wait_ge(s("alpha_ready"), 1)
            with act.Fori(0, IT) as u:
                step.enter(u, 2)
                for h in range(2):
                    step(act.activation(ALS[:, h, :], AL[:, bass.ds((10 * u + 5 * h) * H, 5 * H)], ACT.Copy))
                    for k in range(5):
                        act.wait_ge(gath[5 * h + k], 16 * (IT + u + 1))
                        for q in range(H):
                            v = SL[:, 5 * h + k, q * DH:(q + 1) * DH]
                            a = k * H + q
                            last = act.activation(v, v, ACT.Copy, scale=ALS[:, h, a:a + 1])
                        last.then_inc(s("msg_ready"), 1)
                step.leave(IT)

            def take_columns(name, used, planes, parts):
                with act.Fori(0, NJ) as j:
                    for i in range(2):
                        t = 2 * j + i
                        act.wait_ge(s(used), t + 1)
                        act.activation(AR[0:parts, i, 0:planes * P].rearrange("p (a n) -> p a n", a=planes),
                                       ACC[0:parts, 0:planes, bass.ds(t * P, P)], ACT.Copy).then_inc(s(name), 1)

            act.wait_ge(s("added"), T + 10)
            take_columns("f0_ar", "f0_tp", 3, P)
            act.wait_ge(s("f0_done"), NT + 2)
            act.activation(DG[:, :], DG[:, :], ACT.Sqrt, bias=1.0).then_inc(s("dg_sqrt"), 1)
            norm_rows(1, [("n1_tp", lambda j, t: t + 1, 0), ("n1_done", lambda j, t: t + 1, 0)])

            def edge_hidden(par):
                with act.Fori(0, IT) as u:
                    for kk in range(5):
                        m = IT * 5 * par + 5 * u + kk
                        act.wait_ge(s("ea_used"), m + 1 + 5)
                        act.activation(EAT[0:ED, :], PS[0:ED, 2, 0:P], ACT.Copy).then_inc(s("ea_t"), 1)
                        act.wait_ge(s("hid_ps"), m + 1)
                        act.activation(HM, PS[:, 3, 0:D], ACT.Relu).then_inc(s("hid_ready"), 1)

            edge_hidden(0)
            act.wait_ge(s("added"), 2 * T + 10)
            take_columns("f1_ar", "f1_tp", 1, K)
            act.wait_ge(s("z_shift"), 1)
            act.activation(Z, Z, ACT.Exp).then_inc(s("z_exp"), 1)
            act.wait_ge(s("z_soft"), 1)
            with act.Fori(0, NJ) as j:
                for i in range(2):
                    t = 2 * j + i
                    act.wait_ge(s("g1_tp"), t + 1)
                    act.activation(SR[:, i, :], Z[:, bass.ds(t, 1), :], ACT.Copy).then_inc(s("g1_sr"), 1)
                for i in range(2):
                    t = 2 * j + i
                    act.wait_ge(s("g1_tp"), t + 3)
                    act.wait_ge(s("g1_mm"), t + 1)
                    act.activation(STR[:, i, :], PS[0:K, 2 + i, 0:P], ACT.Copy).then_inc(s("g1_st"), 1)
            norm_rows(2, [("n2_tp", lambda j, t: t + 1, 0), ("h2_out{i}", lambda j, t: 16 * (j + 1), 0)])
            edge_hidden(1)

            with act.Fori(0, NJ) as j:
                for l in range(2):
                    for i in range(2):
                        n = 4 * j + 2 * l + i
                        act.wait_ge(s("m_var"), n + 1)
                        act.activation(SM[:, i, 2:3], SM[:, i, 1:2], ACT.Sqrt, bias=EPSC[:, 0:1])\
                            .then_inc(s("m_sqrt"), 1)
                        act.wait_ge(s("m_scale"), n + 1)
                        act.activation(ZR[:, i, :], ZR[:, i, :], ACT.Identity, scale=SM[:, i, 3:4],
                                       bias=SM[:, i, 4:5]).then_inc(s("m_z"), 1)
                    for i in range(2):
                        n = 4 * j + 2 * l + i
                        act.wait_ge(s("m_t"), 2 * n + 2)
                        for c in range(KH):
                            last = act.activation(H1T[:, i, c, :], PS[:, 4 + 2 * i + c // 4, (c % 4) * P:(c % 4 + 1) * P],
                                                  ACT.Relu, scale=COL8[:, 2 * l, c:c + 1], bias=COL8[:, 2 * l + 1, c:c + 1])
                        last.then_inc(s("m_h"), 1)
                for i in range(2):
                    act.wait_ge(s("y_var"), 2 * j + i + 1)
                    act.activation(SM[:, i, 2:3], SM[:, i, 1:2], ACT.Sqrt, bias=EPSC[:, 0:1]).then_inc(s("y_sqrt"), 1)
            rstd("n3_stats", MV[:, :, 1], RS[:, :])
            act.wait_ge(s("n3_scale"), 1)
            with act.Fori(0, NJ) as j:
                for i in range(2):
                    t = 2 * j + i
                    act.wait_ge(s("n3_tp"), t + 1)
                    act.wait_ge(s(f"h3_out{i}"), 16 * (j + 1))
                    act.activation(HR[:, i, :], X[:, bass.ds(t, 1), :], ACT.Relu, scale=RS[:, bass.ds(t, 1)],
                                   bias=NB[:, bass.ds(t, 1)]).then_inc(s("n3_in"), 1)
                for i in range(2):
                    act.wait_ge(s("n3_var"), 2 * j + i + 1)
                    act.activation(SM[:, i, 2:3], SM[:, i, 1:2], ACT.Sqrt, bias=EPSC[:, 0:1]).then_inc(s("n3_sqrt"), 1)

        @block.tensor
        def _(pe):
            def turn(out_ap, in_ap, k):
                return pe.transpose(out_ap, in_ap, IDENT[0:k, 0:k])

            pe.wait_ge(s("const_ready"), 3)
            pe.wait_ge(s("prep_ready"), 1)
            for bank, a in enumerate((RELF, SF, STF, TF)):
                for b in range(LB):
                    last = turn(PS[:, bank, b * LT:(b + 1) * LT], a[:, b * P:(b + 1) * P], LT)
            for bank, q in ((4, 0), (5, 2)):
                for b in range(LB):
                    last = turn(PS[0:1, bank, b * LT:(b + 1) * LT], QC[:, q, b:b + 1], LT)
            last.then_inc(s("prep_t"), 1)
            pe.wait_ge(s("csum_rows"), 1)
            for c in range(2):
                last = pe.matmul(PS[:, 6, 0:K], HTR[:, 0, c, :], GW[:, c, :], start=(c == 0), stop=(c == 1))
            last.then_inc(s("cw_ps"), 1)
            pe.wait_ge(s("prep_used"), 1)

            def norm_turn(l, t, i):
                pe.wait_ge(s(f"n{l}_hr"), t + 1)
                turn(PS[:, i, 0:P], HR[:, i, 0:P], P)
                turn(PS[:, i, P:D], HR[:, i, P:D], P).then_inc(s(f"n{l}_tp"), 1)

            pe.sem_inc(s("n0_tp"), 2)
            pe.wait_ge(s("aw_ready"), 1)
            with pe.Fori(0, NJ) as j:
                for i in range(2):
                    norm_turn(0, 2 * j + i, i)
                for i in range(2):
                    t = 2 * j + i
                    pe.wait_ge(s("n0_ht"), t + 1)
                    pe.wait_ge(s("elr_done"), t + 1)
                    for c in range(2):
                        last = pe.matmul(PS[:, 2 + i, 0:2 * RH], HTR[:, i, c, :], AW_[:, c, :],
                                         start=(c == 0), stop=(c == 1))
                    last.then_inc(s("elr_ps"), 1)
            pe.sem_inc(s("tab_ps"), 8)
            with pe.Fori(0, NJ) as j:
                for i in range(2):
                    t = 2 * j + i
                    pe.wait_ge(s("tab_in"), t + 1)
                    for q in range(4):
                        pe.wait_ge(s("tab_free"), 4 * t + q + 1)
                        for c in range(2):
                            last = pe.matmul(PS[:, 4 + q, :], HTR[:, i, c, :], WALL[:, c, q * 512:(q + 1) * 512],
                                             start=(c == 0), stop=(c == 1))
                        last.then_inc(s("tab_ps"), 1)
            with pe.Fori(0, IT) as u:
                _, qs = nc.values_load_multi_w_load_instructions(
                    QR[:, bass.ds(10 * u, 10)], engines=[PE], min_val=0, max_val=(NT - 1) * RH,
                    skip_runtime_bounds_check_because="clamped to the last node tile when it was computed")
                for h in range(2):
                    pe.wait_ge(s("oht_ready"), 2 * u + h + 3)
                    pe.wait_ge(s("er_done"), 2 * u + h + 1)
                    for k in range(5):
                        o = PS[:, h, k * RH:(k + 1) * RH]
                        q = qs[5 * h + k]
                        pe.matmul(o, OHT[:, h, 0, k * P:(k + 1) * P], ER[:, bass.ds(q, RH)], start=True, stop=False)
                        last = pe.matmul(o, OHT[:, h, 1, k * P:(k + 1) * P], ER[:, bass.ds(q + RH, RH)],
                                         start=False, stop=True)
                    last.then_inc(s("er_ps"), 1)
            pe.wait_ge(s("e_all"), 1)
            ev = AL[:, 0:T * H].rearrange("p (t h) -> p t h", h=H)
            for h in range(H):
                for b in range(LB):
                    last = turn(PS[0:LT, h, b * P:(b + 1) * P], ev[:, b * LT:(b + 1) * LT, h], P)
            last.then_inc(s("e_ps"), 1)
            for b in range(LB):
                turn(PS[0:H, 4, b * LT:(b + 1) * LT], REP[:, 0, b, :], LT)
                last = turn(PS[0:H, 5, b * LT:(b + 1) * LT], REP[:, 1, b, :], LT)
            last.then_inc(s("rep_ps"), 1)
            for r in range(2):
                pe.wait_ge(s("ends"), r + 1)
                for b in range(LB):
                    turn(PS[0:H, 6, b * LT:(b + 1) * LT], QE[:, 0, b, :], LT)
                    last = turn(PS[0:H, 7, b * LT:(b + 1) * LT], QE[:, 1, b, :], LT)
                last.then_inc(s("ends_ps"), 1)
                pe.wait_ge(s("carry"), r + 1)
                for b in range(LB):
                    turn(PS[0:LT, 4, b * H:(b + 1) * H], CF[:, b * LT:(b + 1) * LT], H)
                    last = turn(PS[0:LT, 5, b * H:(b + 1) * H], CBK[:, b * LT:(b + 1) * LT], H)
                last.then_inc(s("carry_ps"), 1)
            pe.wait_ge(s("alpha_t"), 1)
            for b in range(LB):
                for h in range(H):
                    last = turn(PS[:, b, h * LT:(h + 1) * LT], EX[:, h, b * P:(b + 1) * P], LT)
            last.then_inc(s("alpha_ps"), 1)

            def edge_sums(g, planes, par=None):
                def agg(u, k):
                    n = T * (g - 1) + 10 * u + k
                    if g == 1:
                        pe.wait_ge(s("msg_ready"), 10 * u + k + 1)
                    else:
                        pe.wait_ge(gath[k], 16 * (IT * g + u + 1))
                    pe.wait_ge(s("oh_ready"), 2 * (IT * (g - 1) + u) + k // 5 + 1)
                    pe.wait_ge(s("added"), n + 9)
                    if g == 2:
                        pe.matmul(PS[0:K, k % 2, 0:P], SL[:, k, 0:K], OH[:, k, :], start=True, stop=True)\
                            .then_inc(s("agg_ps"), 1)
                        return
                    for c in range(planes):
                        w = ONES[:, :] if c == 2 else SL[:, k, c * P:(c + 1) * P]
                        last = pe.matmul(PS[:, k % 2, c * P:(c + 1) * P], w, OH[:, k, :], start=True, stop=True)
                    last.then_inc(s("agg_ps"), 1)

                with pe.Fori(0, IT) as u:
                    if par is None:
                        for k in range(10):
                            agg(u, k)
                    else:
                        n0 = 3 - par
                        for kk in range(5):
                            m = IT * 5 * par + 5 * u + kk
                            h, e = (0, kk) if kk < n0 else (1, kk - n0)
                            pe.wait_ge(s(f"ea_in{h}"), (16 if h == 0 else 32) * (IT * par + u + 1))
                            pe.nop(nofuse=True)
                            turn(PS[0:ED, 2, 0:P], EA[:, h, e, :], P).then_inc(s("ea_used"), 1)
                            agg(u, 2 * kk)
                            pe.wait_ge(s("ea_t"), m + 1)
                            pe.matmul(PS[:, 3, 0:D], EAT[:, :], W1A[:, :], start=True, stop=True)\
                                .then_inc(s("hid_ps"), 1)
                            agg(u, 2 * kk + 1)
                            pe.wait_ge(s("hid_ready"), m + 1)
                            pe.wait_ge(s("hs_added"), m + 1)
                            for c in range(2):
                                last = pe.matmul(PS[:, 5, c * P:(c + 1) * P], HM[:, c * P:(c + 1) * P],
                                                 OH[:, 2 * kk + par, :], start=True, stop=True)
                            last.then_inc(s("hs_ps"), 1)

            edge_sums(1, 3)
            pe.sem_inc(s("f0_tp"), 2)
            with pe.Fori(0, NJ) as j:
                for i in range(2):
                    t = 2 * j + i
                    pe.wait_ge(s("f0_ar"), t + 1)
                    pe.wait_ge(s("f0_done"), t + 1)
                    for c in range(3):
                        last = turn(PS[:, i, c * P:(c + 1) * P], AR[:, i, c * P:(c + 1) * P], P)
                    last.then_inc(s("f0_tp"), 1)
            pe.sem_inc(s("n1_tp"), 2)
            with pe.Fori(0, NJ) as j:
                for i in range(2):
                    norm_turn(1, 2 * j + i, i)
                for i in range(2):
                    t = 2 * j + i
                    pe.wait_ge(s("n1_ht"), t + 1)
                    pe.wait_ge(s("n1_done"), t + 1)
                    for c in range(2):
                        last = pe.matmul(PS[:, 2 + i, 0:K], HTR[:, i, c, :], GW[:, c, :], start=(c == 0), stop=(c == 1))
                    last.then_inc(s("n1_ps"), 1)
            pe.sem_inc(s("ea_used"), 5)
            pe.wait_ge(s("b1_relu"), 1)
            for f in range(2):
                for c in range(2):
                    last = pe.matmul(PS[:, 6, f:f + 1], EW2[:, c, f * P:(f + 1) * P], B1C[:, c:c + 1],
                                     start=(c == 0), stop=(c == 1))
            last.then_inc(s("cb2_ps"), 1)
            edge_sums(2, 1, par=0)
            pe.sem_inc(s("f1_tp"), 2)
            with pe.Fori(0, NJ) as j:
                for i in range(2):
                    t = 2 * j + i
                    pe.wait_ge(s("f1_ar"), t + 1)
                    pe.wait_ge(s("f1_done"), t + 1)
                    pe.nop(nofuse=True)
                    turn(PS[:, i, 0:K], AR[0:K, i, 0:P], K).then_inc(s("f1_tp"), 1)
            pe.sem_inc(s("g1_tp"), 2)
            pe.sem_inc(s("g1_mm"), 2)
            with pe.Fori(0, NJ) as j:
                for i in range(2):
                    t = 2 * j + i
                    pe.wait_ge(s("g1_sr"), t + 1)
                    pe.nop(nofuse=True)
                    turn(PS[0:K, 2 + i, 0:P], SR[:, i, :], P).then_inc(s("g1_tp"), 1)
                for i in range(2):
                    t = 2 * j + i
                    pe.wait_ge(s("g1_st"), t + 1)
                    pe.wait_ge(s("g1_done"), t + 1)
                    pe.matmul(PS[:, 4 + i, 0:D], STR[:, i, :], CE[:, :], start=True, stop=True)\
                        .then_inc(s("g1_mm"), 1)
            pe.sem_inc(s("n2_tp"), 2)
            with pe.Fori(0, NJ) as j:
                for i in range(2):
                    pe.wait_ge(s("n2_done"), 2 * j + i + 1)
                    norm_turn(2, 2 * j + i, i)
            edge_sums(3, 2, par=1)
            pe.wait_ge(s("mlp_in"), 16 * 8)

            def dense(t, i, wait_for, lhs, w, banks, width, l):
                pe.wait_ge(s(wait_for[0]), wait_for[1])
                kc = w.shape[1]
                for q in range(banks):
                    for c in range(kc):
                        last = pe.matmul(PS[:, (2 * i + q) if l < 2 else 4 + 2 * i, 0:width], lhs[:, i, c, :],
                                         w[:, c, q * width:(q + 1) * width], start=(c == 0), stop=(c == kc - 1))
                return last

            def turn_hidden(j, i, l):
                n = 4 * j + 2 * l + i
                pe.wait_ge(s("m_z"), n + 1)
                for q in range(2):
                    for c in range(4):
                        last = turn(PS[:, 4 + 2 * i + q, c * P:(c + 1) * P],
                                    ZR[:, i, (4 * q + c) * P:(4 * q + c + 1) * P], P)
                    last.then_inc(s("m_t"), 1)

            with pe.Fori(0, NJ) as j:
                for i in range(2):
                    t = 2 * j + i
                    pe.wait_ge(s("m_out"), t + 1)
                    for f in range(2):
                        for c in range(2):
                            last = pe.matmul(PS[:, 4 + 2 * i, f * P:(f + 1) * P], EW2[:, c, f * P:(f + 1) * P],
                                             HS[:, c, bass.ds(t * P, P)], start=(c == 0), stop=(c == 1))
                    last.then_inc(s("m_ee"), 1)
                for i in range(2):
                    dense(2 * j + i, i, ("m_hin", 2 * j + i + 1), HIN, W1S, 2, 512, 0).then_inc(s("m_ps"), 1)
                for i in range(2):
                    turn_hidden(j, i, 0)
                    dense(2 * j + i, i, ("m_h", 4 * j + i + 1), H1T, W2S, 2, 512, 1).then_inc(s("m_ps"), 1)
                for i in range(2):
                    turn_hidden(j, i, 1)
                    dense(2 * j + i, i, ("m_h", 4 * j + 2 + i + 1), H1T, W3S, 1, D, 2).then_inc(s("m_y"), 1)
            pe.wait_ge(s("l3_in"), 16 * 5)
            for w in range(2):
                for c in range(2):
                    for o in range(2):
                        last = turn(PS[:, 2 + w, (2 * c + o) * P:(2 * c + o + 1) * P], WRAW[:, w, o, c * P:(c + 1) * P], P)
            last.then_inc(s("w3_ps"), 1)
            pe.sem_inc(s("n3_tp"), 2)
            pe.wait_ge(s("w3_sb"), 2)
            with pe.Fori(0, NJ) as j:
                for i in range(2):
                    norm_turn(3, 2 * j + i, i)
                for i in range(2):
                    t = 2 * j + i
                    pe.wait_ge(s("n3_ht"), t + 1)
                    pe.wait_ge(s("n3_done"), t + 1)
                    for c in range(2):
                        last = pe.matmul(PS[:, 4 + i, 0:D], HTR[:, i, c, :], WLR[:, 1, c, :], start=(c == 0), stop=(c == 1))
                    last.then_inc(s("n3_ps"), 1)
            edge_sums(4, 2)
            pe.sem_inc(s("o_ps"), 2)
            with pe.Fori(0, NJ) as j:
                for i in range(2):
                    t = 2 * j + i
                    pe.wait_ge(s("o_ar"), t + 1)
                    pe.wait_ge(s("o_free"), t + 1)
                    for c in range(2):
                        last = pe.matmul(PS[:, i, 0:D], AR[:, i, c * P:(c + 1) * P], WLR[:, 0, c, :],
                                         start=(c == 0), stop=(c == 1))
                    last.then_inc(s("o_ps"), 1)

        @block.vector
        def _(dve):
            step = Steps(dve, s("dve_steps"))
            tt, ts, stt, cp = dve.tensor_tensor, dve.tensor_scalar, dve.scalar_tensor_tensor, dve.tensor_copy

            for t, v in ((DI, int(PAD_DST)), (SI, 0), (TI, 0)):
                dve.memset(t, v).then_inc(s("edge_pads"), 1)
            dve.memset(X[:, NT - 1, :], 0.0).then_inc(s("x_tail_zero"), 1)
            step(dve.memset(EPSC[:, :], LN_EPS))
            step(dve.memset(ONES[:, :], 1.0))
            dve.memset(ER[:, NT * RH:(NT + 1) * RH], 0.0).then_inc(s("ones_row"), 1)
            dve.wait_ge(s("edges_in"), 16 * 9)
            v3 = lambda a: a.rearrange("t (b e) -> t b e", b=LB)
            step(cp(DF, DI))
            step(cp(SF, SI))
            step(cp(TF, TI))
            step(stt(out=STF, in0=SF, scalar=float(R), in1=TF, op0=ALU.mult, op1=ALU.add))
            step(ts(QC[:, 0, :], v3(DF)[:, :, 0], float(N), None, ALU.min))
            step(cp(QI[:, 0, :], QC[:, 0, :]))
            step(ts(QI[:, 1, :], QI[:, 0, :], 7, 7, ALU.logical_shift_right, ALU.logical_shift_left))
            step(cp(QC[:, 1, :], QI[:, 1, :]))
            step(ts(QC[:, 2, :], QC[:, 1, :], float(RH) / P, None, ALU.mult))
            step(tt(v3(RELF), v3(DF), bc(QC[:, 0, :].unsqueeze(2), [LT, LB, P]), ALU.subtract))
            tt(v3(RELQ), v3(DF), bc(QC[:, 1, :].unsqueeze(2), [LT, LB, P]), ALU.subtract).then_inc(s("relq_ready"), 1)
            step(dve.memset(MF, 0.0))
            step(dve.memset(MB, 0.0))
            step(tt(v3(MF)[:, :, 1:P], v3(DF)[:, :, 1:P], v3(DF)[:, :, 0:P - 1], ALU.is_equal))
            step(cp(v3(MB)[:, :, 0:P - 1], v3(MF)[:, :, 1:P]))
            step(ts(MFN, MF, BIG, -BIG, ALU.mult, ALU.add))
            step(ts(MBN, MB, BIG, -BIG, ALU.mult, ALU.add))
            step(cp(REP[:, 0, :, :], bc(v3(DF)[:, :, 0:1], [LT, LB, H])))
            cp(REP[:, 1, :, :], bc(v3(DF)[:, :, P - 1:P], [LT, LB, H])).then_inc(s("prep_ready"), 1)
            dve.wait_ge(s("small_in"), 16 * 15)
            step(dve.tensor_reduce(CSUM, ZR[:, 0, 0:2 * K].rearrange("p (c k) -> p c k", c=2), AX, ALU.add))
            cp(HTR[:, 0, :, :], bc(CSUM.unsqueeze(2), [P, 2, P])).then_inc(s("csum_rows"), 1)
            dve.wait_ge(s("prep_t"), 1)
            dve.wait_ge(s("const_ready"), 3)
            cp(IDXST[:, :], PS[:, 2, 0:T]).then_inc(s("idx_ready"), 1)
            cp(IDXS[:, :], PS[:, 1, 0:T]).then_inc(s("idx_ready"), 1)
            step(cp(DREL[:, :], PS[:, 0, 0:T]))
            step(cp(BASE[:, :], PS[0:1, 4, 0:T]))
            step(cp(QR, PS[0:1, 5, 0:T]))
            step(tt(TM, bc(PS[:, 3, 0:T].unsqueeze(2), [P, T, R]), bc(IOTA[:, 0:R].unsqueeze(1), [P, T, R]), ALU.is_equal))
            dve.wait_ge(s("cw_ps"), 1)
            cp(CW[:, :], PS[:, 6, 0:K]).then_inc(s("prep_used"), 1)

            def row_stats():
                for t in range(NT):
                    last = dve.bn_stats(XST[:, t, :], X[:, t, :])
                step(last)
                for t in range(NT):
                    last = dve.bn_aggr(MV[:, t, :], XST[:, t, :])
                step(last)

            def norm_scale(l):
                dve.engine_nop().then_inc(s(f"n{l}_stats"), 1)
                dve.wait_ge(s(f"n{l}_stats_sqrt"), 1)
                step(dve.reciprocal(RS[:, :], RS[:, :]))
                stt(out=NB[:, :], in0=MV[:, :, 0], scalar=-1.0, in1=RS[:, :], op0=ALU.mult, op1=ALU.mult)\
                    .then_inc(s(f"n{l}_scale"), 1)

            dve.wait_ge(s("x_in"), 32)
            row_stats()
            norm_scale(0)
            dve.wait_ge(s("conv_in"), 32)
            dve.wait_ge(s("attn_in"), 32)
            for c in range(2):
                for a in range(2):
                    step(tt(HT[:, 0, 0:R * D], WALL[:, c, :], ATT[:, a, :], ALU.mult))
                    step(dve.tensor_reduce(AW_[:, c, a * RH:(a + 1) * RH],
                                           HT[:, 0, 0:R * D].rearrange("p (r d) -> p r d", d=DH), AX, ALU.add))
            dve.engine_nop().then_inc(s("aw_ready"), 1)
            dve.sem_inc(s("elr_done"), 2)
            with dve.Fori(0, NJ) as j:
                step.enter(j, 4)
                for i in range(2):
                    t = 2 * j + i
                    dve.wait_ge(s("n0_tp"), t + 3)
                    pv = PS[:, i, 0:D].rearrange("p (c n) -> p c n", c=2)
                    step(cp(HT[:, :, bass.ds(t * P, P)], pv))
                    mine(dve, cp(HTR[:, i, :, :], pv), "n0_ht", t + 1)
                for i in range(2):
                    t = 2 * j + i
                    dve.wait_ge(s("elr_ps"), t + 1)
                    step(cp(ER[:, bass.ds(t * RH, RH)], PS[:, 2 + i, RH:2 * RH]))
                    mine(dve, cp(ELS[:, bass.ds(t, 1), :].rearrange("p a n -> p (a n)"), PS[:, 2 + i, 0:RH]),
                         "elr_done", t + 3)
                step.leave(NJ)
            dve.sem_inc(s("tab_free"), 4)
            with dve.Fori(0, NJ) as j:
                for i in range(2):
                    t = 2 * j + i
                    dve.wait_ge(s("tab_ps"), 4 * t + 4)
                    mine(dve, cp(HTR[:, i, :, :], HT[:, :, bass.ds(t * P, P)]), "tab_in", t + 1)
                    dve.wait_ge(s(f"stage_out{i}"), 16 * (j + 1))
                    for q in range(4):
                        dve.wait_ge(s("tab_ps"), 4 * t + q + 9)
                        cp(STAGE[:, i, q * 512:(q + 1) * 512], PS[:, 4 + q, :]).then_inc(s("tab_free"), 1)
            dve.sem_inc(s("oht_ready"), 2)
            dve.sem_inc(s("er_done"), 2)
            with dve.Fori(0, IT) as u:
                step.enter(u, 4)
                for h in range(2):
                    dve.wait_ge(s(f"rb_in{h}"), 16 * (u + 1))
                    step(ts(OHT[:, h, 0, :], RB[:, h, :], IOTP[:, 0:1], None, ALU.is_equal))
                    mine(dve, ts(OHT[:, h, 1, :], RB[:, h, :], IOTP[:, 1:2], None, ALU.is_equal),
                         "oht_ready", 2 * u + h + 3)
                for h in range(2):
                    dve.wait_ge(s("er_ps"), 2 * u + h + 1)
                    tm = bc(TM[:, bass.ds(10 * u + 5 * h, 5), :].unsqueeze(3), [P, 5, R, H])
                    step(tt(TMP[:, h, :].rearrange("p (k r h) -> p k r h", k=5, r=R),
                            PS[:, h, 0:5 * RH].rearrange("p (k r h) -> p k r h", k=5, r=R), tm, ALU.mult))
                    mine(dve, dve.tensor_reduce(
                        AL[:, bass.ds((10 * u + 5 * h) * H, 5 * H)].rearrange("p (k h) -> p k h", h=H),
                        TMP[:, h, :].rearrange("p (k r h) -> p k h r", k=5, r=R), AX, ALU.add), "er_done", 2 * u + h + 3)
                step.leave(IT)
            dve.wait_ge(s("el_slots"), 2 * IT + 2)
            step(tt(AL[:, 0:T * H], AL[:, 0:T * H], ELA, ALU.add))
            stt(out=AL[:, 0:T * H], in0=AL[:, 0:T * H], scalar=0.2, in1=AL[:, 0:T * H], op0=ALU.mult, op1=ALU.max)\
                .then_inc(s("e_all"), 1)
            DFR, DLR, J, W, KF, KB, KFN, KBN, JN, SFR, SBR = ROWS[0:11]
            for i in range(2):
                dve.wait_ge(s(f"stage_out{i}"), 16 * (NJ + 1))
            dve.wait_ge(s("rep_ps"), 1)
            step(cp(DFR[:, 0:T], PS[0:H, 4, 0:T]))
            step(cp(DLR[:, 0:T], PS[0:H, 5, 0:T]))
            step(dve.memset(J, 0.0))
            step(tt(J[:, 1:T], DFR[:, 1:T], DLR[:, 0:T - 1], ALU.is_equal))
            step(tt(W[:, 0:T], DFR[:, 0:T], DLR[:, 0:T], ALU.is_equal))
            step(tt(KF[:, 0:T], W[:, 0:T], J[:, 0:T], ALU.mult))
            step(tt(KB[:, 0:T], W[:, 0:T], J[:, 1:T + 1], ALU.mult))
            step(ts(KFN[:, 0:T], KF[:, 0:T], BIG, -BIG, ALU.mult, ALU.add))
            step(ts(KBN[:, 0:T], KB[:, 0:T], BIG, -BIG, ALU.mult, ALU.add))
            step(ts(JN, J, BIG, -BIG, ALU.mult, ALU.add))

            v4 = lambda a: a.rearrange("t h (b e) -> t h b e", b=LB)

            def segment(r, op0, op1, none, mf, mb, kf, kb, jn):
                def scans():
                    for h in range(H):
                        step(dve.tensor_tensor_scan(FS[:, h, :], mf, EF[:, h, :], none, op0, op1))
                        step(dve.tensor_tensor_scan(BS[:, h, ::-1], mb[:, ::-1], EB[:, h, ::-1], none, op0, op1))

                scans()
                step(cp(QE[:, 0, :, :].rearrange("t b h -> t h b"), v4(FS)[:, :, :, P - 1]))
                cp(QE[:, 1, :, :].rearrange("t b h -> t h b"), v4(BS)[:, :, :, 0]).then_inc(s("ends"), 1)
                dve.wait_ge(s("ends_ps"), r + 1)
                step(dve.memset(SFR[:, 0:1], none))
                step(dve.memset(SBR[:, T:T + 1], none))
                step(dve.tensor_tensor_scan(SFR[:, 1:T + 1], kf[:, 0:T], PS[0:H, 6, 0:T], none, op0, op1))
                step(dve.tensor_tensor_scan(SBR[:, 0:T][:, ::-1], kb[:, 0:T][:, ::-1], PS[0:H, 7, 0:T][:, ::-1],
                                            none, op0, op1))
                step(tt(CF[:, 0:T], SFR[:, 0:T], jn[:, 0:T], op0))
                tt(CBK[:, 0:T], SBR[:, 1:T + 1], jn[:, 1:T + 1], op0).then_inc(s("carry"), 1)
                dve.wait_ge(s("carry_ps"), r + 1)
                c4 = PS[0:LT, 4:6, 0:LB * H].rearrange("t w (b h) -> t w h b", b=LB)
                step(tt(v4(EF)[:, :, :, 0], v4(EF)[:, :, :, 0], c4[:, 0], op1))
                step(tt(v4(EB)[:, :, :, P - 1], v4(EB)[:, :, :, P - 1], c4[:, 1], op1))
                scans()

            dve.wait_ge(s("e_sb"), 1)
            segment(0, ALU.add, ALU.max, -BIG, MFN, MBN, KFN, KBN, JN)
            step(tt(FS, FS, BS, ALU.max))
            tt(EX, PS[0:LT, 0:H, 0:LB * P], FS, ALU.subtract).then_inc(s("e_shift"), 1)
            dve.wait_ge(s("x_sb"), 2)
            segment(1, ALU.mult, ALU.add, 0.0, MF, MB, KF, KB, J)
            step(tt(FS, FS, BS, ALU.add))
            step(tt(FS, FS, EX, ALU.subtract))
            step(dve.reciprocal(FS, FS))
            tt(EX, EX, FS, ALU.mult).then_inc(s("alpha_t"), 1)
            dve.wait_ge(s("alpha_t"), 1)
            step(dve.memset(ACC[:, :, :], 0.0))
            dve.wait_ge(s("alpha_ps"), 1)
            cp(AL[:, 0:T * H].rearrange("p (b t h) -> p b h t", b=LB, h=H),
               PS[:, 0:LB, 0:LT * H].rearrange("p b (h t) -> p b h t", h=H)).then_inc(s("alpha_ready"), 1)

            dve.sem_inc(s("added"), 10)

            def edge_adds(g, parts, planes, par=None):
                with dve.Fori(0, IT) as u:
                    _, base = nc.values_load_multi_w_load_instructions(
                        BASE[:, bass.ds(10 * u, 10)], engines=[DVE], min_val=0, max_val=N,
                        skip_runtime_bounds_check_because="clamped to N when it was computed")
                    for h in range(2):
                        k = slice(5 * h, 5 * h + 5)
                        mine(dve, tt(OH[:, k, :], bc(IOTA[:, :].unsqueeze(1), [P, 5, P]),
                                     bc(DREL[:, bass.ds(10 * u + 5 * h, 5)].unsqueeze(2), [P, 5, P]), ALU.is_equal),
                             "oh_ready", 2 * (IT * (g - 1) + u) + h + 1)
                    for k in range(10):
                        n = T * (g - 1) + 10 * u + k
                        dve.wait_ge(s("agg_ps"), n + 1)
                        a = ACC[0:parts, 0:planes, bass.ds(base[k], P)]
                        mine(dve, tt(a, a, PS[0:parts, k % 2, 0:planes * P].rearrange("p (a n) -> p a n", a=planes),
                                     ALU.add), "added", n + 11)
                        if par is not None and k % 2 == 1:
                            m = IT * 5 * par + 5 * u + k // 2
                            dve.wait_ge(s("hs_ps"), m + 1)
                            a = HS[:, :, bass.ds(base[k - 1 + par], P)]
                            mine(dve, tt(a, a, PS[:, 5, 0:D].rearrange("p (a n) -> p a n", a=2), ALU.add),
                                 "hs_added", m + 2)

            edge_adds(1, P, 3)
            dve.wait_ge(s("hb_in"), 16)
            dve.sem_inc(s("f0_done"), 2)
            with dve.Fori(0, NJ) as j:
                step.enter(j, 4)
                for i in range(2):
                    t = 2 * j + i
                    dve.wait_ge(s("f0_tp"), t + 3)
                    xt = X[:, bass.ds(t, 1), :].rearrange("p a d -> p (a d)")
                    step(tt(xt, xt, PS[:, i, 0:D], ALU.add))
                    step(tt(xt, xt, HB, ALU.add))
                    mine(dve, cp(DG[:, bass.ds(t, 1)], PS[:, i, D:D + 1]), "f0_done", t + 3)
                step.leave(NJ)
            row_stats()
            dve.wait_ge(s("dg_sqrt"), 1)
            step(dve.reciprocal(DG[:, :], DG[:, :]))
            norm_scale(1)
            dve.sem_inc(s("n1_done"), 2)
            with dve.Fori(0, NJ) as j:
                step.enter(j, 2)
                for i in range(2):
                    t = 2 * j + i
                    dve.wait_ge(s("n1_tp"), t + 3)
                    mine(dve, cp(HTR[:, i, :, :], PS[:, i, 0:D].rearrange("p (c n) -> p c n", c=2)), "n1_ht", t + 1)
                    xt = X[:, bass.ds(t, 1), :].rearrange("p a d -> p (a d)")
                    step(tt(xt, xt, HR[:, i, :], ALU.add))
                for i in range(2):
                    t = 2 * j + i
                    dve.wait_ge(s("n1_ps"), t + 1)
                    mine(dve, cp(Y[:, bass.ds(t, 1), :].rearrange("p a k -> p (a k)"), PS[:, 2 + i, 0:K]),
                         "n1_done", t + 3)
                step.leave(NJ)
            step(tt(Y, Y, bc(CW[:, :].unsqueeze(1), [P, NT, K]), ALU.add))
            tt(Y, Y, bc(DG[:, :].unsqueeze(2), [P, NT, K]), ALU.mult).then_inc(s("y_ready"), 1)
            dve.wait_ge(s("y_ready"), 1)
            step(dve.memset(ACC[0:K, 0, :], 0.0))
            step(dve.memset(HS[:, :, :], 0.0))
            step(dve.memset(EAT[ED:ED + 1, :], 1.0))
            dve.wait_ge(s("cb2_ps"), 1)
            step(tt(CB2, PS[:, 6, 0:2], B2C, ALU.add))
            step(ts(SC2, SC2, 2.0, None, ALU.add))
            dve.sem_inc(s("hs_added"), 1)
            edge_adds(2, K, 1, par=0)
            dve.sem_inc(s("f1_done"), 2)
            with dve.Fori(0, NJ) as j:
                for i in range(2):
                    t = 2 * j + i
                    dve.wait_ge(s("f1_tp"), t + 3)
                    mine(dve, cp(Z[:, bass.ds(t, 1), :].rearrange("p a k -> p (a k)"), PS[:, i, 0:K]), "f1_done", t + 3)
            step(tt(Z, Z, Y, ALU.add))
            step(tt(Z, Z, bc(DG[:, :].unsqueeze(2), [P, NT, K]), ALU.mult))
            step(tt(Z, Z, bc(GB[:, :].unsqueeze(1), [P, NT, K]), ALU.add))
            step(dve.tensor_reduce(ZM, Z, AX, ALU.max))
            tt(Z, Z, bc(ZM.unsqueeze(2), [P, NT, K]), ALU.subtract).then_inc(s("z_shift"), 1)
            dve.wait_ge(s("z_exp"), 1)
            step(dve.tensor_reduce(ZM, Z, AX, ALU.add))
            step(dve.reciprocal(ZM, ZM))
            tt(Z, Z, bc(ZM.unsqueeze(2), [P, NT, K]), ALU.mult).then_inc(s("z_soft"), 1)
            dve.sem_inc(s("g1_done"), 2)
            with dve.Fori(0, NJ) as j:
                for i in range(2):
                    t = 2 * j + i
                    dve.wait_ge(s("g1_mm"), t + 3)
                    xt = X[:, bass.ds(t, 1), :].rearrange("p a d -> p (a d)")
                    mine(dve, tt(xt, xt, PS[:, 4 + i, 0:D], ALU.add), "g1_done", t + 3)
            row_stats()
            norm_scale(2)
            dve.sem_inc(s("n2_done"), 2)
            with dve.Fori(0, NJ) as j:
                step.enter(j, 6)
                for i in range(2):
                    t = 2 * j + i
                    dve.wait_ge(s("n2_tp"), t + 3)
                    a = [ACC[:, c, bass.ds(t * P, P)] for c in range(3)]
                    for c in range(2):
                        step(ts(a[c], PS[:, i, c * P:(c + 1) * P], SC2, CB2[:, c:c + 1], ALU.mult, ALU.add))
                    step(stt(out=a[0], in0=a[2], scalar=B2C[:, 0:1], in1=a[0], op0=ALU.mult, op1=ALU.add))
                    mine(dve, stt(out=a[1], in0=a[2], scalar=B2C[:, 1:2], in1=a[1], op0=ALU.mult, op1=ALU.add),
                         "n2_done", t + 3)
                step.leave(NJ)
            step(dve.memset(ACC[:, 0:2, NPAD:AW], 0.0))
            for i in range(2):
                dve.wait_ge(s(f"h2_out{i}"), 16 * (NJ + 1))
            edge_adds(3, P, 2, par=1)
            dve.wait_ge(s("mlp_in"), 16 * 8)
            dve.sem_inc(s("m_out"), 2)
            dve.sem_inc(s("h2r_free"), 2)

            def scalars(i, name, n):
                dve.wait_ge(s(name), n)
                step(dve.reciprocal(SM[:, i, 3:4], SM[:, i, 2:3]))
                return stt(out=SM[:, i, 4:5], in0=SM[:, i, 0:1], scalar=-1.0, in1=SM[:, i, 3:4],
                           op0=ALU.mult, op1=ALU.mult)

            with dve.Fori(0, NJ) as j:
                step.enter(j, 4 * 3 + 2 * 7)
                for i in range(2):
                    t = 2 * j + i
                    dve.wait_ge(s("m_ee"), t + 1)
                    mine(dve, tt(HIN[:, i, :, :], ACC[:, 0:2, bass.ds(t * P, P)],
                                 PS[:, 4 + 2 * i, 0:D].rearrange("p (c n) -> p c n", c=2), ALU.add), "m_hin", t + 1)
                for l in range(2):
                    for i in range(2):
                        n = 4 * j + 2 * l + i
                        dve.wait_ge(s("m_ps"), n + 1)
                        step(tt(ZR[:, i, :], PS[:, 2 * i:2 * i + 2, :].rearrange("p a n -> p (a n)"), BR[:, l, :], ALU.add))
                        dve.nop(nofuse=True)
                        dve.bn_stats(STAT[:, i, 0:6], ZR[:, i, 0:512])
                        step(dve.bn_stats(STAT[:, i, 6:12], ZR[:, i, 512:1024]))
                        dve.nop(nofuse=True)
                        mine(dve, dve.bn_aggr(SM[:, i, 0:2], STAT[:, i, 0:12]), "m_var", n + 1)
                        mine(dve, scalars(i, "m_sqrt", n + 1), "m_scale", n + 1)
                for i in range(2):
                    t = 2 * j + i
                    dve.wait_ge(s("m_y"), t + 1)
                    dve.wait_ge(s(f"h2r_in{i}"), 16 * (j + 1))
                    yr = HTR[:, i, :, :].rearrange("p c n -> p (c n)")
                    mine(dve, tt(yr, PS[:, 4 + 2 * i, 0:D], B3R, ALU.add), "m_out", t + 3)
                    mine(dve, tt(yr, yr, H2R[:, i, :], ALU.add), "h2r_free", t + 3)
                    dve.nop(nofuse=True)
                    step(dve.bn_stats(STAT[:, i, 0:6], yr))
                    dve.nop(nofuse=True)
                    mine(dve, dve.bn_aggr(SM[:, i, 0:2], STAT[:, i, 0:6]), "y_var", t + 1)
                    step(scalars(i, "y_sqrt", t + 1))
                    step(ts(yr, yr, SM[:, i, 3:4], SM[:, i, 4:5], ALU.mult, ALU.add))
                    step(tt(yr, yr, GNR, ALU.mult))
                    step(tt(yr, yr, BNR, ALU.add))
                    xt = X[:, bass.ds(t, 1), :].rearrange("p a d -> p (a d)")
                    step(stt(out=xt, in0=yr, scalar=0.0, in1=xt, op0=ALU.max, op1=ALU.add))
                step.leave(NJ)
            row_stats()
            norm_scale(3)
            dve.wait_ge(s("w3_ps"), 1)
            for w in range(2):
                cp(WLR[:, w, :, :].rearrange("p c n -> p (c n)"), PS[:, 2 + w, :]).then_inc(s("w3_sb"), 1)
            step(ts(ACC[:, 2, :], ACC[:, 2, :], 1.0, None, ALU.max))
            step(dve.reciprocal(ACC[:, 2, :], ACC[:, 2, :]))
            step(dve.memset(ACC[:, 0:2, :], 0.0))
            dve.sem_inc(s("n3_done"), 2)
            with dve.Fori(0, NJ) as j:
                step.enter(j, 2 * 7)
                for i in range(2):
                    t = 2 * j + i
                    dve.wait_ge(s("n3_in"), t + 1)
                    dve.nop(nofuse=True)
                    step(dve.bn_stats(STAT[:, i, 0:6], HR[:, i, :]))
                    dve.nop(nofuse=True)
                    mine(dve, dve.bn_aggr(SM[:, i, 0:2], STAT[:, i, 0:6]), "n3_var", t + 1)
                for i in range(2):
                    t = 2 * j + i
                    hr = HR[:, i, :]
                    step(scalars(i, "n3_sqrt", t + 1))
                    step(ts(hr, hr, SM[:, i, 3:4], SM[:, i, 4:5], ALU.mult, ALU.add))
                    step(tt(hr, hr, GMR, ALU.mult))
                    step(tt(hr, hr, BTR, ALU.add))
                    mine(dve, ts(hr, hr, 0.0, None, ALU.max), "n3_hr", t + 1)
                for i in range(2):
                    t = 2 * j + i
                    dve.wait_ge(s("n3_tp"), t + 3)
                    mine(dve, cp(HTR[:, i, :, :], PS[:, i, 0:D].rearrange("p (c n) -> p c n", c=2)), "n3_ht", t + 1)
                for i in range(2):
                    t = 2 * j + i
                    dve.wait_ge(s("n3_ps"), t + 1)
                    xt = X[:, bass.ds(t, 1), :].rearrange("p a d -> p (a d)")
                    mine(dve, tt(xt, xt, PS[:, 4 + i, 0:D], ALU.add), "n3_done", t + 3)
                    step(tt(xt, xt, BLR, ALU.add))
                step.leave(NJ)
            for i in range(2):
                dve.wait_ge(s(f"h3_out{i}"), 16 * (NJ + 1))
            edge_adds(4, P, 2)
            dve.sem_inc(s("o_free"), 2)
            with dve.Fori(0, NJ) as j:
                for i in range(2):
                    t = 2 * j + i
                    dve.wait_ge(s("o_ps"), t + 1)
                    mine(dve, tt(AR[:, i, 0:D].rearrange("p (c n) -> p c n", c=2), ACC[:, 0:2, bass.ds(t * P, P)],
                                 bc(ACC[:, 2:3, bass.ds(t * P, P)], [P, 2, P]), ALU.mult), "o_ar", t + 1)
                for i in range(2):
                    t = 2 * j + i
                    dve.wait_ge(s("o_ps"), t + 3)
                    dve.wait_ge(s(f"out{i}"), 16 * (j + 1))
                    dve_out = tt(HR[:, i, :], X[:, bass.ds(t, 1), :].rearrange("p a d -> p (a d)"), PS[:, i, 0:D], ALU.add)
                    mine(dve, dve_out, "o_ready", t + 1)
                    dve.sem_inc(s("o_free"), 1)


_INS = ['x', 'src', 'dst', 'edge_attr_64', 'edge_type_8', 'L0_gnn_conv_weights', 'L0_gnn_attn_l', 'L0_gnn_attn_r',
        'L0_gnn_h_bias', 'L1_gnn_W', 'L1_gnn_bias', 'L1_gnn_cluster_emb', 'L2_gnn_eps', 'L2_gnn_ee_w1', 'L2_gnn_ee_b1',
        'L2_gnn_ee_w2', 'L2_gnn_ee_b2', 'L2_gnn_w1', 'L2_gnn_b1', 'L2_gnn_g1', 'L2_gnn_be1', 'L2_gnn_w2', 'L2_gnn_b2',
        'L2_gnn_g2', 'L2_gnn_be2', 'L2_gnn_w3', 'L2_gnn_b3', 'L2_gnn_bn_g', 'L2_gnn_bn_b', 'L3_gnn_gamma',
        'L3_gnn_beta', 'L3_gnn_W_l', 'L3_gnn_b_l', 'L3_gnn_W_r']
_OUTS = [((3750, 256), 'float32')]


def kernel(**inputs):
    import numpy as _np
    import concourse.bacc as _bacc
    from concourse import mybir as _mybir
    from concourse.bass_utils import run_bass_kernel_spmd as _run

    nc = _bacc.Bacc("TRN2", target_bir_lowering=False, num_devices=1)
    arrays, args = {}, []
    for name in _INS:
        a = _np.ascontiguousarray(inputs[name]).reshape(_np.shape(inputs[name]) or (1,))
        arrays[f"in_{name}_dram"] = a
        args.append(nc.dram_tensor(f"in_{name}_dram", a.shape, _mybir.dt.from_np(a.dtype), kind="ExternalInput").ap())
    for i, (shape, dtype) in enumerate(_OUTS):
        dt = _mybir.dt.from_np(_np.dtype(dtype))
        args.append(nc.dram_tensor(f"out_{i}_dram", shape, dt, kind="ExternalOutput").ap())
    gnn(nc, *args)
    r = _run(nc, [arrays], core_ids=[0])
    got = tuple(r.results[0][f"out_{i}_dram"] for i in range(len(_OUTS)))
    return got[0]
```

```python
from contextlib import ExitStack

import concourse.bass as bass
from concourse import mybir

P = 128
F32 = mybir.dt.float32
BF16 = mybir.dt.bfloat16
I32 = mybir.dt.int32
ALU = mybir.AluOpType
ACT = mybir.ActivationFunctionType
AX = mybir.AxisListType.X
DVE = mybir.EngineType.DVE
PE = mybir.EngineType.PE
BIG = 1e30
LN_EPS = 1e-5


class Steps:

    def __init__(self, eng, sem):
        self.eng, self.sem, self.n, self.u, self.per = eng, sem, 0, None, 0

    def __call__(self, ins):
        self.n += 1
        ins.then_inc(self.sem, 1)
        self.eng.wait_ge(self.sem, self.n if self.u is None else self.u * self.per + self.n)

    def enter(self, u, per):
        self.u, self.per, self.first = u, per, self.n

    def leave(self, trips):
        assert self.n - self.first == self.per, (self.n - self.first, self.per)
        self.n, self.u = self.first + trips * self.per, None


def gnn(nc, x, src, dst, edge_attr, edge_type, conv_w, attn_l, attn_r, h_bias, gcn_w, gcn_b, cluster,
        eps, ee_w1, ee_b1, ee_w2, ee_b2, w1, b1, g1, be1, w2, b2, g2, be2, w3, b3, bn_g, bn_b,
        gamma, beta, w_l, b_l, w_r, out):
    N, D = x.shape
    E = src.shape[0]
    R, H, _, DH = conv_w.shape
    RH = R * H
    K = gcn_w.shape[1]
    HID = w1.shape[1]
    ED = edge_attr.shape[1]
    KH = HID // P
    NT = -(-N // P)
    NJ = NT // 2
    NTAIL = N - (NT - 1) * P
    NPAD = NT * P
    LB, LT = 4, 125
    T = LB * LT
    IT = T // 10
    IL = IT // 2
    EFULL = E // P
    ETAIL = E - EFULL * P
    AW = NPAD + 40
    assert D == 2 * P and R * D == 2048 and NT % 2 == 0 and AW >= N + P and T * P >= E and EFULL == T - 2
    PAD_DST = 8000.0

    feat_d = nc.dram_tensor("feat_d", (NPAD, R * D), F32).ap()
    el_d = nc.dram_tensor("el_d", (NPAD, RH), F32).ap()
    y_d = nc.dram_tensor("y_d", (NPAD, K), F32).ap()
    h2_d = nc.dram_tensor("h2_d", (NPAD, D), F32).ap()
    h3_d = nc.dram_tensor("h3_d", (NPAD, D), F32).ap()
    rel_d = nc.dram_tensor("rel_d", (T * P,), BF16).ap()

    with ExitStack() as ctx:
        def sb(name, shape, dt=F32):
            return ctx.enter_context(nc.sbuf_tensor(name, shape, dt))

        def sem(name):
            return ctx.enter_context(nc.semaphore(name))

        PS = ctx.enter_context(nc.psum_tensor("PS", [P, 8, 512], F32))

        X = sb("X", [P, NT, D])
        ACC = sb("ACC", [P, 3, AW])
        HS = sb("HS", [P, 2, AW])
        SL = sb("SL", [P, 10, D])
        OHB = sb("OHB", [P, 1280])
        AL = sb("AL", [P, 2048])
        BG = sb("BG", [P, 15872])
        DREL = sb("DREL", [P, T + 5])
        IDXST = sb("IDXST", [P, T], I32)
        IDXS = sb("IDXS", [P, T], I32)
        BASE = sb("BASE", [1, T], I32)
        IX = sb("IX", [P, 2, 10], I32)
        IDENT = sb("IDENT", [P, P])
        IOTA = sb("IOTA", [P, P])
        IOTP = sb("IOTP", [P, 2])
        EPSC = sb("EPSC", [P, 1])
        W1A = sb("W1A", [ED + 1, D])
        EW2 = sb("EW2", [P, 2, D])
        GW = sb("GW", [P, 2, K])
        CE = sb("CE", [K, D])
        CW = sb("CW", [P, K])
        GB = sb("GB", [P, K])
        STAT = sb("STAT", [P, 2, 12])
        XST = sb("XST", [P, NT, 6])
        MV = sb("MV", [P, NT, 2])
        RS = sb("RS", [P, NT])
        NB = sb("NB", [P, NT])
        DG = sb("DG", [P, NT])
        COL = sb("COL", [P, 16])
        COL8 = sb("COL8", [P, 4, KH])
        SM = sb("SM", [P, 2, 8])
        YM = sb("YM", [P, 2, 8])
        REP = sb("REP", [LT, 2, LB, H])
        QEC = sb("QEC", [LT, 2, LB, H])
        QC = sb("QC", [LT, 4, LB])
        QI = sb("QI", [LT, 2, LB], I32)
        ALS = sb("ALS", [P, 2, 20])
        ONES = sb("ONES", [P, P])
        B2C, B1C, CSUM, CB2, SC2 = COL[:, 0:2], COL[:, 2:4], COL[:, 4:6], COL[:, 6:8], COL[:, 8:9]

        ACF = ACC[:, :, :].rearrange("p a n -> p (a n)")
        HSF = HS[:, :, :].rearrange("p a n -> p (a n)")
        SLF = SL[:, :, :].rearrange("p a n -> p (a n)")
        WALL = ACF[:, 0:4096].rearrange("p (c n) -> p c n", c=2)
        STAGE = ACF[:, 4096:8192].rearrange("p (i n) -> p i n", i=2)
        ATT = STAGE
        MF, MB, MFN, MBN = (ACF[0:LT, 8192 + 512 * i:8704 + 512 * i] for i in range(4))
        TF, STF = (ACF[0:LT, 10240 + 512 * i:10752 + 512 * i] for i in range(2))
        RELQ = ACF[0:LT, 11264:11520].bitcast(BF16)
        DI, SI, TI = (SLF[0:LT, 512 * i:512 * i + 512].bitcast(I32) for i in range(3))
        DF, SF = (SLF[0:LT, 1536 + 512 * i:2048 + 512 * i] for i in range(2))
        RELF = SLF[0:LT, 0:512]
        TM = HSF[:, 0:T * R].rearrange("p (t r) -> p t r", r=R)
        OHT = HSF[:, 4000:5280].bitcast(BF16).rearrange("p (h q e) -> p h q e", h=2, q=2)
        ELS = HSF[:, 6560:6560 + NT * RH].rearrange("p (t r) -> p t r", r=RH)
        EF, EB, EX = (HSF[0:LT, 2048 * i:2048 * i + 2048].rearrange("p (h n) -> p h n", h=H) for i in range(3))
        HT = BG[:, 0:2 * NPAD].rearrange("p (c n) -> p c n", c=2)
        SA = BG[:, 2 * NPAD:15872]
        ELA = SA[:, 0:T * H]
        FS, BS = (SA[0:LT, 2048 * i + 2048:2048 * i + 4096].rearrange("p (h n) -> p h n", h=H) for i in range(2))
        RB = SA[:, 6144:6784].bitcast(BF16).rearrange("p (h e) -> p h e", h=2)
        QR = SA[0:1, 6784:6784 + T].bitcast(I32)
        TMP = OHB[:, 0:960].rearrange("p (h n) -> p h n", h=2)
        ER = SA[:, 2048:2048 + NT * RH]
        ERB = ACF[:, 0:(NT + 1) * 3 * RH // 2].bitcast(BF16)
        AW_ = SA[:, 3072:3200].rearrange("p (c n) -> p c n", c=2)
        QE = QEC[:, :, :, :]
        ROWS = [HT[0:H, 0, 512 * i:512 * i + T + 1] for i in range(7)] + \
               [HT[0:H, 1, 512 * i:512 * i + T + 1] for i in range(7)]

        CF, CBK = ROWS[11:13]

        AR = OHB[:, 0:768].rearrange("p (i n) -> p i n", i=2)
        HR = OHB[:, 768:1280].rearrange("p (i n) -> p i n", i=2)
        HTR = BG[:, 15360:15872].rearrange("p (i c n) -> p i c n", i=2, c=2)
        HB = AL[:, 0:D]
        OH = OHB[:, :].rearrange("p (k n) -> p k n", k=10)
        EA = AL[:, 0:320].rearrange("p (k n) -> p k n", k=5)
        EAT = AL[0:ED + 1, 320:960].rearrange("p (k n) -> p k n", k=5)
        Y = AL[:, 960:960 + NT * K].rearrange("p (t k) -> p t k", k=K)
        HM = [BG[:, 15104:15616], AL[:, 1260:1772], BG[:, 15616:15872]]
        Z = AL[:, 1260:1260 + NT * K].rearrange("p (t k) -> p t k", k=K)
        ZM = AL[:, 1560:1560 + NT]
        SR = AL[:, 1590:1610].rearrange("p (i k) -> p i k", i=2)
        STR = AL[0:K, 1610:1866].rearrange("p (i n) -> p i n", i=2)

        W1S = BG[:, 0:2048].rearrange("p (c n) -> p c n", c=2)
        W2S = BG[:, 2048:10240].rearrange("p (c n) -> p c n", c=KH)
        W3S = BG[:, 10240:12288].rearrange("p (c n) -> p c n", c=KH)
        BR = [BG[:, 13312:14336], BG[:, 12288:13312]]
        SLOTS = [SL, BG[:, 10240:12800].rearrange("p (k n) -> p k n", k=10)]
        ELSL = SLF[:, 0:20 * H].rearrange("p (b k h) -> p b k h", b=2, k=10)
        B3R, GNR, BNR = (BG[:, 14336 + D * i:14336 + D * (i + 1)] for i in range(3))
        ZR = AL[:, :].rearrange("p (i n) -> p i n", i=2)
        H1T = SLF[:, 0:2048].rearrange("p (i c n) -> p i c n", i=2, c=KH)
        HIN = OHB[:, 0:512].rearrange("p (i c n) -> p i c n", i=2, c=2)
        H2R = OHB[:, 512:1024].rearrange("p (i n) -> p i n", i=2)
        WRAW = HSF[:, 0:1024].rearrange("p (w o n) -> p w o n", w=2, o=2)
        WLR = HSF[:, 1024:2048].rearrange("p (w c n) -> p w c n", w=2, c=2)
        GMR, BTR, BLR = (HSF[:, 2048 + D * i:2048 + D * (i + 1)] for i in range(3))

        S = {}

        def s(name):
            if name not in S:
                S[name] = sem(name)
            return S[name]

        EDGE_ORDER = [[("sum", 0)], [("sum", 1), ("hidden", 0)], [("sum", 2)], [("sum", 3), ("hidden", 1)], [],
                      [("sum", 4), ("hidden", 2)], [("turn", 0)], [], [], []]
        gath = [sem(f"gathered{k}") for k in range(4)]

        def gathered(eng, g, w, b, h):
            eng.wait_ge(gath[2 * b + h], 5 * 16 * (IL * g + w + 1))

        def oh_count(g, u, h):
            return (2 * IT + 1) * (g - 1) + 2 * u + h + 1

        def mine(eng, ins, name, value):
            ins.then_inc(s(name), 1)
            eng.wait_ge(s(name), value)

        def rows_out(k, n):
            return 16 * (NJ * k + n + 1)

        def bc(ap, shape):
            return ap.broadcast_to(shape)

        def rows(d, t):
            return d[bass.ds(t * P, P), :]

        block = ctx.enter_context(nc.Block())

        @block.sync
        def _(sp):
            def load(dst_ap, src_ap, name):
                sp.dma_start(dst_ap, src_ap).then_inc(s(name), 16)

            def row(ap, n):
                return ap.partition_broadcast(n)

            sp.wait_ge(s("edge_pads"), 3)
            for a, t in ((dst, DI), (src, SI), (edge_type, TI)):
                v = t.rearrange("t (b e) -> t b e", b=LB)
                load(v[:, 0:LB - 1, :], a[0:(LB - 1) * LT * P].rearrange("(b t e) -> t b e", b=LB - 1, e=P), "edges_in")
                n = EFULL - (LB - 1) * LT
                load(v[0:n, LB - 1, :], a[(LB - 1) * LT * P:EFULL * P].rearrange("(t e) -> t e", e=P), "edges_in")
                load(v[n:n + 1, LB - 1, 0:ETAIL], a[EFULL * P:E].rearrange("(o e) -> o e", o=1), "edges_in")
            load(X[:, 0:NT - 1, :], x[0:(NT - 1) * P, :].rearrange("(t p) d -> p t d", p=P), "x_in")
            sp.wait_ge(s("x_tail_zero"), 1)
            load(X[0:NTAIL, NT - 1, :], x[(NT - 1) * P:N, :], "x_in")
            for c in range(2):
                load(WALL[:, c, :].rearrange("p (r d) -> p r d", r=RH),
                     conv_w.rearrange("r h i d -> i (r h) d")[c * P:(c + 1) * P], "conv_in")
            load(ATT[:, 0, :], row(attn_l.rearrange("r h d -> (r h d)"), P), "attn_in")
            load(ATT[:, 1, :], row(attn_r.rearrange("r h d -> (r h d)"), P), "attn_in")
            with nc.allow_non_contiguous_dma(reason="small weight columns"):
                load(W1A[0:ED, :], ee_w1, "small_in")
                load(W1A[ED:ED + 1, :], ee_b1.rearrange("(o n) -> o n", o=1), "small_in")
                load(EW2[:, :, :], ee_w2.rearrange("(c p) n -> p c n", p=P), "small_in")
                load(GW[:, :, :], gcn_w.rearrange("(c p) n -> p c n", p=P), "small_in")
                load(CE[:, :], cluster, "small_in")
                load(GB[:, :], row(gcn_b, P), "small_in")
                load(B2C, ee_b2.rearrange("(c p) -> p c", p=P), "small_in")
                load(B1C, ee_b1.rearrange("(c p) -> p c", p=P), "small_in")
                load(SC2, eps.partition_broadcast(P), "small_in")
                for c in range(2):
                    load(ZR[:, 0, c * K:(c + 1) * K], cluster.rearrange("k (c p) -> c p k", p=P)[c], "small_in")
                for i, a in enumerate((g1, be1, g2, be2)):
                    load(COL8[:, i, :], a.rearrange("(c p) -> p c", p=P), "small_in")
            sp.wait_ge(s("relq_ready"), 1)
            load(rel_d.rearrange("(b t e) -> t b e", b=LB, e=P), RELQ.rearrange("t (b e) -> t b e", b=LB), "rel_out")
            sp.wait_ge(s("elr_done"), NT + 2)
            load(el_d.rearrange("(t p) r -> p t r", p=P), ELS, "el_out")
            for i in range(2):
                sp.sem_inc(s(f"rows_out{i}"), 16)
            with sp.Fori(0, NJ) as j:
                for i in range(2):
                    sp.wait_ge(s("tab_free"), (2 * j + i + 1) * 4 + 4)
                    load(rows(feat_d, 2 * j + i), STAGE[:, i, :], f"rows_out{i}")
            sp.wait_ge(s("rel_out"), 16)
            with sp.Fori(0, IT) as u:
                for h in range(2):
                    sp.wait_ge(s("oht_ready"), 2 * u + h + 1)
                    load(RB[:, h, :], rel_d[bass.ds((10 * u + 5 * h) * P, 5 * P)].partition_broadcast(P), f"rb_in{h}")
            sp.wait_ge(s("msg_ready"), T)
            load(HB, row(h_bias, P), "hb_in")
            sp.wait_ge(s("y_ready"), 1)
            load(y_d.rearrange("(t p) k -> p t k", p=P), Y, "y_out")
            load(W1S, w1.rearrange("(c p) n -> p c n", p=P), "mlp_in")
            load(W2S, w2.rearrange("(c p) n -> p c n", p=P), "mlp_in")
            for t, a in ((BR[0], b1), (B3R, b3), (GNR, bn_g), (BNR, bn_b)):
                load(t, row(a, P), "mlp_in")

            ea_even = edge_attr[0:EFULL * P, :].rearrange("(v q p) f -> p v q f", q=2, p=P)

            def edge_rows(par, u, last):
                sp.wait_ge(s("ea_used"), IT * par + u + 1)
                load(EA[:, 0:4, :], ea_even[:, bass.ds(5 * u, 4), par, :], "ea_in")
                if not last:
                    load(EA[:, 4:5, :], ea_even[:, bass.ds(5 * u + 4, 1), par, :], "ea_in")
                elif par == 0:
                    load(EA[0:ETAIL, 4, :], edge_attr[EFULL * P:E, :], "ea_in")
                else:
                    load(EA[:, 4, :], ea_even[:, 5 * u + 3, par, :], "ea_in")

            sp.wait_ge(s("f0_done"), NT + 2)
            with sp.Fori(0, IT - 1) as u:
                edge_rows(0, u, False)
            edge_rows(0, IT - 1, True)
            with sp.Fori(0, NJ) as j:
                for i in range(2):
                    sp.wait_ge(s("n2_hr"), 2 * j + i + 1)
                    load(rows(h2_d, 2 * j + i), HR[:, i, :], f"rows_out{i}")
            with sp.Fori(0, IT - 1) as u:
                edge_rows(1, u, False)
            edge_rows(1, IT - 1, True)
            sp.wait_ge(s("agg_ps"), 3 * T + 20)
            load(BR[1], row(b2, P), "mlp_late")
            load(W3S, w3.rearrange("(c p) n -> p c n", p=P), "mlp_late")
            with sp.Fori(0, NJ) as j:
                for i in range(2):
                    sp.wait_ge(s(f"h2r_free{i}"), j + 1)
                    load(H2R[:, i, :], rows(h2_d, 2 * j + i), f"h2r_in{i}")
            for i in range(2):
                sp.wait_ge(s(f"m_y{i}"), NJ)
            for w, a in ((0, w_l), (1, w_r)):
                load(WRAW[:, w, :, :], a.rearrange("(o p) n -> p o n", p=P), "l3_in")
            for t, a in ((GMR, gamma), (BTR, beta), (BLR, b_l)):
                load(t, row(a, P), "l3_in")
            with sp.Fori(0, NJ) as j:
                for i in range(2):
                    sp.wait_ge(s("n3_hr"), 2 * j + i + 1)
                    load(rows(h3_d, 2 * j + i), HR[:, i, :], f"rows_out{i}")
            with sp.Fori(0, NJ - 1) as j:
                for i in range(2):
                    sp.wait_ge(s("o_ready"), 2 * j + i + 1)
                    load(rows(out, 2 * j + i), HR[:, i, :], f"rows_out{i}")
            sp.wait_ge(s("o_ready"), NT - 1)
            load(out[(NT - 2) * P:(NT - 1) * P, :], HR[:, 0, :], "rows_out0")
            sp.wait_ge(s("o_ready"), NT)
            load(out[(NT - 1) * P:N, :], HR[0:NTAIL, 1, :], "rows_out1")
            for i in range(2):
                sp.wait_ge(s(f"rows_out{i}"), rows_out(3, NJ))
            sp.wait_ge(s("el_out"), 16)
            sp.wait_ge(s("y_out"), 16)

        @block.gpsimd
        def _(pool):
            step = Steps(pool, s("pool_steps"))
            step(pool.memset(IDENT[:, :], 0.0))
            pool.affine_select(out=IDENT[:, :], in_=IDENT[:, :], compare_op=ALU.not_equal, fill=1.0, base=0,
                               pattern=[[-1, P]], channel_multiplier=1).then_inc(s("const_ready"), 1)
            pool.iota(IOTA[:, :], pattern=[[1, P]], base=0, channel_multiplier=0,
                      allow_small_or_imprecise_dtypes=True).then_inc(s("const_ready"), 1)
            pool.iota(IOTP[:, :], pattern=[[P, 2]], base=0, channel_multiplier=1,
                      allow_small_or_imprecise_dtypes=True).then_inc(s("const_ready"), 1)

            def gather(g, table, width, idx):
                with pool.Fori(0, IL) as w:
                    step.enter(w, 2)
                    for b in range(2):
                        u = 2 * w + b
                        if g == 0:
                            pool.wait_ge(s("el_slots"), u + 1)
                        else:
                            pool.wait_ge(s("agg_ps"), T * (g - 1) + 10 * u + 10)
                        step(pool.tensor_copy(IX[:, b, :], idx[:, bass.ds(10 * u, 10)]))
                        pool.nop(nofuse=True)
                        for k in range(10):
                            pool.indirect_dma_start(
                                ELSL[:, b, k, :] if g == 0 else SLOTS[b][:, k, 0:width], None, table,
                                bass.IndirectOffsetOnAxis(ap=IX[:, b, k:k + 1], axis=0),
                            ).then_inc(gath[2 * b + k // 5], 16)
                    step.leave(IL)

            pool.wait_ge(s("idx_ready"), 2)
            pool.wait_ge(s("el_out"), 16)
            gather(0, el_d.rearrange("n (r h) -> (n r) h", r=R), H, IDXST)
            pool.wait_ge(s("el_slots"), IT + 2)
            pool.wait_ge(s("alpha_t"), 1)
            for i in range(2):
                pool.wait_ge(s(f"rows_out{i}"), rows_out(0, NJ))
            gather(1, feat_d.rearrange("n (r d) -> (n r) d", r=R), D, IDXST)
            pool.wait_ge(s("y_out"), 16)
            gather(2, y_d, K, IDXS)
            for i in range(2):
                pool.wait_ge(s(f"rows_out{i}"), rows_out(1, NJ))
            gather(3, h2_d, D, IDXS)
            for i in range(2):
                pool.wait_ge(s(f"rows_out{i}"), rows_out(2, NJ))
            for i in range(2):
                pool.wait_ge(s(f"m_y{i}"), NJ)
            gather(4, h3_d, D, IDXS)

        @block.scalar
        def _(act):
            step = Steps(act, s("act_steps"))

            def rstd(l):
                act.wait_ge(s("norm_stats"), l + 1)
                act.activation(RS[:, :], MV[:, :, 1], ACT.Sqrt, bias=EPSC[:, 0:1]).then_inc(s("norm_sqrt"), 1)
                act.wait_ge(s("norm_scale"), l + 1)

            def norm_rows(l, used):
                rstd(l)
                with act.Fori(0, NJ) as j:
                    for i in range(2):
                        t = 2 * j + i
                        for name, k, c in used:
                            act.wait_ge(s(name.format(i=i)), k(j, t))
                        act.activation(HR[:, i, :], X[:, bass.ds(t, 1), :], ACT.Relu, scale=RS[:, bass.ds(t, 1)],
                                       bias=NB[:, bass.ds(t, 1)]).then_inc(s(f"n{l}_hr"), 1)

            norm_rows(0, [("n0_tp", lambda j, t: t + 1, 0)])
            act.wait_ge(s("small_in"), 16 * 15)
            act.activation(B1C, B1C, ACT.Relu).then_inc(s("b1_relu"), 1)
            act.sem_inc(s("el_slots"), 2)
            with act.Fori(0, IL) as w:
                for b in range(2):
                    for h in range(2):
                        gathered(act, 0, w, b, h)
                    act.activation(ELA[:, bass.ds(10 * (2 * w + b) * H, 10 * H)].rearrange("p (k h) -> p k h", h=H),
                                   ELSL[:, b, :, :], ACT.Copy).then_inc(s("el_slots"), 1)
            act.wait_ge(s("e_ps"), 1)
            step(act.activation(EF, PS[0:LT, 0:H, 0:LB * P], ACT.Copy))
            act.activation(EB, PS[0:LT, 0:H, 0:LB * P], ACT.Copy).then_inc(s("e_sb"), 1)
            act.wait_ge(s("e_shift"), 1)
            act.activation(EX, EX, ACT.Exp).then_inc(s("e_exp"), 1)
            act.wait_ge(s("e_exp"), 1)
            act.activation(EF, EX, ACT.Copy).then_inc(s("x_sb"), 1)
            act.activation(EB, EX, ACT.Copy).then_inc(s("x_sb"), 1)
            act.wait_ge(s("alpha_ready"), 1)
            with act.Fori(0, IL) as w:
                step.enter(w, 4)
                for b in range(2):
                    for h in range(2):
                        t = 10 * (2 * w + b) + 5 * h
                        step(act.activation(ALS[:, h, :], AL[:, bass.ds(t * H, 5 * H)], ACT.Copy))
                        gathered(act, 1, w, b, h)
                        for k in range(5):
                            for q in range(H):
                                v = SLOTS[b][:, 5 * h + k, q * DH:(q + 1) * DH]
                                a = k * H + q
                                last = act.activation(v, v, ACT.Copy, scale=ALS[:, h, a:a + 1])
                            last.then_inc(s("msg_ready"), 1)
                step.leave(IL)

            def take_columns(name, used, planes, parts):
                with act.Fori(0, NJ) as j:
                    for i in range(2):
                        t = 2 * j + i
                        act.wait_ge(s(used), t + 1)
                        act.activation(AR[0:parts, i, 0:planes * P].rearrange("p (a n) -> p a n", a=planes),
                                       ACC[0:parts, 0:planes, bass.ds(t * P, P)], ACT.Copy).then_inc(s(name), 1)

            act.wait_ge(s("added"), T + 10)
            take_columns("f0_ar", "f0_tp", 3, P)
            act.wait_ge(s("f0_done"), NT + 2)
            act.activation(DG[:, :], DG[:, :], ACT.Sqrt, bias=1.0).then_inc(s("dg_sqrt"), 1)
            norm_rows(1, [("n1_tp", lambda j, t: t + 1, 0), ("n1_done", lambda j, t: t + 1, 0)])

            def edge_hidden(par):
                with act.Fori(0, IT) as u:
                    n = IT * par + u
                    act.wait_ge(s("ea_used"), n + 2)
                    act.activation(EAT[0:ED, 0:4, :], PS[0:ED, 2, :].rearrange("p (k n) -> p k n", k=4), ACT.Copy)
                    act.activation(EAT[0:ED, 4, :], PS[0:ED, 3, 0:P], ACT.Copy).then_inc(s("ea_t"), 1)
                    for q in range(3):
                        act.wait_ge(s("hid_ps"), 3 * n + q + 1)
                        act.activation(HM[q], PS[:, 4 + q, 0:512 if q < 2 else D], ACT.Relu).then_inc(s("hid_ready"), 1)

            edge_hidden(0)
            act.wait_ge(s("added"), 2 * T + 10)
            take_columns("f1_ar", "f1_tp", 1, K)
            act.wait_ge(s("z_shift"), 1)
            act.activation(Z, Z, ACT.Exp).then_inc(s("z_exp"), 1)
            act.wait_ge(s("z_soft"), 1)
            with act.Fori(0, NJ) as j:
                for i in range(2):
                    t = 2 * j + i
                    act.wait_ge(s("g1_tp"), t + 1)
                    act.activation(SR[:, i, :], Z[:, bass.ds(t, 1), :], ACT.Copy).then_inc(s("g1_sr"), 1)
                for i in range(2):
                    t = 2 * j + i
                    act.wait_ge(s("g1_tp"), t + 3)
                    act.wait_ge(s("g1_mm"), t + 1)
                    act.activation(STR[:, i, :], PS[0:K, 2 + i, 0:P], ACT.Copy).then_inc(s("g1_st"), 1)
            norm_rows(2, [("n2_tp", lambda j, t: t + 1, 0), ("rows_out{i}", lambda j, t: rows_out(1, j), 0)])
            edge_hidden(1)

            def hidden_norm(i, j, l):
                n = 2 * j + l + 1
                act.wait_ge(s(f"m_var{i}"), n)
                act.activation(SM[:, i, 2:3], SM[:, i, 1:2], ACT.Sqrt, bias=EPSC[:, 0:1]).then_inc(s(f"m_sqrt{i}"), 1)
                act.wait_ge(s(f"m_scale{i}"), n)
                act.activation(ZR[:, i, :], ZR[:, i, :], ACT.Identity, scale=SM[:, i, 3:4],
                               bias=SM[:, i, 4:5]).then_inc(s(f"m_z{i}"), 1)

            def hidden_relu(i, j, l):
                act.wait_ge(s(f"m_t{i}"), 2 * j + l + 1)
                for c in range(KH):
                    last = act.activation(H1T[:, i, c, :], PS[:, 4 + 2 * i + c // 4, (c % 4) * P:(c % 4 + 1) * P],
                                          ACT.Relu, scale=COL8[:, 2 * l, c:c + 1], bias=COL8[:, 2 * l + 1, c:c + 1])
                last.then_inc(s(f"m_h{i}"), 1)

            def dense_pair(j, more):
                hidden_relu(0, j, 0)
                hidden_norm(1, j, 0)
                hidden_relu(1, j, 0)
                hidden_norm(0, j, 1)
                hidden_relu(0, j, 1)
                hidden_norm(1, j, 1)
                hidden_relu(1, j, 1)
                if more:
                    hidden_norm(0, j + 1, 0)
                for i in range(2):
                    act.wait_ge(s(f"y_var{i}"), j + 1)
                    act.activation(YM[:, i, 2:3], YM[:, i, 1:2], ACT.Sqrt, bias=EPSC[:, 0:1]).then_inc(s(f"y_sqrt{i}"), 1)

            hidden_norm(0, 0, 0)
            with act.Fori(0, NJ - 1) as j:
                dense_pair(j, True)
            dense_pair(NJ - 1, False)
            rstd(3)
            with act.Fori(0, NJ) as j:
                for i in range(2):
                    t = 2 * j + i
                    act.wait_ge(s("n3_tp"), t + 1)
                    act.wait_ge(s(f"rows_out{i}"), rows_out(2, j))
                    act.activation(HR[:, i, :], X[:, bass.ds(t, 1), :], ACT.Relu, scale=RS[:, bass.ds(t, 1)],
                                   bias=NB[:, bass.ds(t, 1)]).then_inc(s("n3_in"), 1)
                for i in range(2):
                    act.wait_ge(s("n3_var"), 2 * j + i + 1)
                    act.activation(SM[:, i, 2:3], SM[:, i, 1:2], ACT.Sqrt, bias=EPSC[:, 0:1]).then_inc(s("n3_sqrt"), 1)

        @block.tensor
        def _(pe):
            def turn(out_ap, in_ap, k):
                return pe.transpose(out_ap, in_ap, IDENT[0:k, 0:k])

            pe.sem_inc(s("agg_ps"), 20)
            pe.wait_ge(s("const_ready"), 3)
            pe.wait_ge(s("prep_ready"), 1)
            for bank, a in enumerate((RELF, SF, STF, TF)):
                for b in range(LB):
                    last = turn(PS[:, bank, b * LT:(b + 1) * LT], a[:, b * P:(b + 1) * P], LT)
            for bank, q in ((4, 0), (5, 2)):
                for b in range(LB):
                    last = turn(PS[0:1, bank, b * LT:(b + 1) * LT], QC[:, q, b:b + 1], LT)
            last.then_inc(s("prep_t"), 1)
            pe.wait_ge(s("csum_rows"), 1)
            for c in range(2):
                last = pe.matmul(PS[:, 6, 0:K], HTR[:, 0, c, :], GW[:, c, :], start=(c == 0), stop=(c == 1))
            last.then_inc(s("cw_ps"), 1)
            pe.wait_ge(s("prep_used"), 1)

            def norm_turn(l, t, i):
                pe.wait_ge(s(f"n{l}_hr"), t + 1)
                turn(PS[:, i, 0:P], HR[:, i, 0:P], P)
                turn(PS[:, i, P:D], HR[:, i, P:D], P).then_inc(s(f"n{l}_tp"), 1)

            pe.sem_inc(s("n0_tp"), 2)
            pe.wait_ge(s("aw_ready"), 1)
            with pe.Fori(0, NJ) as j:
                for i in range(2):
                    norm_turn(0, 2 * j + i, i)
                for i in range(2):
                    t = 2 * j + i
                    pe.wait_ge(s("n0_ht"), t + 1)
                    pe.wait_ge(s("elr_done"), t + 1)
                    for c in range(2):
                        last = pe.matmul(PS[:, 2 + i, 0:2 * RH], HTR[:, i, c, :], AW_[:, c, :],
                                         start=(c == 0), stop=(c == 1))
                    last.then_inc(s("elr_ps"), 1)
            pe.sem_inc(s("tab_ps"), 8)
            with pe.Fori(0, NJ) as j:
                for i in range(2):
                    t = 2 * j + i
                    pe.wait_ge(s("tab_in"), t + 1)
                    for q in range(4):
                        pe.wait_ge(s("tab_free"), 4 * t + q + 1)
                        for c in range(2):
                            last = pe.matmul(PS[:, 4 + q, :], HTR[:, i, c, :], WALL[:, c, q * 512:(q + 1) * 512],
                                             start=(c == 0), stop=(c == 1))
                        last.then_inc(s("tab_ps"), 1)
            pe.wait_ge(s("er_parts"), 1)
            with pe.Fori(0, IT) as u:
                _, qs = nc.values_load_multi_w_load_instructions(
                    QR[:, bass.ds(10 * u, 10)], engines=[PE], min_val=0, max_val=(NT - 1) * 3 * RH,
                    skip_runtime_bounds_check_because="clamped to the last node tile when it was computed")
                for h in range(2):
                    pe.wait_ge(s("oht_ready"), 2 * u + h + 3)
                    pe.wait_ge(s("er_done"), 2 * u + h + 1)
                    for k in range(5):
                        o = PS[:, h, k * 3 * RH:(k + 1) * 3 * RH]
                        q = qs[5 * h + k]
                        pe.matmul(o, OHT[:, h, 0, k * P:(k + 1) * P], ERB[:, bass.ds(q, 3 * RH)], start=True, stop=False)
                        last = pe.matmul(o, OHT[:, h, 1, k * P:(k + 1) * P], ERB[:, bass.ds(q + 3 * RH, 3 * RH)],
                                         start=False, stop=True)
                    last.then_inc(s("er_ps"), 1)
            pe.wait_ge(s("e_all"), 1)
            ev = AL[:, 0:T * H].rearrange("p (t h) -> p t h", h=H)
            for h in range(H):
                for b in range(LB):
                    last = turn(PS[0:LT, h, b * P:(b + 1) * P], ev[:, b * LT:(b + 1) * LT, h], P)
            last.then_inc(s("e_ps"), 1)
            for b in range(LB):
                turn(PS[0:H, 4, b * LT:(b + 1) * LT], REP[:, 0, b, :], LT)
                last = turn(PS[0:H, 5, b * LT:(b + 1) * LT], REP[:, 1, b, :], LT)
            last.then_inc(s("rep_ps"), 1)
            for r in range(2):
                pe.wait_ge(s("ends"), r + 1)
                for b in range(LB):
                    turn(PS[0:H, 6, b * LT:(b + 1) * LT], QE[:, 0, b, :], LT)
                    last = turn(PS[0:H, 7, b * LT:(b + 1) * LT], QE[:, 1, b, :], LT)
                last.then_inc(s("ends_ps"), 1)
                pe.wait_ge(s("carry"), r + 1)
                for b in range(LB):
                    turn(PS[0:LT, 4, b * H:(b + 1) * H], CF[:, b * LT:(b + 1) * LT], H)
                    last = turn(PS[0:LT, 5, b * H:(b + 1) * H], CBK[:, b * LT:(b + 1) * LT], H)
                last.then_inc(s("carry_ps"), 1)
            pe.wait_ge(s("alpha_t"), 1)
            for b in range(LB):
                for h in range(H):
                    last = turn(PS[:, b, h * LT:(h + 1) * LT], EX[:, h, b * P:(b + 1) * P], LT)
            last.then_inc(s("alpha_ps"), 1)

            def edge_sums(g, planes, par=None):
                def agg(w, b, k):
                    u = 2 * w + b
                    n = T * (g - 1) + 10 * u + k
                    rows_in = SLOTS[b]
                    if g == 1:
                        pe.wait_ge(s("msg_ready"), 10 * u + k + 1)
                    elif k % 5 == 0:
                        gathered(pe, g, w, b, k // 5)
                    if k % 5 == 0:
                        pe.wait_ge(s("oh_ready"), oh_count(g, u, k // 5))
                    pe.wait_ge(s("added"), n + 9)
                    if g == 2:
                        pe.matmul(PS[0:K, k % 2, 0:P], rows_in[:, k, 0:K], OH[:, k, :], start=True, stop=True)\
                            .then_inc(s("agg_ps"), 1)
                        return
                    for c in range(planes):
                        w = ONES[:, :] if c == 2 else rows_in[:, k, c * P:(c + 1) * P]
                        last = pe.matmul(PS[:, k % 2, c * P:(c + 1) * P], w, OH[:, k, :], start=True, stop=True)
                    last.then_inc(s("agg_ps"), 1)

                def net_turn(v, sums):
                    pe.wait_ge(s("ea_in"), 32 * (v + 1))
                    pe.wait_ge(s("hs_added"), sums + 1)
                    pe.nop(nofuse=True)
                    for kk in range(5):
                        last = turn(PS[0:ED, 2 + kk // 4, (kk % 4) * P:(kk % 4 + 1) * P], EA[:, kk, :], P)
                    last.then_inc(s("ea_used"), 1)

                def hidden(v, q):
                    pe.wait_ge(s("ea_t"), v + 1)
                    for kk in range(2 * q, min(2 * q + 2, 5)):
                        last = pe.matmul(PS[:, 4 + q, (kk % 2) * D:(kk % 2 + 1) * D], EAT[:, kk, :], W1A[:, :],
                                         start=True, stop=True)
                    last.then_inc(s("hid_ps"), 1)

                def hidden_sum(u, v, kk, more):
                    m = 5 * v + kk
                    pe.wait_ge(s("hid_ready"), 3 * v + kk // 2 + 1)
                    pe.wait_ge(s("oh_ready"), oh_count(g, u, (2 * kk + par) // 5))
                    if kk == 1 and more:
                        pe.wait_ge(s("ea_t"), v + 2)
                    pe.wait_ge(s("hs_added"), m + (1 if kk == 0 else 0))
                    for c in range(2):
                        o = (kk % 2) * D + c * P
                        last = pe.matmul(PS[:, 7 - 4 * (kk % 2), c * P:(c + 1) * P], HM[kk // 2][:, o:o + P],
                                         OH[:, 2 * kk + par, :], start=True, stop=True)
                    last.then_inc(s("hs_ps"), 1)

                def step_pair(w, end):
                    for b in range(2):
                        u = 2 * w + b
                        for k in range(10):
                            agg(w, b, k)
                            for what, q in EDGE_ORDER[k] if par is not None else []:
                                v = IT * par + u
                                if what == "sum":
                                    hidden_sum(u, v, q, not (end and b == 1))
                                elif what == "hidden" and not (end and b == 1):
                                    hidden(v + 1, q)
                                elif what == "turn" and not end:
                                    net_turn(v + 2, 5 * v + 4)

                if par is not None:
                    net_turn(IT * par, 5 * IT * par)
                    for q in range(3):
                        hidden(IT * par, q)
                    net_turn(IT * par + 1, 5 * IT * par)
                with pe.Fori(0, IL - 1) as w:
                    step_pair(w, False)
                step_pair(IL - 1, True)

            edge_sums(1, 3)
            pe.sem_inc(s("f0_tp"), 2)
            with pe.Fori(0, NJ) as j:
                for i in range(2):
                    t = 2 * j + i
                    pe.wait_ge(s("f0_ar"), t + 1)
                    pe.wait_ge(s("f0_done"), t + 1)
                    for c in range(3):
                        last = turn(PS[:, i, c * P:(c + 1) * P], AR[:, i, c * P:(c + 1) * P], P)
                    last.then_inc(s("f0_tp"), 1)
            pe.sem_inc(s("n1_tp"), 2)
            with pe.Fori(0, NJ) as j:
                for i in range(2):
                    norm_turn(1, 2 * j + i, i)
                for i in range(2):
                    t = 2 * j + i
                    pe.wait_ge(s("n1_ht"), t + 1)
                    pe.wait_ge(s("n1_done"), t + 1)
                    for c in range(2):
                        last = pe.matmul(PS[:, 2 + i, 0:K], HTR[:, i, c, :], GW[:, c, :], start=(c == 0), stop=(c == 1))
                    last.then_inc(s("n1_ps"), 1)
            pe.sem_inc(s("ea_used"), 1)
            pe.wait_ge(s("b1_relu"), 1)
            for f in range(2):
                for c in range(2):
                    last = pe.matmul(PS[:, 6, f:f + 1], EW2[:, c, f * P:(f + 1) * P], B1C[:, c:c + 1],
                                     start=(c == 0), stop=(c == 1))
            last.then_inc(s("cb2_ps"), 1)
            edge_sums(2, 1, par=0)
            pe.sem_inc(s("f1_tp"), 2)
            with pe.Fori(0, NJ) as j:
                for i in range(2):
                    t = 2 * j + i
                    pe.wait_ge(s("f1_ar"), t + 1)
                    pe.wait_ge(s("f1_done"), t + 1)
                    pe.nop(nofuse=True)
                    turn(PS[:, i, 0:K], AR[0:K, i, 0:P], K).then_inc(s("f1_tp"), 1)
            pe.sem_inc(s("g1_tp"), 2)
            pe.sem_inc(s("g1_mm"), 2)
            with pe.Fori(0, NJ) as j:
                for i in range(2):
                    t = 2 * j + i
                    pe.wait_ge(s("g1_sr"), t + 1)
                    pe.nop(nofuse=True)
                    turn(PS[0:K, 2 + i, 0:P], SR[:, i, :], P).then_inc(s("g1_tp"), 1)
                for i in range(2):
                    t = 2 * j + i
                    pe.wait_ge(s("g1_st"), t + 1)
                    pe.wait_ge(s("g1_done"), t + 1)
                    pe.matmul(PS[:, 4 + i, 0:D], STR[:, i, :], CE[:, :], start=True, stop=True)\
                        .then_inc(s("g1_mm"), 1)
            pe.sem_inc(s("n2_tp"), 2)
            with pe.Fori(0, NJ) as j:
                for i in range(2):
                    pe.wait_ge(s("n2_done"), 2 * j + i + 1)
                    norm_turn(2, 2 * j + i, i)
            edge_sums(3, 2, par=1)
            pe.wait_ge(s("mlp_in"), 16 * 6)
            pe.wait_ge(s("added"), 3 * T + 10)
            pe.wait_ge(s("hs_added"), T + 1)

            def edge_part(i, j):
                for f in range(2):
                    for c in range(2):
                        last = pe.matmul(PS[:, 2 * i, f * P:(f + 1) * P], EW2[:, c, f * P:(f + 1) * P],
                                         HS[:, c, bass.ds((2 * j + i) * P, P)], start=(c == 0), stop=(c == 1))
                last.then_inc(s(f"m_ee{i}"), 1)

            def dense(i, lhs, w, banks, width, to):
                kc = w.shape[1]
                for q in banks:
                    for c in range(kc):
                        last = pe.matmul(PS[:, to + q, 0:width], lhs[:, i, c, :], w[:, c, q * width:(q + 1) * width],
                                         start=(c == 0), stop=(c == kc - 1))
                return last

            def dense1(i, j):
                pe.wait_ge(s(f"m_hin{i}"), j + 1)
                dense(i, HIN, W1S, range(2), 512, 2 * i).then_inc(s(f"m_ps{i}"), 1)

            def dense2(i, j, q):
                pe.wait_ge(s(f"m_h{i}"), 2 * j + 1)
                last = dense(i, H1T, W2S, [q], 512, 2 * i)
                if q == 1:
                    last.then_inc(s(f"m_ps{i}"), 1)

            def dense3(i, j):
                pe.wait_ge(s(f"m_h{i}"), 2 * j + 2)
                dense(i, H1T, W3S, [0], D, 4 + 2 * i).then_inc(s(f"m_y{i}"), 1)

            def turn_hidden(i, j, l):
                pe.wait_ge(s(f"m_z{i}"), 2 * j + l + 1)
                if l == 0:
                    pe.wait_ge(s(f"m_out{i}"), j + 1)
                for c in range(KH):
                    last = turn(PS[:, 4 + 2 * i + c // 4, (c % 4) * P:(c % 4 + 1) * P], ZR[:, i, c * P:(c + 1) * P], P)
                last.then_inc(s(f"m_t{i}"), 1)

            def dense_pair(j, more):
                edge_part(1, j)
                turn_hidden(0, j, 0)
                dense1(1, j)
                dense2(0, j, 0)
                turn_hidden(1, j, 0)
                dense2(0, j, 1)
                dense2(1, j, 0)
                turn_hidden(0, j, 1)
                if more:
                    pe.wait_ge(s("m_var0"), 2 * j + 2)
                    edge_part(0, j + 1)
                dense2(1, j, 1)
                if more:
                    dense1(0, j + 1)
                turn_hidden(1, j, 1)
                dense3(0, j)
                dense3(1, j)

            edge_part(0, 0)
            dense1(0, 0)
            pe.wait_ge(s("mlp_late"), 32)
            with pe.Fori(0, NJ - 1) as j:
                dense_pair(j, True)
            dense_pair(NJ - 1, False)
            pe.wait_ge(s("l3_in"), 16 * 5)
            for w in range(2):
                for c in range(2):
                    for o in range(2):
                        last = turn(PS[:, 2 + w, (2 * c + o) * P:(2 * c + o + 1) * P], WRAW[:, w, o, c * P:(c + 1) * P], P)
            last.then_inc(s("w3_ps"), 1)
            pe.sem_inc(s("n3_tp"), 2)
            pe.wait_ge(s("w3_sb"), 2)
            with pe.Fori(0, NJ) as j:
                for i in range(2):
                    norm_turn(3, 2 * j + i, i)
                for i in range(2):
                    t = 2 * j + i
                    pe.wait_ge(s("n3_ht"), t + 1)
                    pe.wait_ge(s("n3_done"), t + 1)
                    for c in range(2):
                        last = pe.matmul(PS[:, 4 + i, 0:D], HTR[:, i, c, :], WLR[:, 1, c, :], start=(c == 0), stop=(c == 1))
                    last.then_inc(s("n3_ps"), 1)
            edge_sums(4, 2)
            pe.sem_inc(s("o_ps"), 2)
            with pe.Fori(0, NJ) as j:
                for i in range(2):
                    t = 2 * j + i
                    pe.wait_ge(s("o_ar"), t + 1)
                    pe.wait_ge(s("o_free"), t + 1)
                    for c in range(2):
                        last = pe.matmul(PS[:, i, 0:D], AR[:, i, c * P:(c + 1) * P], WLR[:, 0, c, :],
                                         start=(c == 0), stop=(c == 1))
                    last.then_inc(s("o_ps"), 1)

        @block.vector
        def _(dve):
            step = Steps(dve, s("dve_steps"))
            tt, ts, stt, cp = dve.tensor_tensor, dve.tensor_scalar, dve.scalar_tensor_tensor, dve.tensor_copy

            for t, v in ((DI, int(PAD_DST)), (SI, 0), (TI, 0)):
                dve.memset(t, v).then_inc(s("edge_pads"), 1)
            dve.memset(X[:, NT - 1, :], 0.0).then_inc(s("x_tail_zero"), 1)
            step(dve.memset(EPSC[:, :], LN_EPS))
            step(dve.memset(ONES[:, :], 1.0))
            dve.wait_ge(s("edges_in"), 16 * 9)
            v3 = lambda a: a.rearrange("t (b e) -> t b e", b=LB)
            step(cp(DF, DI))
            step(cp(SF, SI))
            step(cp(TF, TI))
            step(stt(out=STF, in0=SF, scalar=float(R), in1=TF, op0=ALU.mult, op1=ALU.add))
            step(ts(QC[:, 0, :], v3(DF)[:, :, 0], float(N), None, ALU.min))
            step(cp(QI[:, 0, :], QC[:, 0, :]))
            step(ts(QI[:, 1, :], QI[:, 0, :], 7, 7, ALU.logical_shift_right, ALU.logical_shift_left))
            step(cp(QC[:, 1, :], QI[:, 1, :]))
            step(ts(QC[:, 2, :], QC[:, 1, :], 3.0 * RH / P, None, ALU.mult))
            step(tt(v3(RELF), v3(DF), bc(QC[:, 0, :].unsqueeze(2), [LT, LB, P]), ALU.subtract))
            tt(v3(RELQ), v3(DF), bc(QC[:, 1, :].unsqueeze(2), [LT, LB, P]), ALU.subtract).then_inc(s("relq_ready"), 1)
            step(dve.memset(MF, 0.0))
            step(dve.memset(MB, 0.0))
            step(tt(v3(MF)[:, :, 1:P], v3(DF)[:, :, 1:P], v3(DF)[:, :, 0:P - 1], ALU.is_equal))
            step(cp(v3(MB)[:, :, 0:P - 1], v3(MF)[:, :, 1:P]))
            step(ts(MFN, MF, BIG, -BIG, ALU.mult, ALU.add))
            step(ts(MBN, MB, BIG, -BIG, ALU.mult, ALU.add))
            step(cp(REP[:, 0, :, :], bc(v3(DF)[:, :, 0:1], [LT, LB, H])))
            cp(REP[:, 1, :, :], bc(v3(DF)[:, :, P - 1:P], [LT, LB, H])).then_inc(s("prep_ready"), 1)
            dve.wait_ge(s("prep_t"), 1)
            dve.wait_ge(s("const_ready"), 3)
            cp(IDXST[:, :], PS[:, 2, 0:T]).then_inc(s("idx_ready"), 1)
            cp(IDXS[:, :], PS[:, 1, 0:T]).then_inc(s("idx_ready"), 1)
            step(cp(DREL[:, 0:T], PS[:, 0, 0:T]))
            step(cp(DREL[:, T:T + 5], PS[:, 0, 0:5]))
            step(cp(BASE[:, :], PS[0:1, 4, 0:T]))
            step(cp(QR, PS[0:1, 5, 0:T]))
            step(tt(TM, bc(PS[:, 3, 0:T].unsqueeze(2), [P, T, R]), bc(IOTA[:, 0:R].unsqueeze(1), [P, T, R]), ALU.is_equal))
            dve.wait_ge(s("small_in"), 16 * 15)
            step(dve.tensor_reduce(CSUM, ZR[:, 0, 0:2 * K].rearrange("p (c k) -> p c k", c=2), AX, ALU.add))
            cp(HTR[:, 0, :, :], bc(CSUM.unsqueeze(2), [P, 2, P])).then_inc(s("csum_rows"), 1)
            dve.wait_ge(s("cw_ps"), 1)
            cp(CW[:, :], PS[:, 6, 0:K]).then_inc(s("prep_used"), 1)

            def row_stats():
                for t in range(NT):
                    last = dve.bn_stats(XST[:, t, :], X[:, t, :])
                step(last)
                for t in range(NT):
                    last = dve.bn_aggr(MV[:, t, :], XST[:, t, :])
                step(last)

            def norm_scale(l):
                dve.engine_nop().then_inc(s("norm_stats"), 1)
                dve.wait_ge(s("norm_sqrt"), l + 1)
                step(dve.reciprocal(RS[:, :], RS[:, :]))
                stt(out=NB[:, :], in0=MV[:, :, 0], scalar=-1.0, in1=RS[:, :], op0=ALU.mult, op1=ALU.mult)\
                    .then_inc(s("norm_scale"), 1)

            dve.wait_ge(s("x_in"), 32)
            row_stats()
            norm_scale(0)
            dve.wait_ge(s("conv_in"), 32)
            dve.wait_ge(s("attn_in"), 32)
            for c in range(2):
                for a in range(2):
                    step(tt(HT[:, 0, 0:R * D], WALL[:, c, :], ATT[:, a, :], ALU.mult))
                    step(dve.tensor_reduce(AW_[:, c, a * RH:(a + 1) * RH],
                                           HT[:, 0, 0:R * D].rearrange("p (r d) -> p r d", d=DH), AX, ALU.add))
            dve.engine_nop().then_inc(s("aw_ready"), 1)
            dve.sem_inc(s("elr_done"), 2)
            with dve.Fori(0, NJ) as j:
                step.enter(j, 4)
                for i in range(2):
                    t = 2 * j + i
                    dve.wait_ge(s("n0_tp"), t + 3)
                    pv = PS[:, i, 0:D].rearrange("p (c n) -> p c n", c=2)
                    step(cp(HT[:, :, bass.ds(t * P, P)], pv))
                    mine(dve, cp(HTR[:, i, :, :], pv), "n0_ht", t + 1)
                for i in range(2):
                    t = 2 * j + i
                    dve.wait_ge(s("elr_ps"), t + 1)
                    step(cp(ER[:, bass.ds(t * RH, RH)], PS[:, 2 + i, RH:2 * RH]))
                    mine(dve, cp(ELS[:, bass.ds(t, 1), :].rearrange("p a n -> p (a n)"), PS[:, 2 + i, 0:RH]),
                         "elr_done", t + 3)
                step.leave(NJ)
            dve.sem_inc(s("tab_free"), 4)
            with dve.Fori(0, NJ) as j:
                for i in range(2):
                    t = 2 * j + i
                    dve.wait_ge(s("tab_ps"), 4 * t + 4)
                    mine(dve, cp(HTR[:, i, :, :], HT[:, :, bass.ds(t * P, P)]), "tab_in", t + 1)
                    dve.wait_ge(s(f"rows_out{i}"), rows_out(0, j))
                    for q in range(4):
                        dve.wait_ge(s("tab_ps"), 4 * t + q + 9)
                        cp(STAGE[:, i, q * 512:(q + 1) * 512], PS[:, 4 + q, :]).then_inc(s("tab_free"), 1)
            er3 = ERB.rearrange("p (t a r) -> p t a r", a=3, r=RH)
            er1 = ER.rearrange("p (t r) -> p t r", r=RH)
            dve.wait_ge(s("tab_ps"), 4 * NT + 8)
            step(dve.memset(er3[:, NT:NT + 1, :, :], 0.0))
            for a in range(3):
                step(cp(er3[:, 0:NT, a, :], er1))
                if a < 2:
                    step(tt(er1, er1, er3[:, 0:NT, a, :], ALU.subtract))
            dve.engine_nop().then_inc(s("er_parts"), 1)
            dve.sem_inc(s("oht_ready"), 2)
            dve.sem_inc(s("er_done"), 2)
            with dve.Fori(0, IT) as u:
                step.enter(u, 4)
                for h in range(2):
                    dve.wait_ge(s(f"rb_in{h}"), 16 * (u + 1))
                    step(ts(OHT[:, h, 0, :], RB[:, h, :], IOTP[:, 0:1], None, ALU.is_equal))
                    mine(dve, ts(OHT[:, h, 1, :], RB[:, h, :], IOTP[:, 1:2], None, ALU.is_equal),
                         "oht_ready", 2 * u + h + 3)
                for h in range(2):
                    dve.wait_ge(s("er_ps"), 2 * u + h + 1)
                    for k in range(5):
                        tm = bc(TM[:, bass.ds(10 * u + 5 * h + k, 1), :].rearrange("p o r -> p (o r)")
                                .unsqueeze(1).unsqueeze(3), [P, 3, R, H])
                        kr = slice(k * 3 * RH, (k + 1) * 3 * RH)
                        last = tt(TMP[:, h, kr].rearrange("p (a r h) -> p a r h", a=3, r=R),
                                  PS[:, h, kr].rearrange("p (a r h) -> p a r h", a=3, r=R), tm, ALU.mult)
                    step(last)
                    mine(dve, dve.tensor_reduce(
                        AL[:, bass.ds((10 * u + 5 * h) * H, 5 * H)].rearrange("p (k h) -> p k h", h=H),
                        TMP[:, h, :].rearrange("p (k r h) -> p k h r", k=5, h=H), AX, ALU.add), "er_done", 2 * u + h + 3)
                step.leave(IT)
            dve.wait_ge(s("el_slots"), IT + 2)
            step(tt(AL[:, 0:T * H], AL[:, 0:T * H], ELA, ALU.add))
            stt(out=AL[:, 0:T * H], in0=AL[:, 0:T * H], scalar=0.2, in1=AL[:, 0:T * H], op0=ALU.mult, op1=ALU.max)\
                .then_inc(s("e_all"), 1)
            DFR, DLR, J, W, KF, KB, KFN, KBN, JN, SFR, SBR = ROWS[0:11]
            for i in range(2):
                dve.wait_ge(s(f"rows_out{i}"), rows_out(0, NJ))
            dve.wait_ge(s("rep_ps"), 1)
            step(cp(DFR[:, 0:T], PS[0:H, 4, 0:T]))
            step(cp(DLR[:, 0:T], PS[0:H, 5, 0:T]))
            step(dve.memset(J, 0.0))
            step(tt(J[:, 1:T], DFR[:, 1:T], DLR[:, 0:T - 1], ALU.is_equal))
            step(tt(W[:, 0:T], DFR[:, 0:T], DLR[:, 0:T], ALU.is_equal))
            step(tt(KF[:, 0:T], W[:, 0:T], J[:, 0:T], ALU.mult))
            step(tt(KB[:, 0:T], W[:, 0:T], J[:, 1:T + 1], ALU.mult))
            step(ts(KFN[:, 0:T], KF[:, 0:T], BIG, -BIG, ALU.mult, ALU.add))
            step(ts(KBN[:, 0:T], KB[:, 0:T], BIG, -BIG, ALU.mult, ALU.add))
            step(ts(JN, J, BIG, -BIG, ALU.mult, ALU.add))

            v4 = lambda a: a.rearrange("t h (b e) -> t h b e", b=LB)

            def segment(r, op0, op1, none, mf, mb, kf, kb, jn):
                def scans():
                    for h in range(H):
                        step(dve.tensor_tensor_scan(FS[:, h, :], mf, EF[:, h, :], none, op0, op1))
                        step(dve.tensor_tensor_scan(BS[:, h, ::-1], mb[:, ::-1], EB[:, h, ::-1], none, op0, op1))

                scans()
                step(cp(QE[:, 0, :, :].rearrange("t b h -> t h b"), v4(FS)[:, :, :, P - 1]))
                cp(QE[:, 1, :, :].rearrange("t b h -> t h b"), v4(BS)[:, :, :, 0]).then_inc(s("ends"), 1)
                dve.wait_ge(s("ends_ps"), r + 1)
                step(dve.memset(SFR[:, 0:1], none))
                step(dve.memset(SBR[:, T:T + 1], none))
                step(dve.tensor_tensor_scan(SFR[:, 1:T + 1], kf[:, 0:T], PS[0:H, 6, 0:T], none, op0, op1))
                step(dve.tensor_tensor_scan(SBR[:, 0:T][:, ::-1], kb[:, 0:T][:, ::-1], PS[0:H, 7, 0:T][:, ::-1],
                                            none, op0, op1))
                step(tt(CF[:, 0:T], SFR[:, 0:T], jn[:, 0:T], op0))
                tt(CBK[:, 0:T], SBR[:, 1:T + 1], jn[:, 1:T + 1], op0).then_inc(s("carry"), 1)
                dve.wait_ge(s("carry_ps"), r + 1)
                c4 = PS[0:LT, 4:6, 0:LB * H].rearrange("t w (b h) -> t w h b", b=LB)
                step(tt(v4(EF)[:, :, :, 0], v4(EF)[:, :, :, 0], c4[:, 0], op1))
                step(tt(v4(EB)[:, :, :, P - 1], v4(EB)[:, :, :, P - 1], c4[:, 1], op1))
                scans()

            dve.wait_ge(s("e_sb"), 1)
            segment(0, ALU.add, ALU.max, -BIG, MFN, MBN, KFN, KBN, JN)
            step(tt(FS, FS, BS, ALU.max))
            tt(EX, PS[0:LT, 0:H, 0:LB * P], FS, ALU.subtract).then_inc(s("e_shift"), 1)
            dve.wait_ge(s("x_sb"), 2)
            segment(1, ALU.mult, ALU.add, 0.0, MF, MB, KF, KB, J)
            step(tt(FS, FS, BS, ALU.add))
            step(tt(FS, FS, EX, ALU.subtract))
            step(dve.reciprocal(FS, FS))
            tt(EX, EX, FS, ALU.mult).then_inc(s("alpha_t"), 1)
            dve.wait_ge(s("alpha_t"), 1)
            step(dve.memset(ACC[:, :, :], 0.0))
            dve.wait_ge(s("alpha_ps"), 1)
            cp(AL[:, 0:T * H].rearrange("p (b t h) -> p b h t", b=LB, h=H),
               PS[:, 0:LB, 0:LT * H].rearrange("p b (h t) -> p b h t", h=H)).then_inc(s("alpha_ready"), 1)

            dve.sem_inc(s("added"), 10)

            def edge_adds(g, parts, planes, par=None):
                def one_hot(u, h):
                    k = slice(5 * (h % 2), 5 * (h % 2) + 5)
                    mine(dve, tt(OH[:, k, :], bc(IOTA[:, :].unsqueeze(1), [P, 5, P]),
                                 bc(DREL[:, bass.ds(10 * u + 5 * h, 5)].unsqueeze(2), [P, 5, P]), ALU.is_equal),
                         "oh_ready", oh_count(g, u, h))

                one_hot(0, 0)
                with dve.Fori(0, IL) as w:
                    for b in range(2):
                        u = 2 * w + b
                        one_hot(u, 1)
                        _, base = nc.values_load_multi_w_load_instructions(
                            BASE[:, bass.ds(10 * u, 10)], engines=[DVE], min_val=0, max_val=N,
                            skip_runtime_bounds_check_because="clamped to N when it was computed")
                        for k in range(10):
                            n = T * (g - 1) + 10 * u + k
                            dve.wait_ge(s("agg_ps"), n + 21)
                            dve.wait_ge(s("added"), n + 10)
                            a = ACC[0:parts, 0:planes, bass.ds(base[k], P)]
                            tt(a, a, PS[0:parts, k % 2, 0:planes * P].rearrange("p (a n) -> p a n", a=planes),
                               ALU.add).then_inc(s("added"), 1)
                            for what, kk in EDGE_ORDER[k] if par is not None else []:
                                if what == "sum":
                                    m = 5 * (IT * par + u) + kk
                                    dve.wait_ge(s("hs_ps"), m + 1)
                                    dve.wait_ge(s("hs_added"), m + 1)
                                    a = HS[:, :, bass.ds(base[2 * kk + par], P)]
                                    hv = PS[:, 7 - 4 * (kk % 2), 0:D].rearrange("p (a n) -> p a n", a=2)
                                    tt(a, a, hv, ALU.add).then_inc(s("hs_added"), 1)
                            if k == 6:
                                one_hot(u, 2)
                dve.wait_ge(s("added"), T * g + 10)

            edge_adds(1, P, 3)
            dve.wait_ge(s("hb_in"), 16)
            dve.sem_inc(s("f0_done"), 2)
            with dve.Fori(0, NJ) as j:
                step.enter(j, 4)
                for i in range(2):
                    t = 2 * j + i
                    dve.wait_ge(s("f0_tp"), t + 3)
                    xt = X[:, bass.ds(t, 1), :].rearrange("p a d -> p (a d)")
                    step(tt(xt, xt, PS[:, i, 0:D], ALU.add))
                    step(tt(xt, xt, HB, ALU.add))
                    mine(dve, cp(DG[:, bass.ds(t, 1)], PS[:, i, D:D + 1]), "f0_done", t + 3)
                step.leave(NJ)
            row_stats()
            dve.wait_ge(s("dg_sqrt"), 1)
            step(dve.reciprocal(DG[:, :], DG[:, :]))
            norm_scale(1)
            dve.sem_inc(s("n1_done"), 2)
            with dve.Fori(0, NJ) as j:
                step.enter(j, 2)
                for i in range(2):
                    t = 2 * j + i
                    dve.wait_ge(s("n1_tp"), t + 3)
                    mine(dve, cp(HTR[:, i, :, :], PS[:, i, 0:D].rearrange("p (c n) -> p c n", c=2)), "n1_ht", t + 1)
                    xt = X[:, bass.ds(t, 1), :].rearrange("p a d -> p (a d)")
                    step(tt(xt, xt, HR[:, i, :], ALU.add))
                for i in range(2):
                    t = 2 * j + i
                    dve.wait_ge(s("n1_ps"), t + 1)
                    mine(dve, cp(Y[:, bass.ds(t, 1), :].rearrange("p a k -> p (a k)"), PS[:, 2 + i, 0:K]),
                         "n1_done", t + 3)
                step.leave(NJ)
            step(tt(Y, Y, bc(CW[:, :].unsqueeze(1), [P, NT, K]), ALU.add))
            tt(Y, Y, bc(DG[:, :].unsqueeze(2), [P, NT, K]), ALU.mult).then_inc(s("y_ready"), 1)
            dve.wait_ge(s("y_ready"), 1)
            step(dve.memset(ACC[0:K, 0, :], 0.0))
            step(dve.memset(HS[:, :, :], 0.0))
            step(dve.memset(EAT[ED:ED + 1, :], 1.0))
            dve.wait_ge(s("cb2_ps"), 1)
            step(tt(CB2, PS[:, 6, 0:2], B2C, ALU.add))
            step(ts(SC2, SC2, 2.0, None, ALU.add))
            dve.sem_inc(s("hs_added"), 1)
            edge_adds(2, K, 1, par=0)
            dve.sem_inc(s("f1_done"), 2)
            with dve.Fori(0, NJ) as j:
                for i in range(2):
                    t = 2 * j + i
                    dve.wait_ge(s("f1_tp"), t + 3)
                    mine(dve, cp(Z[:, bass.ds(t, 1), :].rearrange("p a k -> p (a k)"), PS[:, i, 0:K]), "f1_done", t + 3)
            step(tt(Z, Z, Y, ALU.add))
            step(tt(Z, Z, bc(DG[:, :].unsqueeze(2), [P, NT, K]), ALU.mult))
            step(tt(Z, Z, bc(GB[:, :].unsqueeze(1), [P, NT, K]), ALU.add))
            step(dve.tensor_reduce(ZM, Z, AX, ALU.max))
            tt(Z, Z, bc(ZM.unsqueeze(2), [P, NT, K]), ALU.subtract).then_inc(s("z_shift"), 1)
            dve.wait_ge(s("z_exp"), 1)
            step(dve.tensor_reduce(ZM, Z, AX, ALU.add))
            step(dve.reciprocal(ZM, ZM))
            tt(Z, Z, bc(ZM.unsqueeze(2), [P, NT, K]), ALU.mult).then_inc(s("z_soft"), 1)
            dve.sem_inc(s("g1_done"), 2)
            with dve.Fori(0, NJ) as j:
                for i in range(2):
                    t = 2 * j + i
                    dve.wait_ge(s("g1_mm"), t + 3)
                    xt = X[:, bass.ds(t, 1), :].rearrange("p a d -> p (a d)")
                    mine(dve, tt(xt, xt, PS[:, 4 + i, 0:D], ALU.add), "g1_done", t + 3)
            row_stats()
            norm_scale(2)
            dve.sem_inc(s("n2_done"), 2)
            with dve.Fori(0, NJ) as j:
                step.enter(j, 6)
                for i in range(2):
                    t = 2 * j + i
                    dve.wait_ge(s("n2_tp"), t + 3)
                    a = [ACC[:, c, bass.ds(t * P, P)] for c in range(3)]
                    for c in range(2):
                        step(ts(a[c], PS[:, i, c * P:(c + 1) * P], SC2, CB2[:, c:c + 1], ALU.mult, ALU.add))
                    step(stt(out=a[0], in0=a[2], scalar=B2C[:, 0:1], in1=a[0], op0=ALU.mult, op1=ALU.add))
                    mine(dve, stt(out=a[1], in0=a[2], scalar=B2C[:, 1:2], in1=a[1], op0=ALU.mult, op1=ALU.add),
                         "n2_done", t + 3)
                step.leave(NJ)
            step(dve.memset(ACC[:, 0:2, NPAD:AW], 0.0))
            for i in range(2):
                dve.wait_ge(s(f"rows_out{i}"), rows_out(1, NJ))
            edge_adds(3, P, 2, par=1)
            dve.wait_ge(s("mlp_in"), 16 * 6)
            dve.wait_ge(s("hs_added"), T + 1)
            for i in range(2):
                dve.sem_inc(s(f"m_out{i}"), 1)
                dve.sem_inc(s(f"h2r_free{i}"), 1)

            def scalars(m, i, name, n):
                dve.wait_ge(s(name), n)
                step(dve.reciprocal(m[:, i, 3:4], m[:, i, 2:3]))
                return stt(out=m[:, i, 4:5], in0=m[:, i, 0:1], scalar=-1.0, in1=m[:, i, 3:4],
                           op0=ALU.mult, op1=ALU.mult)

            def dense_in(i, j):
                dve.wait_ge(s(f"m_ee{i}"), j + 1)
                mine(dve, tt(HIN[:, i, :, :], ACC[:, 0:2, bass.ds((2 * j + i) * P, P)],
                             PS[:, 2 * i, 0:D].rearrange("p (c n) -> p c n", c=2), ALU.add), f"m_hin{i}", j + 1)

            def hidden_stats(i, j, l):
                n = 2 * j + l + 1
                dve.wait_ge(s(f"m_ps{i}"), n)
                step(tt(ZR[:, i, :], PS[:, 2 * i:2 * i + 2, :].rearrange("p a n -> p (a n)"), BR[l], ALU.add))
                dve.nop(nofuse=True)
                dve.bn_stats(STAT[:, i, 0:6], ZR[:, i, 0:512])
                step(dve.bn_stats(STAT[:, i, 6:12], ZR[:, i, 512:1024]))
                dve.nop(nofuse=True)
                mine(dve, dve.bn_aggr(SM[:, i, 0:2], STAT[:, i, 0:12]), f"m_var{i}", n)
                mine(dve, scalars(SM, i, f"m_sqrt{i}", n), f"m_scale{i}", n)

            def dense_out(i, j):
                dve.wait_ge(s(f"m_y{i}"), j + 1)
                dve.wait_ge(s(f"h2r_in{i}"), 16 * (j + 1))
                yr = HTR[:, i, :, :].rearrange("p c n -> p (c n)")
                mine(dve, tt(yr, PS[:, 4 + 2 * i, 0:D], B3R, ALU.add), f"m_out{i}", j + 2)
                mine(dve, tt(yr, yr, H2R[:, i, :], ALU.add), f"h2r_free{i}", j + 2)
                dve.nop(nofuse=True)
                step(dve.bn_stats(STAT[:, i, 0:6], yr))
                dve.nop(nofuse=True)
                mine(dve, dve.bn_aggr(YM[:, i, 0:2], STAT[:, i, 0:6]), f"y_var{i}", j + 1)
                step(scalars(YM, i, f"y_sqrt{i}", j + 1))
                step(ts(yr, yr, YM[:, i, 3:4], YM[:, i, 4:5], ALU.mult, ALU.add))
                step(tt(yr, yr, GNR, ALU.mult))
                step(tt(yr, yr, BNR, ALU.add))
                xt = X[:, bass.ds(2 * j + i, 1), :].rearrange("p a d -> p (a d)")
                step(stt(out=xt, in0=yr, scalar=0.0, in1=xt, op0=ALU.max, op1=ALU.add))

            def dense_pair(j, more):
                dense_in(1, j)
                hidden_stats(1, j, 0)
                hidden_stats(0, j, 1)
                if more:
                    dense_in(0, j + 1)
                hidden_stats(1, j, 1)
                if more:
                    hidden_stats(0, j + 1, 0)
                dense_out(0, j)
                dense_out(1, j)

            dense_in(0, 0)
            hidden_stats(0, 0, 0)
            dve.wait_ge(s("mlp_late"), 32)
            with dve.Fori(0, NJ - 1) as j:
                step.enter(j, 4 * 3 + 2 * 7)
                dense_pair(j, True)
                step.leave(NJ - 1)
            dense_pair(NJ - 1, False)
            row_stats()
            norm_scale(3)
            dve.wait_ge(s("w3_ps"), 1)
            for w in range(2):
                cp(WLR[:, w, :, :].rearrange("p c n -> p (c n)"), PS[:, 2 + w, :]).then_inc(s("w3_sb"), 1)
            step(ts(ACC[:, 2, :], ACC[:, 2, :], 1.0, None, ALU.max))
            step(dve.reciprocal(ACC[:, 2, :], ACC[:, 2, :]))
            step(dve.memset(ACC[:, 0:2, :], 0.0))
            dve.sem_inc(s("n3_done"), 2)
            with dve.Fori(0, NJ) as j:
                step.enter(j, 2 * 7)
                for i in range(2):
                    t = 2 * j + i
                    dve.wait_ge(s("n3_in"), t + 1)
                    dve.nop(nofuse=True)
                    step(dve.bn_stats(STAT[:, i, 0:6], HR[:, i, :]))
                    dve.nop(nofuse=True)
                    mine(dve, dve.bn_aggr(SM[:, i, 0:2], STAT[:, i, 0:6]), "n3_var", t + 1)
                for i in range(2):
                    t = 2 * j + i
                    hr = HR[:, i, :]
                    step(scalars(SM, i, "n3_sqrt", t + 1))
                    step(ts(hr, hr, SM[:, i, 3:4], SM[:, i, 4:5], ALU.mult, ALU.add))
                    step(tt(hr, hr, GMR, ALU.mult))
                    step(tt(hr, hr, BTR, ALU.add))
                    mine(dve, ts(hr, hr, 0.0, None, ALU.max), "n3_hr", t + 1)
                for i in range(2):
                    t = 2 * j + i
                    dve.wait_ge(s("n3_tp"), t + 3)
                    mine(dve, cp(HTR[:, i, :, :], PS[:, i, 0:D].rearrange("p (c n) -> p c n", c=2)), "n3_ht", t + 1)
                for i in range(2):
                    t = 2 * j + i
                    dve.wait_ge(s("n3_ps"), t + 1)
                    xt = X[:, bass.ds(t, 1), :].rearrange("p a d -> p (a d)")
                    mine(dve, tt(xt, xt, PS[:, 4 + i, 0:D], ALU.add), "n3_done", t + 3)
                    step(tt(xt, xt, BLR, ALU.add))
                step.leave(NJ)
            for i in range(2):
                dve.wait_ge(s(f"rows_out{i}"), rows_out(2, NJ))
            edge_adds(4, P, 2)
            dve.sem_inc(s("o_free"), 2)
            with dve.Fori(0, NJ) as j:
                for i in range(2):
                    t = 2 * j + i
                    dve.wait_ge(s("o_ps"), t + 1)
                    mine(dve, tt(AR[:, i, 0:D].rearrange("p (c n) -> p c n", c=2), ACC[:, 0:2, bass.ds(t * P, P)],
                                 bc(ACC[:, 2:3, bass.ds(t * P, P)], [P, 2, P]), ALU.mult), "o_ar", t + 1)
                for i in range(2):
                    t = 2 * j + i
                    dve.wait_ge(s("o_ps"), t + 3)
                    dve.wait_ge(s(f"rows_out{i}"), rows_out(3, j))
                    dve_out = tt(HR[:, i, :], X[:, bass.ds(t, 1), :].rearrange("p a d -> p (a d)"), PS[:, i, 0:D], ALU.add)
                    mine(dve, dve_out, "o_ready", t + 1)
                    dve.sem_inc(s("o_free"), 1)


_INS = ['x', 'src', 'dst', 'edge_attr_64', 'edge_type_8', 'L0_gnn_conv_weights', 'L0_gnn_attn_l', 'L0_gnn_attn_r',
        'L0_gnn_h_bias', 'L1_gnn_W', 'L1_gnn_bias', 'L1_gnn_cluster_emb', 'L2_gnn_eps', 'L2_gnn_ee_w1', 'L2_gnn_ee_b1',
        'L2_gnn_ee_w2', 'L2_gnn_ee_b2', 'L2_gnn_w1', 'L2_gnn_b1', 'L2_gnn_g1', 'L2_gnn_be1', 'L2_gnn_w2', 'L2_gnn_b2',
        'L2_gnn_g2', 'L2_gnn_be2', 'L2_gnn_w3', 'L2_gnn_b3', 'L2_gnn_bn_g', 'L2_gnn_bn_b', 'L3_gnn_gamma',
        'L3_gnn_beta', 'L3_gnn_W_l', 'L3_gnn_b_l', 'L3_gnn_W_r']
_OUTS = [((3750, 256), 'float32')]


def kernel(**inputs):
    import numpy as _np
    import concourse.bacc as _bacc
    from concourse import mybir as _mybir
    from concourse.bass_utils import run_bass_kernel_spmd as _run

    nc = _bacc.Bacc("TRN2", target_bir_lowering=False, num_devices=1)
    arrays, args = {}, []
    for name in _INS:
        a = _np.ascontiguousarray(inputs[name]).reshape(_np.shape(inputs[name]) or (1,))
        arrays[f"in_{name}_dram"] = a
        args.append(nc.dram_tensor(f"in_{name}_dram", a.shape, _mybir.dt.from_np(a.dtype), kind="ExternalInput").ap())
    for i, (shape, dtype) in enumerate(_OUTS):
        dt = _mybir.dt.from_np(_np.dtype(dtype))
        args.append(nc.dram_tensor(f"out_{i}_dram", shape, dt, kind="ExternalOutput").ap())
    gnn(nc, *args)
    r = _run(nc, [arrays], core_ids=[0])
    got = tuple(r.results[0][f"out_{i}_dram"] for i in range(len(_OUTS)))
    return got[0]
```

```python
from contextlib import ExitStack

import concourse.bass as bass
from concourse import mybir

P = 128
F32 = mybir.dt.float32
BF16 = mybir.dt.bfloat16
I32 = mybir.dt.int32
ALU = mybir.AluOpType
ACT = mybir.ActivationFunctionType
AX = mybir.AxisListType.X
DVE = mybir.EngineType.DVE
PE = mybir.EngineType.PE
BIG = 1e30
LN_EPS = 1e-5


class Steps:

    def __init__(self, eng, sem):
        self.eng, self.sem, self.n, self.u, self.per = eng, sem, 0, None, 0

    def __call__(self, ins):
        self.n += 1
        ins.then_inc(self.sem, 1)
        self.eng.wait_ge(self.sem, self.n if self.u is None else self.u * self.per + self.n)

    def enter(self, u, per):
        self.u, self.per, self.first = u, per, self.n

    def leave(self, trips):
        assert self.n - self.first == self.per, (self.n - self.first, self.per)
        self.n, self.u = self.first + trips * self.per, None


def gnn(nc, x, src, dst, edge_attr, edge_type, conv_w, attn_l, attn_r, h_bias, gcn_w, gcn_b, cluster,
        eps, ee_w1, ee_b1, ee_w2, ee_b2, w1, b1, g1, be1, w2, b2, g2, be2, w3, b3, bn_g, bn_b,
        gamma, beta, w_l, b_l, w_r, out):
    N, D = x.shape
    E = src.shape[0]
    R, H, _, DH = conv_w.shape
    RH = R * H
    K = gcn_w.shape[1]
    HID = w1.shape[1]
    ED = edge_attr.shape[1]
    KH = HID // P
    NT = -(-N // P)
    NJ = NT // 2
    NTAIL = N - (NT - 1) * P
    NPAD = NT * P
    LB, LT = 4, 125
    T = LB * LT
    IT = T // 10
    IL = IT // 2
    EFULL = E // P
    ETAIL = E - EFULL * P
    AW = NPAD + 40
    assert D == 2 * P and R * D == 2048 and NT % 2 == 0 and AW >= N + P and T * P >= E and EFULL == T - 2
    PAD_DST = 8000.0

    feat_d = nc.dram_tensor("feat_d", (NPAD, R * D), F32).ap()
    el_d = nc.dram_tensor("el_d", (NPAD, RH), F32).ap()
    y_d = nc.dram_tensor("y_d", (NPAD, K), F32).ap()
    h2_d = nc.dram_tensor("h2_d", (NPAD, D), F32).ap()
    h3_d = nc.dram_tensor("h3_d", (NPAD, D), F32).ap()
    rel_d = nc.dram_tensor("rel_d", (T * P,), BF16).ap()

    with ExitStack() as ctx:
        def sb(name, shape, dt=F32):
            return ctx.enter_context(nc.sbuf_tensor(name, shape, dt))

        def sem(name):
            return ctx.enter_context(nc.semaphore(name))

        PS = ctx.enter_context(nc.psum_tensor("PS", [P, 8, 512], F32))

        X = sb("X", [P, NT, D])
        ACC = sb("ACC", [P, 3, AW])
        HS = sb("HS", [P, 2, AW])
        SL = sb("SL", [P, 10, D])
        OHB = sb("OHB", [P, 1280])
        AL = sb("AL", [P, 2048])
        BG = sb("BG", [P, 15872])
        DREL = sb("DREL", [P, T + 5])
        IDXST = sb("IDXST", [P, T], I32)
        IDXS = sb("IDXS", [P, T], I32)
        BASE = sb("BASE", [1, T], I32)
        IX = sb("IX", [P, 2, 10], I32)
        IDENT = sb("IDENT", [P, P])
        IOTA = sb("IOTA", [P, P])
        IOTP = sb("IOTP", [P, 2])
        EPSC = sb("EPSC", [P, 1])
        W1A = sb("W1A", [ED + 1, D])
        EW2 = sb("EW2", [P, 2, D])
        GW = sb("GW", [P, 2, K])
        CE = sb("CE", [K, D])
        CW = sb("CW", [P, K])
        GB = sb("GB", [P, K])
        STAT = sb("STAT", [P, 2, 12])
        XST = sb("XST", [P, NT, 6])
        MV = sb("MV", [P, NT, 2])
        RS = sb("RS", [P, NT])
        NB = sb("NB", [P, NT])
        DG = sb("DG", [P, NT])
        COL = sb("COL", [P, 16])
        COL8 = sb("COL8", [P, 4, KH])
        SM = sb("SM", [P, 2, 8])
        YM = sb("YM", [P, 2, 8])
        REP = sb("REP", [LT, 2, LB, H])
        QEC = sb("QEC", [LT, 2, LB, H])
        QC = sb("QC", [LT, 4, LB])
        QI = sb("QI", [LT, 2, LB], I32)
        ALS = sb("ALS", [P, 2, 20])
        ONES = sb("ONES", [P, P])
        B2C, B1C, CSUM, CB2, SC2 = COL[:, 0:2], COL[:, 2:4], COL[:, 4:6], COL[:, 6:8], COL[:, 8:9]

        ACF = ACC[:, :, :].rearrange("p a n -> p (a n)")
        HSF = HS[:, :, :].rearrange("p a n -> p (a n)")
        SLF = SL[:, :, :].rearrange("p a n -> p (a n)")
        WALL = ACF[:, 0:4096].rearrange("p (c n) -> p c n", c=2)
        STAGE = ACF[:, 4096:8192].rearrange("p (i n) -> p i n", i=2)
        ATT = STAGE
        MF, MB, MFN, MBN = (ACF[0:LT, 8192 + 512 * i:8704 + 512 * i] for i in range(4))
        TF, STF = (ACF[0:LT, 10240 + 512 * i:10752 + 512 * i] for i in range(2))
        RELQ = ACF[0:LT, 11264:11520].bitcast(BF16)
        DI, SI, TI = (SLF[0:LT, 512 * i:512 * i + 512].bitcast(I32) for i in range(3))
        DF, SF = (SLF[0:LT, 1536 + 512 * i:2048 + 512 * i] for i in range(2))
        RELF = SLF[0:LT, 0:512]
        TM = HSF[:, 0:T * R].rearrange("p (t r) -> p t r", r=R)
        OHT = HSF[:, 4000:5280].bitcast(BF16).rearrange("p (h q e) -> p h q e", h=2, q=2)
        ELS = HSF[:, 6560:6560 + NT * RH].rearrange("p (t r) -> p t r", r=RH)
        EF, EB, EX = (HSF[0:LT, 2048 * i:2048 * i + 2048].rearrange("p (h n) -> p h n", h=H) for i in range(3))
        HT = BG[:, 0:2 * NPAD].rearrange("p (c n) -> p c n", c=2)
        SA = BG[:, 2 * NPAD:15872]
        ELA = SA[:, 0:T * H]
        FS, BS = (SA[0:LT, 5120 * i:5120 * i + 2048].rearrange("p (h n) -> p h n", h=H) for i in range(2))
        RB = SA[:, 6144:6784].bitcast(BF16).rearrange("p (h e) -> p h e", h=2)
        QR = SA[0:1, 6784:6784 + T].bitcast(I32)
        TMP = OHB[:, 0:10 * RH].rearrange("p (h n) -> p h n", h=2)
        ER = SA[:, 2048:2048 + NT * RH]
        ERB = ACF[:, 0:(NT + 1) * 3 * RH // 2].bitcast(BF16)
        AW_ = SA[:, 3072:3200].rearrange("p (c n) -> p c n", c=2)
        QE = QEC[:, :, :, :]
        ROWS = [HT[0:H, 0, 512 * i:512 * i + T + 1] for i in range(7)] + \
               [HT[0:H, 1, 512 * i:512 * i + T + 1] for i in range(7)]

        CF, CBK = ROWS[11:13]

        HTR = BG[:, 15360:15872].rearrange("p (i c n) -> p i c n", i=2, c=2)
        HB = AL[:, 0:D]
        CSR = AL[:, D:2 * D].rearrange("p (c n) -> p c n", c=2)
        OH = OHB[:, :].rearrange("p (k n) -> p k n", k=10)
        EA = AL[:, 0:320].rearrange("p (k n) -> p k n", k=5)
        EAT = AL[0:ED + 1, 320:960].rearrange("p (k n) -> p k n", k=5)
        Y = AL[:, 960:960 + NT * K].rearrange("p (t k) -> p t k", k=K)
        HM = [BG[:, 15104:15616], AL[:, 1260:1772], BG[:, 15616:15872]]
        Z = AL[:, 1260:1260 + NT * K].rearrange("p (t k) -> p t k", k=K)
        ZM = AL[:, 1560:1560 + NT]

        W1S = BG[:, 0:2048].rearrange("p (c n) -> p c n", c=2)
        W2S = BG[:, 2048:10240].rearrange("p (c n) -> p c n", c=KH)
        W3S = BG[:, 10240:12288].rearrange("p (c n) -> p c n", c=KH)
        BR = [BG[:, 13312:14336], BG[:, 12288:13312]]
        SLOTS = [SL, BG[:, 10240:12800].rearrange("p (k n) -> p k n", k=10)]
        STRS = [SLF[0:K, 0:20 * P], BG[0:K, 10240:10240 + 10 * P]]
        ELSL = SLF[:, 0:20 * H].rearrange("p (b k h) -> p b k h", b=2, k=10)
        B3R, GNR, BNR = (BG[:, 14336 + D * i:14336 + D * (i + 1)] for i in range(3))
        ZR = AL[:, :].rearrange("p (i n) -> p i n", i=2)
        H1T = SLF[:, 0:2048].rearrange("p (i c n) -> p i c n", i=2, c=KH)
        HIN = OHB[:, 0:512].rearrange("p (i c n) -> p i c n", i=2, c=2)
        H2R = OHB[:, 512:1024].rearrange("p (i n) -> p i n", i=2)
        WRAW = HSF[:, 0:1024].rearrange("p (w o n) -> p w o n", w=2, o=2)
        WLR = HSF[:, 1024:2048].rearrange("p (w c n) -> p w c n", w=2, c=2)
        HALL = BG[:, 0:NT * D].rearrange("p (t n) -> p t n", n=D)
        HR3 = AL[:, 0:2 * D].rearrange("p (i n) -> p i n", i=2)
        GMR, BTR, BLR = (HSF[:, 2048 + D * i:2048 + D * (i + 1)] for i in range(3))

        S = {}

        def s(name):
            if name not in S:
                S[name] = sem(name)
            return S[name]

        EDGE_ORDER = [[("sum", 0)], [("sum", 1), ("hidden", 0)], [("sum", 2)], [("sum", 3), ("hidden", 1)], [],
                      [("sum", 4), ("hidden", 2)], [("turn", 0)], [], [], []]
        gath = [sem(f"gathered{k}") for k in range(4)]

        def gathered(eng, g, w, b, h):
            eng.wait_ge(gath[2 * b + h], 5 * 16 * (IL * g + w + 1))

        def oh_count(g, u, h):
            return (2 * IT + 1) * (g - 1) + 2 * u + h + 1

        def mine(eng, ins, name, value):
            ins.then_inc(s(name), 1)
            eng.wait_ge(s(name), value)

        def pairs(eng, step=None, per=0):
            assert NJ % 3 == 0
            first = step.n if step else 0
            with eng.Fori(0, NJ // 3) as w:
                for b in range(3):
                    if step:
                        step.enter(3 * w + b, per)
                    yield 3 * w + b
                    if step:
                        assert step.n - first == per
                        step.n = first
            if step:
                step.n, step.u = first + NJ * per, None

        def ring_size(l):
            return 20 if l == 2 else 10

        def ring(l, t):
            k = t % ring_size(l)
            return SLOTS[k // 10][:, k % 10, :]

        def bc(ap, shape):
            return ap.broadcast_to(shape)

        def rows(d, t):
            return d[bass.ds(t * P, P), :]

        block = ctx.enter_context(nc.Block())

        @block.sync
        def _(sp):
            def load(dst_ap, src_ap, name):
                sp.dma_start(dst_ap, src_ap).then_inc(s(name), 16)

            def row(ap, n):
                return ap.partition_broadcast(n)

            sp.wait_ge(s("edge_pads"), 3)
            for a, t in ((dst, DI), (src, SI), (edge_type, TI)):
                v = t.rearrange("t (b e) -> t b e", b=LB)
                load(v[:, 0:LB - 1, :], a[0:(LB - 1) * LT * P].rearrange("(b t e) -> t b e", b=LB - 1, e=P), "edges_in")
                n = EFULL - (LB - 1) * LT
                load(v[0:n, LB - 1, :], a[(LB - 1) * LT * P:EFULL * P].rearrange("(t e) -> t e", e=P), "edges_in")
                load(v[n:n + 1, LB - 1, 0:ETAIL], a[EFULL * P:E].rearrange("(o e) -> o e", o=1), "edges_in")
            load(X[:, 0:NT - 1, :], x[0:(NT - 1) * P, :].rearrange("(t p) d -> p t d", p=P), "x_in")
            sp.wait_ge(s("x_tail_zero"), 1)
            load(X[0:NTAIL, NT - 1, :], x[(NT - 1) * P:N, :], "x_in")
            for c in range(2):
                load(WALL[:, c, :].rearrange("p (r d) -> p r d", r=RH),
                     conv_w.rearrange("r h i d -> i (r h) d")[c * P:(c + 1) * P], "conv_in")
            load(ATT[:, 0, :], row(attn_l.rearrange("r h d -> (r h d)"), P), "attn_in")
            load(ATT[:, 1, :], row(attn_r.rearrange("r h d -> (r h d)"), P), "attn_in")
            with nc.allow_non_contiguous_dma(reason="small weight columns"):
                load(W1A[0:ED, :], ee_w1, "small_in")
                load(W1A[ED:ED + 1, :], ee_b1.rearrange("(o n) -> o n", o=1), "small_in")
                load(EW2[:, :, :], ee_w2.rearrange("(c p) n -> p c n", p=P), "small_in")
                load(GW[:, :, :], gcn_w.rearrange("(c p) n -> p c n", p=P), "small_in")
                load(CE[:, :], cluster, "small_in")
                load(GB[:, :], row(gcn_b, P), "small_in")
                load(B2C, ee_b2.rearrange("(c p) -> p c", p=P), "small_in")
                load(B1C, ee_b1.rearrange("(c p) -> p c", p=P), "small_in")
                load(SC2, eps.partition_broadcast(P), "small_in")
                for c in range(2):
                    load(ZR[:, 0, c * K:(c + 1) * K], cluster.rearrange("k (c p) -> c p k", p=P)[c], "small_in")
                for i, a in enumerate((g1, be1, g2, be2)):
                    load(COL8[:, i, :], a.rearrange("(c p) -> p c", p=P), "small_in")
            sp.wait_ge(s("relq_ready"), 1)
            load(rel_d.rearrange("(b t e) -> t b e", b=LB, e=P), RELQ.rearrange("t (b e) -> t b e", b=LB), "rel_out")
            sp.wait_ge(s("elr_done"), 2 * 4)
            load(el_d.rearrange("(t p) r -> p t r", p=P), ELS, "el_out")
            for i in range(2):
                sp.sem_inc(s(f"stage_out{i}"), 16)
            for j in pairs(sp):
                for i in range(2):
                    sp.wait_ge(s("tab_free"), (2 * j + i + 1) * 4 + 4)
                    load(rows(feat_d, 2 * j + i), STAGE[:, i, :], f"stage_out{i}")
            sp.wait_ge(s("rel_out"), 16)
            with sp.Fori(0, IT) as u:
                for h in range(2):
                    sp.wait_ge(s("oht_ready"), 2 * u + h + 1)
                    load(RB[:, h, :], rel_d[bass.ds((10 * u + 5 * h) * P, 5 * P)].partition_broadcast(P), f"rb_in{h}")
            sp.wait_ge(s("msg_ready"), T)
            load(HB, row(h_bias, P), "hb_in")
            sp.wait_ge(s("y_ready"), 1)
            load(y_d.rearrange("(t p) k -> p t k", p=P), Y, "y_out")
            load(W1S, w1.rearrange("(c p) n -> p c n", p=P), "mlp_in")
            load(W2S, w2.rearrange("(c p) n -> p c n", p=P), "mlp_in")
            for t, a in ((BR[0], b1), (B3R, b3), (GNR, bn_g), (BNR, bn_b)):
                load(t, row(a, P), "mlp_in")

            ea_even = edge_attr[0:EFULL * P, :].rearrange("(v q p) f -> p v q f", q=2, p=P)

            def edge_rows(par, u, last):
                sp.wait_ge(s("ea_used"), IT * par + u + 1)
                load(EA[:, 0:4, :], ea_even[:, bass.ds(5 * u, 4), par, :], "ea_in")
                if not last:
                    load(EA[:, 4:5, :], ea_even[:, bass.ds(5 * u + 4, 1), par, :], "ea_in")
                elif par == 0:
                    load(EA[0:ETAIL, 4, :], edge_attr[EFULL * P:E, :], "ea_in")
                else:
                    load(EA[:, 4, :], ea_even[:, 5 * u + 3, par, :], "ea_in")

            sp.wait_ge(s("f0_done"), NT)
            with sp.Fori(0, IT - 1) as u:
                edge_rows(0, u, False)
            edge_rows(0, IT - 1, True)
            for q in range(NT // 5):
                sp.wait_ge(s("n2_hr"), 5 * q + 5)
                k = 5 * q % 10
                load(h2_d[5 * q * P:5 * (q + 1) * P, :].rearrange("(t p) d -> p t d", p=P),
                     SLOTS[q // 2 % 2][:, k:k + 5, :], f"h2_out{min(q, 2)}")
            with sp.Fori(0, IT - 1) as u:
                edge_rows(1, u, False)
            edge_rows(1, IT - 1, True)
            sp.wait_ge(s("agg_ps"), 3 * T + 20)
            load(BR[1], row(b2, P), "mlp_late")
            load(W3S, w3.rearrange("(c p) n -> p c n", p=P), "mlp_late")
            for j in pairs(sp):
                for i in range(2):
                    sp.wait_ge(s(f"h2r_free{i}"), j + 1)
                    load(H2R[:, i, :], rows(h2_d, 2 * j + i), f"h2r_in{i}")
            for i in range(2):
                sp.wait_ge(s(f"m_y{i}"), NJ)
            for w, a in ((0, w_l), (1, w_r)):
                load(WRAW[:, w, :, :], a.rearrange("(o p) n -> p o n", p=P), "l3_in")
            for t, a in ((GMR, gamma), (BTR, beta), (BLR, b_l)):
                load(t, row(a, P), "l3_in")
            for q in range(NT // 5):
                sp.wait_ge(s("h3_rows"), q + 1)
                load(h3_d[5 * q * P:5 * (q + 1) * P, :].rearrange("(t p) d -> p t d", p=P), HALL[:, 5 * q:5 * q + 5, :],
                     "h3_out")
            for q in range(NT // 5):
                sp.wait_ge(s("o_ready"), 5 * q + 5)
                n = 5 if q < NT // 5 - 1 else 4
                load(out[5 * q * P:(5 * q + n) * P, :].rearrange("(t p) d -> p t d", p=P), X[:, 5 * q:5 * q + n, :], "out")
            load(out[(NT - 1) * P:N, :], X[0:NTAIL, NT - 1, :], "out")
            sp.wait_ge(s("out"), 16 * (NT // 5 + 1))
            for i in range(2):
                sp.wait_ge(s(f"stage_out{i}"), 16 * (NJ + 1))
            sp.wait_ge(s("el_out"), 16)
            sp.wait_ge(s("y_out"), 16)

        @block.gpsimd
        def _(pool):
            step = Steps(pool, s("pool_steps"))
            step(pool.memset(IDENT[:, :], 0.0))
            pool.affine_select(out=IDENT[:, :], in_=IDENT[:, :], compare_op=ALU.not_equal, fill=1.0, base=0,
                               pattern=[[-1, P]], channel_multiplier=1).then_inc(s("const_ready"), 1)
            pool.iota(IOTA[:, :], pattern=[[1, P]], base=0, channel_multiplier=0,
                      allow_small_or_imprecise_dtypes=True).then_inc(s("const_ready"), 1)
            pool.iota(IOTP[:, :], pattern=[[P, 2]], base=0, channel_multiplier=1,
                      allow_small_or_imprecise_dtypes=True).then_inc(s("const_ready"), 1)

            def gather(g, table, width, idx):
                with pool.Fori(0, IL) as w:
                    step.enter(w, 2)
                    for b in range(2):
                        u = 2 * w + b
                        if g == 0:
                            pool.wait_ge(s("el_slots"), u + 1)
                        else:
                            pool.wait_ge(s("agg_ps"), T * (g - 1) + 10 * u + 10)
                        step(pool.tensor_copy(IX[:, b, :], idx[:, bass.ds(10 * u, 10)]))
                        pool.nop(nofuse=True)
                        for k in range(10):
                            pool.indirect_dma_start(
                                ELSL[:, b, k, :] if g == 0 else SLOTS[b][:, k, 0:width], None, table,
                                bass.IndirectOffsetOnAxis(ap=IX[:, b, k:k + 1], axis=0),
                            ).then_inc(gath[2 * b + k // 5], 16)
                    step.leave(IL)

            pool.wait_ge(s("idx_ready"), 2)
            pool.wait_ge(s("el_out"), 16)
            gather(0, el_d.rearrange("n (r h) -> (n r) h", r=R), H, IDXST)
            pool.wait_ge(s("el_slots"), IT + 2)
            pool.wait_ge(s("e_all"), 1)
            pool.memset(ACF[:, 0:8192], 0.0).then_inc(s("acc_zero"), 1)
            for i in range(2):
                pool.wait_ge(s(f"stage_out{i}"), 16 * (NJ + 1))
            gather(1, feat_d.rearrange("n (r d) -> (n r) d", r=R), D, IDXST)
            pool.wait_ge(s("y_out"), 16)
            gather(2, y_d, K, IDXS)
            pool.wait_ge(s("h2_out0"), 16)
            pool.wait_ge(s("h2_out1"), 16)
            pool.wait_ge(s("h2_out2"), 16 * (NT // 5 - 2))
            pool.wait_ge(s("n2_tp"), NT)
            gather(3, h2_d, D, IDXS)
            for i in range(2):
                pool.wait_ge(s(f"m_y{i}"), NJ)
                pool.wait_ge(s(f"m_hin{i}"), NJ)
            pool.memset(ACC[:, 0:2, :], 0.0).then_inc(s("acc_zero"), 1)
            pool.wait_ge(s("h3_out"), 16 * (NT // 5))
            gather(4, h3_d, D, IDXS)

        @block.scalar
        def _(act):
            step = Steps(act, s("act_steps"))

            def rstd(l):
                act.wait_ge(s("norm_stats"), l + 1)
                act.activation(RS[:, :], MV[:, :, 1], ACT.Sqrt, bias=EPSC[:, 0:1]).then_inc(s("norm_sqrt"), 1)
                act.wait_ge(s("norm_scale"), l + 1)

            def norm_ring(l):
                rstd(l)
                n = ring_size(l)
                for t in range(NT):
                    if t >= n:
                        act.wait_ge(s(("n0_tp", "n1_used", "n2_tp")[l]), t - n + 1)
                    if l == 2 and t >= n and t % 5 == 0:
                        act.wait_ge(s(f"h2_out{(t - n) // 5}"), 16)
                    act.activation(ring(l, t), X[:, t, :], ACT.Relu, scale=RS[:, t:t + 1],
                                   bias=NB[:, t:t + 1]).then_inc(s(f"n{l}_hr"), 1)

            norm_ring(0)
            act.wait_ge(s("small_in"), 16 * 15)
            act.activation(B1C, B1C, ACT.Relu).then_inc(s("b1_relu"), 1)
            act.sem_inc(s("el_slots"), 2)
            with act.Fori(0, IL) as w:
                for b in range(2):
                    for h in range(2):
                        gathered(act, 0, w, b, h)
                    act.activation(ELA[:, bass.ds(10 * (2 * w + b) * H, 10 * H)].rearrange("p (k h) -> p k h", h=H),
                                   ELSL[:, b, :, :], ACT.Copy).then_inc(s("el_slots"), 1)
            act.wait_ge(s("e_ps"), 1)
            step(act.activation(EF, PS[0:LT, 0:H, 0:LB * P], ACT.Copy))
            act.activation(EB, PS[0:LT, 0:H, 0:LB * P], ACT.Copy).then_inc(s("e_sb"), 1)
            act.wait_ge(s("e_shift"), 1)
            act.activation(EX, EX, ACT.Exp).then_inc(s("e_exp"), 1)
            act.wait_ge(s("e_exp"), 1)
            act.activation(EF, EX, ACT.Copy).then_inc(s("x_sb"), 1)
            act.activation(EB, EX, ACT.Copy).then_inc(s("x_sb"), 1)
            act.wait_ge(s("alpha_ps"), 1)
            step(act.activation(AL[:, 0:T * H].rearrange("p (b t h) -> p b h t", b=LB, h=H),
                                PS[:, 0:LB, 0:LT * H].rearrange("p b (h t) -> p b h t", h=H), ACT.Copy))
            with act.Fori(0, IL) as w:
                step.enter(w, 4)
                for b in range(2):
                    for h in range(2):
                        t = 10 * (2 * w + b) + 5 * h
                        step(act.activation(ALS[:, h, :], AL[:, bass.ds(t * H, 5 * H)], ACT.Copy))
                        gathered(act, 1, w, b, h)
                        for k in range(5):
                            for q in range(H):
                                v = SLOTS[b][:, 5 * h + k, q * DH:(q + 1) * DH]
                                a = k * H + q
                                last = act.activation(v, v, ACT.Copy, scale=ALS[:, h, a:a + 1])
                            last.then_inc(s("msg_ready"), 1)
                step.leave(IL)

            act.wait_ge(s("f0_done"), NT)
            act.activation(DG[:, :], DG[:, :], ACT.Sqrt, bias=1.0).then_inc(s("dg_sqrt"), 1)
            norm_ring(1)

            def edge_hidden(par):
                with act.Fori(0, IT) as u:
                    n = IT * par + u
                    act.wait_ge(s("ea_used"), n + 2)
                    act.activation(EAT[0:ED, 0:4, :], PS[0:ED, 2, :].rearrange("p (k n) -> p k n", k=4), ACT.Copy)
                    act.activation(EAT[0:ED, 4, :], PS[0:ED, 3, 0:P], ACT.Copy).then_inc(s("ea_t"), 1)
                    for q in range(3):
                        act.wait_ge(s("hid_ps"), 3 * n + q + 1)
                        act.activation(HM[q], PS[:, 4 + q, 0:512 if q < 2 else D], ACT.Relu).then_inc(s("hid_ready"), 1)

            edge_hidden(0)
            act.wait_ge(s("z_shift"), 1)
            act.activation(Z, Z, ACT.Exp).then_inc(s("z_exp"), 1)
            act.wait_ge(s("z_soft"), 1)
            for q in range(-(-NT // 4)):
                n = min(4, NT - 4 * q)
                act.wait_ge(s("g1_tp"), q + 1)
                act.activation(STRS[q // 5][:, (q % 5) * 4 * P:((q % 5) * 4 + n) * P], PS[0:K, q % 4, 0:n * P],
                               ACT.Copy).then_inc(s("g1_st"), 1)
            norm_ring(2)
            edge_hidden(1)

            def hidden_norm(i, j, l):
                n = 2 * j + l + 1
                act.wait_ge(s(f"m_var{i}"), n)
                act.activation(SM[:, i, 2:3], SM[:, i, 1:2], ACT.Sqrt, bias=EPSC[:, 0:1]).then_inc(s(f"m_sqrt{i}"), 1)
                act.wait_ge(s(f"m_scale{i}"), n)
                act.activation(ZR[:, i, :], ZR[:, i, :], ACT.Identity, scale=SM[:, i, 3:4],
                               bias=SM[:, i, 4:5]).then_inc(s(f"m_z{i}"), 1)

            def hidden_relu(i, j, l):
                act.wait_ge(s(f"m_t{i}"), 2 * j + l + 1)
                for c in range(KH):
                    last = act.activation(H1T[:, i, c, :], PS[:, 4 + 2 * i + c // 4, (c % 4) * P:(c % 4 + 1) * P],
                                          ACT.Relu, scale=COL8[:, 2 * l, c:c + 1], bias=COL8[:, 2 * l + 1, c:c + 1])
                last.then_inc(s(f"m_h{i}"), 1)

            def dense_pair(j, more):
                hidden_relu(0, j, 0)
                hidden_norm(1, j, 0)
                hidden_relu(1, j, 0)
                hidden_norm(0, j, 1)
                hidden_relu(0, j, 1)
                hidden_norm(1, j, 1)
                hidden_relu(1, j, 1)
                if more:
                    hidden_norm(0, j + 1, 0)
                for i in range(2):
                    act.wait_ge(s(f"y_var{i}"), j + 1)
                    act.activation(YM[:, i, 2:3], YM[:, i, 1:2], ACT.Sqrt, bias=EPSC[:, 0:1]).then_inc(s(f"y_sqrt{i}"), 1)

            hidden_norm(0, 0, 0)
            with act.Fori(0, NJ - 1) as j:
                dense_pair(j, True)
            dense_pair(NJ - 1, False)
            rstd(3)
            for i in range(2):
                act.wait_ge(s(f"m_y{i}"), NJ)
            for t in range(NT):
                act.activation(HALL[:, t, :], X[:, t, :], ACT.Relu, scale=RS[:, t:t + 1],
                               bias=NB[:, t:t + 1]).then_inc(s("n3_in"), 1)
            rstd(4)
            for t in range(NT):
                act.activation(HALL[:, t, :], HALL[:, t, :], ACT.Identity, scale=RS[:, t:t + 1],
                               bias=NB[:, t:t + 1]).then_inc(s("n3_z"), 1)
            act.wait_ge(s("h3_rows"), NT // 5)
            with act.Fori(0, NJ) as j:
                for i in range(2):
                    t = 2 * j + i
                    act.wait_ge(s("n3_tp"), t + 1)
                    act.activation(HR3[:, i, :], HALL[:, bass.ds(t, 1), :], ACT.Copy).then_inc(s("n3_hr"), 1)

        @block.tensor
        def _(pe):
            def turn(out_ap, in_ap, k):
                return pe.transpose(out_ap, in_ap, IDENT[0:k, 0:k])

            pe.sem_inc(s("agg_ps"), 20)
            pe.wait_ge(s("const_ready"), 3)
            pe.wait_ge(s("prep_ready"), 1)
            for bank, a in enumerate((RELF, SF, STF, TF)):
                for b in range(LB):
                    last = turn(PS[:, bank, b * LT:(b + 1) * LT], a[:, b * P:(b + 1) * P], LT)
            for bank, q in ((4, 0), (5, 2)):
                for b in range(LB):
                    last = turn(PS[0:1, bank, b * LT:(b + 1) * LT], QC[:, q, b:b + 1], LT)
            last.then_inc(s("prep_t"), 1)
            pe.wait_ge(s("prep_used"), 1)

            def turn_ring(l, t):
                pe.wait_ge(s(f"n{l}_hr"), t + 1)
                if t >= 4:
                    pe.wait_ge(s(f"n{l}_ht"), t - 3)
                turn(PS[:, t % 4, 0:P], ring(l, t)[:, 0:P], P)
                turn(PS[:, t % 4, P:D], ring(l, t)[:, P:D], P).then_inc(s(f"n{l}_tp"), 1)

            pe.wait_ge(s("aw_ready"), 1)
            for t in range(NT + 2):
                if t < NT:
                    turn_ring(0, t)
                if t >= 2:
                    v = t - 2
                    pe.wait_ge(s("n0_ht"), v + 1)
                    for c in range(2):
                        last = pe.matmul(PS[:, 4 + v // 8, (v % 8) * 2 * RH:(v % 8 + 1) * 2 * RH],
                                         HT[:, c, v * P:(v + 1) * P], AW_[:, c, :], start=(c == 0), stop=(c == 1))
                    if v % 8 == 7 or v == NT - 1:
                        last.then_inc(s("elr_ps"), 1)
            pe.wait_ge(s("elr_done"), 2 * 4)
            for c in range(2):
                last = pe.matmul(PS[:, 6, 0:K], CSR[:, c, :], GW[:, c, :], start=(c == 0), stop=(c == 1))
            last.then_inc(s("cw_ps"), 1)
            pe.sem_inc(s("tab_ps"), 8)
            for j in pairs(pe):
                for i in range(2):
                    t = 2 * j + i
                    pe.wait_ge(s("tab_in"), t + 1)
                    for q in range(4):
                        pe.wait_ge(s("tab_free"), 4 * t + q + 1)
                        for c in range(2):
                            last = pe.matmul(PS[:, 4 + q, :], HTR[:, i, c, :], WALL[:, c, q * 512:(q + 1) * 512],
                                             start=(c == 0), stop=(c == 1))
                        last.then_inc(s("tab_ps"), 1)
            pe.wait_ge(s("er_parts"), 1)
            with pe.Fori(0, IT) as u:
                _, qs = nc.values_load_multi_w_load_instructions(
                    QR[:, bass.ds(10 * u, 10)], engines=[PE], min_val=0, max_val=(NT - 1) * 3 * RH,
                    skip_runtime_bounds_check_because="clamped to the last node tile when it was computed")
                for h in range(2):
                    pe.wait_ge(s("oht_ready"), 2 * u + h + 3)
                    pe.wait_ge(s("er_done"), 2 * u + h + 1)
                    for k in range(5):
                        o = PS[:, h, k * 3 * RH:(k + 1) * 3 * RH]
                        q = qs[5 * h + k]
                        pe.matmul(o, OHT[:, h, 0, k * P:(k + 1) * P], ERB[:, bass.ds(q, 3 * RH)], start=True, stop=False)
                        last = pe.matmul(o, OHT[:, h, 1, k * P:(k + 1) * P], ERB[:, bass.ds(q + 3 * RH, 3 * RH)],
                                         start=False, stop=True)
                    last.then_inc(s("er_ps"), 1)
            pe.wait_ge(s("e_all"), 1)
            ev = AL[:, 0:T * H].rearrange("p (t h) -> p t h", h=H)
            for h in range(H):
                for b in range(LB):
                    last = turn(PS[0:LT, h, b * P:(b + 1) * P], ev[:, b * LT:(b + 1) * LT, h], P)
            last.then_inc(s("e_ps"), 1)
            for b in range(LB):
                turn(PS[0:H, 4, b * LT:(b + 1) * LT], REP[:, 0, b, :], LT)
                last = turn(PS[0:H, 5, b * LT:(b + 1) * LT], REP[:, 1, b, :], LT)
            last.then_inc(s("rep_ps"), 1)
            for r in range(2):
                pe.wait_ge(s("ends"), r + 1)
                for b in range(LB):
                    turn(PS[0:H, 6, b * LT:(b + 1) * LT], QE[:, 0, b, :], LT)
                    last = turn(PS[0:H, 7, b * LT:(b + 1) * LT], QE[:, 1, b, :], LT)
                last.then_inc(s("ends_ps"), 1)
                pe.wait_ge(s("carry"), r + 1)
                for b in range(LB):
                    turn(PS[0:LT, 4, b * H:(b + 1) * H], CF[:, b * LT:(b + 1) * LT], H)
                    last = turn(PS[0:LT, 5, b * H:(b + 1) * H], CBK[:, b * LT:(b + 1) * LT], H)
                last.then_inc(s("carry_ps"), 1)
            pe.wait_ge(s("alpha_t"), 1)
            for b in range(LB):
                for h in range(H):
                    last = turn(PS[:, b, h * LT:(h + 1) * LT], EX[:, h, b * P:(b + 1) * P], LT)
            last.then_inc(s("alpha_ps"), 1)

            def edge_sums(g, planes, par=None, beside=None):
                def agg(w, b, k):
                    u = 2 * w + b
                    n = T * (g - 1) + 10 * u + k
                    rows_in = SLOTS[b]
                    if g == 1:
                        pe.wait_ge(s("msg_ready"), 10 * u + k + 1)
                    elif k % 5 == 0:
                        gathered(pe, g, w, b, k // 5)
                    if k % 5 == 0:
                        pe.wait_ge(s("oh_ready"), oh_count(g, u, k // 5))
                    pe.wait_ge(s("added"), n + 9)
                    if g == 2:
                        pe.matmul(PS[0:K, k % 2, 0:P], rows_in[:, k, 0:K], OH[:, k, :], start=True, stop=True)\
                            .then_inc(s("agg_ps"), 1)
                        return
                    for c in range(planes):
                        w = ONES[:, :] if c == 2 else rows_in[:, k, c * P:(c + 1) * P]
                        last = pe.matmul(PS[:, k % 2, c * P:(c + 1) * P], w, OH[:, k, :], start=True, stop=True)
                    last.then_inc(s("agg_ps"), 1)

                def net_turn(v, sums):
                    pe.wait_ge(s("ea_in"), 32 * (v + 1))
                    pe.wait_ge(s("hs_added"), sums + 1)
                    pe.nop(nofuse=True)
                    for kk in range(5):
                        last = turn(PS[0:ED, 2 + kk // 4, (kk % 4) * P:(kk % 4 + 1) * P], EA[:, kk, :], P)
                    last.then_inc(s("ea_used"), 1)

                def hidden(v, q):
                    pe.wait_ge(s("ea_t"), v + 1)
                    for kk in range(2 * q, min(2 * q + 2, 5)):
                        last = pe.matmul(PS[:, 4 + q, (kk % 2) * D:(kk % 2 + 1) * D], EAT[:, kk, :], W1A[:, :],
                                         start=True, stop=True)
                    last.then_inc(s("hid_ps"), 1)

                def hidden_sum(u, v, kk, more):
                    m = 5 * v + kk
                    pe.wait_ge(s("hid_ready"), 3 * v + kk // 2 + 1)
                    pe.wait_ge(s("oh_ready"), oh_count(g, u, (2 * kk + par) // 5))
                    if kk == 1 and more:
                        pe.wait_ge(s("ea_t"), v + 2)
                    pe.wait_ge(s("hs_added"), m + (1 if kk == 0 else 0))
                    for c in range(2):
                        o = (kk % 2) * D + c * P
                        last = pe.matmul(PS[:, 7 - 4 * (kk % 2), c * P:(c + 1) * P], HM[kk // 2][:, o:o + P],
                                         OH[:, 2 * kk + par, :], start=True, stop=True)
                    last.then_inc(s("hs_ps"), 1)

                def step_pair(w, end, beside=()):
                    for b in range(2):
                        u = 2 * w + b
                        for k in range(10):
                            agg(w, b, k)
                            if (b, k) in beside:
                                beside[b, k](w)
                            for what, q in EDGE_ORDER[k] if par is not None else []:
                                v = IT * par + u
                                if what == "sum":
                                    hidden_sum(u, v, q, not (end and b == 1))
                                elif what == "hidden" and not (end and b == 1):
                                    hidden(v + 1, q)
                                elif what == "turn" and not end:
                                    net_turn(v + 2, 5 * v + 4)

                if par is not None:
                    net_turn(IT * par, 5 * IT * par)
                    for q in range(3):
                        hidden(IT * par, q)
                    net_turn(IT * par + 1, 5 * IT * par)
                first = NJ if beside else 0
                if beside:
                    with pe.Fori(0, NJ) as w:
                        step_pair(w, False, beside)
                with pe.Fori(first, IL - 1) as w:
                    step_pair(w, False)
                step_pair(IL - 1, True)

            edge_sums(1, 3)
            pe.wait_ge(s("added"), T + 10)
            for t in range(NT):
                if t >= 2:
                    pe.wait_ge(s("f0_done"), t - 1)
                for c in range(3):
                    last = turn(PS[:, t % 2, c * P:(c + 1) * P], ACC[:, c, t * P:(t + 1) * P], P)
                last.then_inc(s("f0_tp"), 1)
            for t in range(NT + 2):
                if t < NT:
                    turn_ring(1, t)
                if t >= 2:
                    v = t - 2
                    pe.wait_ge(s("n1_ht"), v + 1)
                    for c in range(2):
                        last = pe.matmul(PS[:, 4, v * K:(v + 1) * K], HT[:, c, v * P:(v + 1) * P], GW[:, c, :],
                                         start=(c == 0), stop=(c == 1))
            last.then_inc(s("n1_ps"), 1)
            pe.sem_inc(s("ea_used"), 1)
            pe.wait_ge(s("b1_relu"), 1)
            for f in range(2):
                for c in range(2):
                    last = pe.matmul(PS[:, 6, f:f + 1], EW2[:, c, f * P:(f + 1) * P], B1C[:, c:c + 1],
                                     start=(c == 0), stop=(c == 1))
            last.then_inc(s("cb2_ps"), 1)
            edge_sums(2, 1, par=0)
            pe.wait_ge(s("added"), 2 * T + 10)
            for t in range(NT):
                last = turn(PS[:, 0, t * K:(t + 1) * K], ACC[0:K, 0, t * P:(t + 1) * P], K)
            last.then_inc(s("f1_tp"), 1)
            NQ = -(-NT // 4)
            pe.wait_ge(s("z_soft"), 1)
            for q in range(NQ + 1):
                if q < NQ:
                    if q >= 4:
                        pe.wait_ge(s("g1_st"), q - 3)
                    for t in range(4 * q, min(4 * q + 4, NT)):
                        last = turn(PS[0:K, q % 4, (t % 4) * P:(t % 4 + 1) * P], Z[:, t, :], P)
                    last.then_inc(s("g1_tp"), 1)
                if q >= 1:
                    pe.wait_ge(s("g1_st"), q)
                    for t in range(4 * (q - 1), min(4 * q, NT)):
                        if t >= 4:
                            pe.wait_ge(s("g1_done"), t - 3)
                        pe.matmul(PS[:, 4 + t % 4, 0:D], STRS[t // 20][:, (t % 20) * P:(t % 20 + 1) * P], CE[:, :],
                                  start=True, stop=True).then_inc(s("g1_mm"), 1)
            for t in range(NT):
                turn_ring(2, t)
            pe.wait_ge(s("n2_ht"), NT)
            edge_sums(3, 2, par=1)
            pe.wait_ge(s("mlp_in"), 16 * 6)
            pe.wait_ge(s("added"), 3 * T + 10)
            pe.wait_ge(s("hs_added"), T + 1)

            def edge_part(i, j):
                for f in range(2):
                    for c in range(2):
                        last = pe.matmul(PS[:, 2 * i, f * P:(f + 1) * P], EW2[:, c, f * P:(f + 1) * P],
                                         HS[:, c, bass.ds((2 * j + i) * P, P)], start=(c == 0), stop=(c == 1))
                last.then_inc(s(f"m_ee{i}"), 1)

            def dense(i, lhs, w, banks, width, to):
                kc = w.shape[1]
                for q in banks:
                    for c in range(kc):
                        last = pe.matmul(PS[:, to + q, 0:width], lhs[:, i, c, :], w[:, c, q * width:(q + 1) * width],
                                         start=(c == 0), stop=(c == kc - 1))
                return last

            def dense1(i, j):
                pe.wait_ge(s(f"m_hin{i}"), j + 1)
                dense(i, HIN, W1S, range(2), 512, 2 * i).then_inc(s(f"m_ps{i}"), 1)

            def dense2(i, j, q):
                pe.wait_ge(s(f"m_h{i}"), 2 * j + 1)
                last = dense(i, H1T, W2S, [q], 512, 2 * i)
                if q == 1:
                    last.then_inc(s(f"m_ps{i}"), 1)

            def dense3(i, j):
                pe.wait_ge(s(f"m_h{i}"), 2 * j + 2)
                dense(i, H1T, W3S, [0], D, 4 + 2 * i).then_inc(s(f"m_y{i}"), 1)

            def turn_hidden(i, j, l):
                pe.wait_ge(s(f"m_z{i}"), 2 * j + l + 1)
                if l == 0:
                    pe.wait_ge(s(f"m_out{i}"), j + 1)
                for c in range(KH):
                    last = turn(PS[:, 4 + 2 * i + c // 4, (c % 4) * P:(c % 4 + 1) * P], ZR[:, i, c * P:(c + 1) * P], P)
                last.then_inc(s(f"m_t{i}"), 1)

            def dense_pair(j, more):
                turn_hidden(0, j, 0)
                dense1(1, j)
                dense2(0, j, 0)
                turn_hidden(1, j, 0)
                dense2(0, j, 1)
                dense2(1, j, 0)
                turn_hidden(0, j, 1)
                if more:
                    pe.wait_ge(s("m_var0"), 2 * j + 2)
                    edge_part(0, j + 1)
                dense2(1, j, 1)
                if more:
                    dense1(0, j + 1)
                turn_hidden(1, j, 1)
                if more:
                    edge_part(1, j + 1)
                dense3(0, j)
                dense3(1, j)

            edge_part(0, 0)
            edge_part(1, 0)
            dense1(0, 0)
            pe.wait_ge(s("mlp_late"), 32)
            with pe.Fori(0, NJ - 1) as j:
                dense_pair(j, True)
            dense_pair(NJ - 1, False)
            pe.wait_ge(s("l3_in"), 16 * 5)
            for w in range(2):
                for c in range(2):
                    for o in range(2):
                        last = turn(PS[:, 2 + w, (2 * c + o) * P:(2 * c + o + 1) * P], WRAW[:, w, o, c * P:(c + 1) * P], P)
            last.then_inc(s("w3_ps"), 1)
            pe.sem_inc(s("n3_tp"), 2)
            pe.wait_ge(s("w3_sb"), 2)

            def self_turn(j):
                for i in range(2):
                    pe.wait_ge(s("n3_hr"), 2 * j + i + 1)
                    pe.nop(nofuse=True)
                    turn(PS[:, 2 + i, 0:P], HR3[:, i, 0:P], P)
                    turn(PS[:, 2 + i, P:D], HR3[:, i, P:D], P).then_inc(s("n3_tp"), 1)

            def self_product(j):
                for i in range(2):
                    pe.wait_ge(s("n3_ht"), 2 * j + i + 1)
                    pe.wait_ge(s("n3_done"), 2 * j + i + 1)
                    for c in range(2):
                        last = pe.matmul(PS[:, 4 + i, 0:D], HTR[:, i, c, :], WLR[:, 1, c, :],
                                         start=(c == 0), stop=(c == 1))
                    last.then_inc(s("n3_ps"), 1)

            edge_sums(4, 2, beside={(0, 3): self_turn, (0, 8): self_product})
            for t in range(NT):
                pe.wait_ge(s("o_mean"), t // 5 + 1)
                if t >= 8:
                    pe.wait_ge(s("o_ready"), t - 7)
                for c in range(2):
                    last = pe.matmul(PS[:, t % 8, 0:D], ACC[:, c, t * P:(t + 1) * P], WLR[:, 0, c, :],
                                     start=(c == 0), stop=(c == 1))
                last.then_inc(s("o_ps"), 1)

        @block.vector
        def _(dve):
            step = Steps(dve, s("dve_steps"))
            tt, ts, stt, cp = dve.tensor_tensor, dve.tensor_scalar, dve.scalar_tensor_tensor, dve.tensor_copy

            for t, v in ((DI, int(PAD_DST)), (SI, 0), (TI, 0)):
                dve.memset(t, v).then_inc(s("edge_pads"), 1)
            dve.memset(X[:, NT - 1, :], 0.0).then_inc(s("x_tail_zero"), 1)
            step(dve.memset(EPSC[:, :], LN_EPS))
            step(dve.memset(ONES[:, :], 1.0))
            dve.wait_ge(s("edges_in"), 16 * 9)
            v3 = lambda a: a.rearrange("t (b e) -> t b e", b=LB)
            step(cp(DF, DI))
            step(cp(SF, SI))
            step(cp(TF, TI))
            step(stt(out=STF, in0=SF, scalar=float(R), in1=TF, op0=ALU.mult, op1=ALU.add))
            step(ts(QC[:, 0, :], v3(DF)[:, :, 0], float(N), None, ALU.min))
            step(cp(QI[:, 0, :], QC[:, 0, :]))
            step(ts(QI[:, 1, :], QI[:, 0, :], 7, 7, ALU.logical_shift_right, ALU.logical_shift_left))
            step(cp(QC[:, 1, :], QI[:, 1, :]))
            step(ts(QC[:, 2, :], QC[:, 1, :], 3.0 * RH / P, None, ALU.mult))
            step(tt(v3(RELF), v3(DF), bc(QC[:, 0, :].unsqueeze(2), [LT, LB, P]), ALU.subtract))
            tt(v3(RELQ), v3(DF), bc(QC[:, 1, :].unsqueeze(2), [LT, LB, P]), ALU.subtract).then_inc(s("relq_ready"), 1)
            step(dve.memset(MF, 0.0))
            step(dve.memset(MB, 0.0))
            step(tt(v3(MF)[:, :, 1:P], v3(DF)[:, :, 1:P], v3(DF)[:, :, 0:P - 1], ALU.is_equal))
            step(cp(v3(MB)[:, :, 0:P - 1], v3(MF)[:, :, 1:P]))
            step(ts(MFN, MF, BIG, -BIG, ALU.mult, ALU.add))
            step(ts(MBN, MB, BIG, -BIG, ALU.mult, ALU.add))
            step(cp(REP[:, 0, :, :], bc(v3(DF)[:, :, 0:1], [LT, LB, H])))
            cp(REP[:, 1, :, :], bc(v3(DF)[:, :, P - 1:P], [LT, LB, H])).then_inc(s("prep_ready"), 1)
            dve.wait_ge(s("prep_t"), 1)
            dve.wait_ge(s("const_ready"), 3)
            cp(IDXST[:, :], PS[:, 2, 0:T]).then_inc(s("idx_ready"), 1)
            cp(IDXS[:, :], PS[:, 1, 0:T]).then_inc(s("idx_ready"), 1)
            step(cp(DREL[:, 0:T], PS[:, 0, 0:T]))
            step(cp(DREL[:, T:T + 5], PS[:, 0, 0:5]))
            step(cp(BASE[:, :], PS[0:1, 4, 0:T]))
            step(cp(QR, PS[0:1, 5, 0:T]))
            mine(dve, tt(TM, bc(PS[:, 3, 0:T].unsqueeze(2), [P, T, R]), bc(IOTA[:, 0:R].unsqueeze(1), [P, T, R]),
                         ALU.is_equal), "prep_used", 1)
            def row_stats(of=X, ready=None):
                for t in range(NT):
                    if ready:
                        dve.wait_ge(s(ready), t + 1)
                    last = dve.bn_stats(XST[:, t, :], of[:, t, :])
                step(last)
                row_means()

            def row_means():
                for t in range(NT):
                    last = dve.bn_aggr(MV[:, t, :], XST[:, t, :])
                step(last)

            def norm_scale(l):
                dve.engine_nop().then_inc(s("norm_stats"), 1)
                dve.wait_ge(s("norm_sqrt"), l + 1)
                step(dve.reciprocal(RS[:, :], RS[:, :]))
                stt(out=NB[:, :], in0=MV[:, :, 0], scalar=-1.0, in1=RS[:, :], op0=ALU.mult, op1=ALU.mult)\
                    .then_inc(s("norm_scale"), 1)

            dve.wait_ge(s("x_in"), 32)
            row_stats()
            norm_scale(0)
            dve.wait_ge(s("conv_in"), 32)
            dve.wait_ge(s("attn_in"), 32)
            for c in range(2):
                for a in range(2):
                    step(tt(HT[:, 0, 0:R * D], WALL[:, c, :], ATT[:, a, :], ALU.mult))
                    step(dve.tensor_reduce(AW_[:, c, a * RH:(a + 1) * RH],
                                           HT[:, 0, 0:R * D].rearrange("p (r d) -> p r d", d=DH), AX, ALU.add))
            dve.wait_ge(s("small_in"), 16 * 15)
            step(dve.tensor_reduce(CSUM, ZR[:, 0, 0:2 * K].rearrange("p (c k) -> p c k", c=2), AX, ALU.add))
            cp(CSR, bc(CSUM.unsqueeze(2), [P, 2, P])).then_inc(s("aw_ready"), 1)
            def take_turned(l, t):
                dve.wait_ge(s(f"n{l}_tp"), t + 1)
                cp(HT[:, :, t * P:(t + 1) * P], PS[:, t % 4, 0:D].rearrange("p (c n) -> p c n", c=2))\
                    .then_inc(s(f"n{l}_ht"), 1)

            for t in range(NT):
                take_turned(0, t)
            dve.wait_ge(s("n0_ht"), NT)
            for q in range(4):
                n = min(8, NT - 8 * q)
                dve.wait_ge(s("elr_ps"), q + 1)
                v = PS[:, 4 + q, 0:n * 2 * RH].rearrange("p (t w r) -> p t w r", w=2, r=RH)
                cp(ELS[:, 8 * q:8 * q + n, :], v[:, :, 0, :]).then_inc(s("elr_done"), 1)
                cp(ER.rearrange("p (t r) -> p t r", r=RH)[:, 8 * q:8 * q + n, :], v[:, :, 1, :])\
                    .then_inc(s("elr_done"), 1)
            dve.wait_ge(s("elr_done"), 2 * 4)
            dve.wait_ge(s("cw_ps"), 1)
            cp(CW[:, :], PS[:, 6, 0:K]).then_inc(s("tab_free"), 4)
            for j in pairs(dve):
                for i in range(2):
                    t = 2 * j + i
                    dve.wait_ge(s("tab_ps"), 4 * t + 4)
                    mine(dve, cp(HTR[:, i, :, :], HT[:, :, bass.ds(t * P, P)]), "tab_in", t + 1)
                    dve.wait_ge(s(f"stage_out{i}"), 16 * (j + 1))
                    for q in range(4):
                        dve.wait_ge(s("tab_ps"), 4 * t + q + 9)
                        cp(STAGE[:, i, q * 512:(q + 1) * 512], PS[:, 4 + q, :]).then_inc(s("tab_free"), 1)
            er3 = ERB.rearrange("p (t a r) -> p t a r", a=3, r=RH)
            er1 = ER.rearrange("p (t r) -> p t r", r=RH)
            dve.wait_ge(s("tab_ps"), 4 * NT + 8)
            step(dve.memset(er3[:, NT:NT + 1, :, :], 0.0))
            for a in range(3):
                step(cp(er3[:, 0:NT, a, :], er1))
                if a < 2:
                    step(tt(er1, er1, er3[:, 0:NT, a, :], ALU.subtract))
            dve.engine_nop().then_inc(s("er_parts"), 1)
            dve.sem_inc(s("oht_ready"), 2)
            dve.sem_inc(s("er_done"), 2)

            def dst_one_hot(u, h):
                dve.wait_ge(s(f"rb_in{h}"), 16 * (u + 1))
                step(ts(OHT[:, h, 0, :], RB[:, h, :], IOTP[:, 0:1], None, ALU.is_equal))
                mine(dve, ts(OHT[:, h, 1, :], RB[:, h, :], IOTP[:, 1:2], None, ALU.is_equal), "oht_ready", 2 * u + h + 3)

            def er_step(u, more):
                for h in range(2):
                    dve.wait_ge(s("er_ps"), 2 * u + h + 1)
                    mine(dve, dve.tensor_reduce(
                        TMP[:, h, :].rearrange("p (k c) -> p k c", k=5),
                        PS[:, h, 0:15 * RH].rearrange("p (k a c) -> p k c a", k=5, a=3), AX, ALU.add),
                        "er_done", 2 * u + h + 3)
                    if more:
                        dst_one_hot(u + 1, h)
                tm = TMP.rearrange("p h (k c) -> p (h k c)", c=RH)
                step(tt(tm.rearrange("p (k h) -> p k h", h=H), tm.rearrange("p (k h) -> p k h", h=H),
                        bc(TM[:, bass.ds(10 * u, 10), :].rearrange("p k r -> p (k r)").unsqueeze(2), [P, 10 * R, H]),
                        ALU.mult))
                step(dve.tensor_reduce(AL[:, bass.ds(10 * u * H, 10 * H)].rearrange("p (k h) -> p k h", h=H),
                                       tm.rearrange("p (k r h) -> p k h r", k=10, h=H), AX, ALU.add))

            for h in range(2):
                dst_one_hot(0, h)
            with dve.Fori(0, IT - 1) as u:
                step.enter(u, 4)
                er_step(u, True)
                step.leave(IT - 1)
            er_step(IT - 1, False)
            dve.wait_ge(s("el_slots"), IT + 2)
            step(tt(AL[:, 0:T * H], AL[:, 0:T * H], ELA, ALU.add))
            stt(out=AL[:, 0:T * H], in0=AL[:, 0:T * H], scalar=0.2, in1=AL[:, 0:T * H], op0=ALU.mult, op1=ALU.max)\
                .then_inc(s("e_all"), 1)
            DFR, DLR, J, W, KF, KB, KFN, KBN, JN, SFR, SBR = ROWS[0:11]
            for i in range(2):
                dve.wait_ge(s(f"stage_out{i}"), 16 * (NJ + 1))
            dve.wait_ge(s("rep_ps"), 1)
            step(cp(DFR[:, 0:T], PS[0:H, 4, 0:T]))
            step(cp(DLR[:, 0:T], PS[0:H, 5, 0:T]))
            step(dve.memset(J, 0.0))
            step(tt(J[:, 1:T], DFR[:, 1:T], DLR[:, 0:T - 1], ALU.is_equal))
            step(tt(W[:, 0:T], DFR[:, 0:T], DLR[:, 0:T], ALU.is_equal))
            step(tt(KF[:, 0:T], W[:, 0:T], J[:, 0:T], ALU.mult))
            step(tt(KB[:, 0:T], W[:, 0:T], J[:, 1:T + 1], ALU.mult))
            step(ts(KFN[:, 0:T], KF[:, 0:T], BIG, -BIG, ALU.mult, ALU.add))
            step(ts(KBN[:, 0:T], KB[:, 0:T], BIG, -BIG, ALU.mult, ALU.add))
            step(ts(JN, J, BIG, -BIG, ALU.mult, ALU.add))

            v4 = lambda a: a.rearrange("t h (b e) -> t h b e", b=LB)

            def segment(r, op0, op1, none, mf, mb, kf, kb, jn):
                def scans():
                    for h in range(H):
                        step(dve.tensor_tensor_scan(FS[:, h, :], mf, EF[:, h, :], none, op0, op1))
                        step(dve.tensor_tensor_scan(BS[:, h, ::-1], mb[:, ::-1], EB[:, h, ::-1], none, op0, op1))

                scans()
                step(cp(QE[:, 0, :, :].rearrange("t b h -> t h b"), v4(FS)[:, :, :, P - 1]))
                cp(QE[:, 1, :, :].rearrange("t b h -> t h b"), v4(BS)[:, :, :, 0]).then_inc(s("ends"), 1)
                dve.wait_ge(s("ends_ps"), r + 1)
                step(dve.memset(SFR[:, 0:1], none))
                step(dve.memset(SBR[:, T:T + 1], none))
                step(dve.tensor_tensor_scan(SFR[:, 1:T + 1], kf[:, 0:T], PS[0:H, 6, 0:T], none, op0, op1))
                step(dve.tensor_tensor_scan(SBR[:, 0:T][:, ::-1], kb[:, 0:T][:, ::-1], PS[0:H, 7, 0:T][:, ::-1],
                                            none, op0, op1))
                step(tt(CF[:, 0:T], SFR[:, 0:T], jn[:, 0:T], op0))
                tt(CBK[:, 0:T], SBR[:, 1:T + 1], jn[:, 1:T + 1], op0).then_inc(s("carry"), 1)
                dve.wait_ge(s("carry_ps"), r + 1)
                c4 = PS[0:LT, 4:6, 0:LB * H].rearrange("t w (b h) -> t w h b", b=LB)
                step(tt(v4(EF)[:, :, :, 0], v4(EF)[:, :, :, 0], c4[:, 0], op1))
                step(tt(v4(EB)[:, :, :, P - 1], v4(EB)[:, :, :, P - 1], c4[:, 1], op1))
                scans()

            dve.wait_ge(s("e_sb"), 1)
            segment(0, ALU.add, ALU.max, -BIG, MFN, MBN, KFN, KBN, JN)
            step(tt(FS, FS, BS, ALU.max))
            tt(EX, PS[0:LT, 0:H, 0:LB * P], FS, ALU.subtract).then_inc(s("e_shift"), 1)
            dve.wait_ge(s("x_sb"), 2)
            segment(1, ALU.mult, ALU.add, 0.0, MF, MB, KF, KB, J)
            step(tt(FS, FS, BS, ALU.add))
            step(tt(FS, FS, EX, ALU.subtract))
            step(dve.reciprocal(FS, FS))
            tt(EX, EX, FS, ALU.mult).then_inc(s("alpha_t"), 1)
            dve.wait_ge(s("alpha_t"), 1)
            step(dve.memset(ACF[:, 8192:3 * AW], 0.0))
            dve.wait_ge(s("acc_zero"), 1)
            dve.sem_inc(s("added"), 10)

            def edge_adds(g, parts, planes, par=None, beside=None):
                def one_hot(u, h):
                    k = slice(5 * (h % 2), 5 * (h % 2) + 5)
                    mine(dve, tt(OH[:, k, :], bc(IOTA[:, :].unsqueeze(1), [P, 5, P]),
                                 bc(DREL[:, bass.ds(10 * u + 5 * h, 5)].unsqueeze(2), [P, 5, P]), ALU.is_equal),
                         "oh_ready", oh_count(g, u, h))

                def step_pair(w, beside=()):
                    for b in range(2):
                        u = 2 * w + b
                        one_hot(u, 1)
                        _, base = nc.values_load_multi_w_load_instructions(
                            BASE[:, bass.ds(10 * u, 10)], engines=[DVE], min_val=0, max_val=N,
                            skip_runtime_bounds_check_because="clamped to N when it was computed")
                        for k in range(10):
                            n = T * (g - 1) + 10 * u + k
                            dve.wait_ge(s("agg_ps"), n + 21)
                            dve.wait_ge(s("added"), n + 10)
                            a = ACC[0:parts, 0:planes, bass.ds(base[k], P)]
                            tt(a, a, PS[0:parts, k % 2, 0:planes * P].rearrange("p (a n) -> p a n", a=planes),
                               ALU.add).then_inc(s("added"), 1)
                            if (b, k) in beside:
                                beside[b, k](w)
                            for what, kk in EDGE_ORDER[k] if par is not None else []:
                                if what == "sum":
                                    m = 5 * (IT * par + u) + kk
                                    dve.wait_ge(s("hs_ps"), m + 1)
                                    dve.wait_ge(s("hs_added"), m + 1)
                                    a = HS[:, :, bass.ds(base[2 * kk + par], P)]
                                    hv = PS[:, 7 - 4 * (kk % 2), 0:D].rearrange("p (a n) -> p a n", a=2)
                                    tt(a, a, hv, ALU.add).then_inc(s("hs_added"), 1)
                            if k == 6:
                                one_hot(u, 2)

                one_hot(0, 0)
                if beside:
                    with dve.Fori(0, NJ) as w:
                        step_pair(w, beside)
                with dve.Fori(NJ if beside else 0, IL) as w:
                    step_pair(w)
                dve.wait_ge(s("added"), T * g + 10)

            edge_adds(1, P, 3)
            dve.wait_ge(s("hb_in"), 16)
            for t in range(NT + 1):
                if t < NT:
                    dve.wait_ge(s("f0_tp"), t + 1)
                    tt(X[:, t, :], X[:, t, :], PS[:, t % 2, 0:D], ALU.add).then_inc(s("f0_x"), 1)
                    cp(DG[:, t:t + 1], PS[:, t % 2, D:D + 1]).then_inc(s("f0_done"), 1)
                if t >= 1:
                    dve.wait_ge(s("f0_b"), t)
                    last = dve.bn_stats(XST[:, t - 1, :], X[:, t - 1, :])
                if t < NT:
                    dve.wait_ge(s("f0_x"), t + 1)
                    tt(X[:, t, :], X[:, t, :], HB, ALU.add).then_inc(s("f0_b"), 1)
            step(last)
            row_means()
            dve.wait_ge(s("dg_sqrt"), 1)
            step(dve.reciprocal(DG[:, :], DG[:, :]))
            norm_scale(1)
            for t in range(NT):
                take_turned(1, t)
                tt(X[:, t, :], X[:, t, :], SL[:, t % 10, :], ALU.add).then_inc(s("n1_used"), 1)
            dve.wait_ge(s("n1_used"), NT)
            dve.wait_ge(s("n1_ps"), 1)
            step(tt(Y, PS[:, 4, 0:NT * K].rearrange("p (t k) -> p t k", k=K), bc(CW[:, :].unsqueeze(1), [P, NT, K]),
                    ALU.add))
            tt(Y, Y, bc(DG[:, :].unsqueeze(2), [P, NT, K]), ALU.mult).then_inc(s("y_ready"), 1)
            dve.wait_ge(s("y_ready"), 1)
            step(dve.memset(ACC[0:K, 0, :], 0.0))
            step(dve.memset(HS[:, :, :], 0.0))
            step(dve.memset(EAT[ED:ED + 1, :], 1.0))
            dve.wait_ge(s("cb2_ps"), 1)
            step(tt(CB2, PS[:, 6, 0:2], B2C, ALU.add))
            step(ts(SC2, SC2, 2.0, None, ALU.add))
            dve.sem_inc(s("hs_added"), 1)
            edge_adds(2, K, 1, par=0)
            dve.wait_ge(s("f1_tp"), 1)
            step(tt(Z, PS[:, 0, 0:NT * K].rearrange("p (t k) -> p t k", k=K), Y, ALU.add))
            step(tt(Z, Z, bc(DG[:, :].unsqueeze(2), [P, NT, K]), ALU.mult))
            step(tt(Z, Z, bc(GB[:, :].unsqueeze(1), [P, NT, K]), ALU.add))
            step(dve.tensor_reduce(ZM, Z, AX, ALU.max))
            tt(Z, Z, bc(ZM.unsqueeze(2), [P, NT, K]), ALU.subtract).then_inc(s("z_shift"), 1)
            dve.wait_ge(s("z_exp"), 1)
            step(dve.tensor_reduce(ZM, Z, AX, ALU.add))
            step(dve.reciprocal(ZM, ZM))
            tt(Z, Z, bc(ZM.unsqueeze(2), [P, NT, K]), ALU.mult).then_inc(s("z_soft"), 1)
            for t in range(NT + 1):
                if t < NT:
                    dve.wait_ge(s("g1_mm"), t + 1)
                    tt(X[:, t, :], X[:, t, :], PS[:, 4 + t % 4, 0:D], ALU.add).then_inc(s("g1_done"), 1)
                if t >= 1:
                    dve.wait_ge(s("g1_done"), t)
                    last = dve.bn_stats(XST[:, t - 1, :], X[:, t - 1, :])
            step(last)
            row_means()
            norm_scale(2)
            for t in range(NT):
                dve.wait_ge(s("n2_tp"), t + 1)
                for c in range(2):
                    last = ts(ACC[:, c, t * P:(t + 1) * P], PS[:, t % 4, c * P:(c + 1) * P], SC2, CB2[:, c:c + 1],
                              ALU.mult, ALU.add)
                last.then_inc(s("n2_ht"), 1)
            dve.wait_ge(s("n2_ht"), NT)
            for c in range(2):
                step(stt(out=ACC[:, c, 0:NPAD], in0=ACC[:, 2, 0:NPAD], scalar=B2C[:, c:c + 1], in1=ACC[:, c, 0:NPAD],
                         op0=ALU.mult, op1=ALU.add))
            step(dve.memset(ACC[:, 0:2, NPAD:AW], 0.0))
            edge_adds(3, P, 2, par=1)
            dve.wait_ge(s("mlp_in"), 16 * 6)
            dve.wait_ge(s("hs_added"), T + 1)
            for i in range(2):
                dve.sem_inc(s(f"m_out{i}"), 1)
                dve.sem_inc(s(f"h2r_free{i}"), 1)

            def scalars(m, i, name, n):
                dve.wait_ge(s(name), n)
                step(dve.reciprocal(m[:, i, 3:4], m[:, i, 2:3]))
                return stt(out=m[:, i, 4:5], in0=m[:, i, 0:1], scalar=-1.0, in1=m[:, i, 3:4],
                           op0=ALU.mult, op1=ALU.mult)

            def dense_in(i, j):
                dve.wait_ge(s(f"m_ee{i}"), j + 1)
                mine(dve, tt(HIN[:, i, :, :], ACC[:, 0:2, bass.ds((2 * j + i) * P, P)],
                             PS[:, 2 * i, 0:D].rearrange("p (c n) -> p c n", c=2), ALU.add), f"m_hin{i}", j + 1)

            def hidden_stats(i, j, l):
                n = 2 * j + l + 1
                dve.wait_ge(s(f"m_ps{i}"), n)
                step(tt(ZR[:, i, :], PS[:, 2 * i:2 * i + 2, :].rearrange("p a n -> p (a n)"), BR[l], ALU.add))
                dve.nop(nofuse=True)
                dve.bn_stats(STAT[:, i, 0:6], ZR[:, i, 0:512])
                step(dve.bn_stats(STAT[:, i, 6:12], ZR[:, i, 512:1024]))
                dve.nop(nofuse=True)
                mine(dve, dve.bn_aggr(SM[:, i, 0:2], STAT[:, i, 0:12]), f"m_var{i}", n)
                mine(dve, scalars(SM, i, f"m_sqrt{i}", n), f"m_scale{i}", n)

            def dense_out(i, j):
                dve.wait_ge(s(f"m_y{i}"), j + 1)
                dve.wait_ge(s(f"h2r_in{i}"), 16 * (j + 1))
                yr = HTR[:, i, :, :].rearrange("p c n -> p (c n)")
                mine(dve, tt(yr, PS[:, 4 + 2 * i, 0:D], B3R, ALU.add), f"m_out{i}", j + 2)
                mine(dve, tt(yr, yr, H2R[:, i, :], ALU.add), f"h2r_free{i}", j + 2)
                dve.nop(nofuse=True)
                step(dve.bn_stats(STAT[:, i, 0:6], yr))
                dve.nop(nofuse=True)
                mine(dve, dve.bn_aggr(YM[:, i, 0:2], STAT[:, i, 0:6]), f"y_var{i}", j + 1)
                step(scalars(YM, i, f"y_sqrt{i}", j + 1))
                step(ts(yr, yr, YM[:, i, 3:4], YM[:, i, 4:5], ALU.mult, ALU.add))
                step(tt(yr, yr, GNR, ALU.mult))
                step(tt(yr, yr, BNR, ALU.add))
                xt = X[:, bass.ds(2 * j + i, 1), :].rearrange("p a d -> p (a d)")
                step(stt(out=xt, in0=yr, scalar=0.0, in1=xt, op0=ALU.max, op1=ALU.add))

            def mean_factor(j):
                a = ACC[:, 2:3, bass.ds(2 * j * P, 2 * P)]
                step(ts(a, a, 1.0, None, ALU.max))
                dve.nop(nofuse=True)
                step(dve.reciprocal(a, a))

            def dense_pair(j, more):
                hidden_stats(1, j, 0)
                mean_factor(j)
                hidden_stats(0, j, 1)
                if more:
                    dense_in(0, j + 1)
                hidden_stats(1, j, 1)
                if more:
                    hidden_stats(0, j + 1, 0)
                    dense_in(1, j + 1)
                dense_out(0, j)
                dense_out(1, j)

            for i in range(2):
                dense_in(i, 0)
            hidden_stats(0, 0, 0)
            dve.wait_ge(s("mlp_late"), 32)
            with dve.Fori(0, NJ - 1) as j:
                step.enter(j, 4 * 3 + 2 * 7 + 2)
                dense_pair(j, True)
                step.leave(NJ - 1)
            dense_pair(NJ - 1, False)
            row_stats()
            norm_scale(3)
            dve.wait_ge(s("w3_ps"), 1)
            for w in range(2):
                cp(WLR[:, w, :, :].rearrange("p c n -> p (c n)"), PS[:, 2 + w, :]).then_inc(s("w3_sb"), 1)
            row_stats(HALL, "n3_in")
            norm_scale(4)
            for q in range(NT // 5):
                dve.wait_ge(s("n3_z"), 5 * q + 5)
                v = HALL[:, 5 * q:5 * q + 5, :]
                step(tt(v, v, bc(GMR.unsqueeze(1), [P, 5, D]), ALU.mult))
                step(tt(v, v, bc(BTR.unsqueeze(1), [P, 5, D]), ALU.add))
                mine(dve, ts(v, v, 0.0, None, ALU.max), "h3_rows", q + 1)
            dve.wait_ge(s("acc_zero"), 2)
            dve.sem_inc(s("n3_done"), 2)

            def self_columns(j):
                for i in range(2):
                    t = 2 * j + i
                    dve.wait_ge(s("n3_tp"), t + 3)
                    mine(dve, cp(HTR[:, i, :, :], PS[:, 2 + i, 0:D].rearrange("p (c n) -> p c n", c=2)), "n3_ht", t + 1)

            def self_add(j):
                for i in range(2):
                    t = 2 * j + i
                    dve.wait_ge(s("n3_ps"), t + 1)
                    xt = X[:, bass.ds(t, 1), :].rearrange("p a d -> p (a d)")
                    mine(dve, tt(xt, xt, PS[:, 4 + i, 0:D], ALU.add), "n3_done", t + 3)
                    mine(dve, tt(xt, xt, BLR, ALU.add), "n3_x", t + 1)

            edge_adds(4, P, 2, beside={(0, 5): self_columns, (1, 2): self_add})
            for q in range(NT // 5 + 1):
                if q < NT // 5:
                    v = ACC[:, :, 5 * q * P:5 * (q + 1) * P]
                    tt(v[:, 0:2], v[:, 0:2], bc(v[:, 2:3], [P, 2, 5 * P]), ALU.mult).then_inc(s("o_mean"), 1)
                if q >= 1:
                    for t in range(5 * q - 5, 5 * q):
                        dve.wait_ge(s("o_ps"), t + 1)
                        tt(X[:, t, :], X[:, t, :], PS[:, t % 8, 0:D], ALU.add).then_inc(s("o_ready"), 1)


_INS = ['x', 'src', 'dst', 'edge_attr_64', 'edge_type_8', 'L0_gnn_conv_weights', 'L0_gnn_attn_l', 'L0_gnn_attn_r',
        'L0_gnn_h_bias', 'L1_gnn_W', 'L1_gnn_bias', 'L1_gnn_cluster_emb', 'L2_gnn_eps', 'L2_gnn_ee_w1', 'L2_gnn_ee_b1',
        'L2_gnn_ee_w2', 'L2_gnn_ee_b2', 'L2_gnn_w1', 'L2_gnn_b1', 'L2_gnn_g1', 'L2_gnn_be1', 'L2_gnn_w2', 'L2_gnn_b2',
        'L2_gnn_g2', 'L2_gnn_be2', 'L2_gnn_w3', 'L2_gnn_b3', 'L2_gnn_bn_g', 'L2_gnn_bn_b', 'L3_gnn_gamma',
        'L3_gnn_beta', 'L3_gnn_W_l', 'L3_gnn_b_l', 'L3_gnn_W_r']
_OUTS = [((3750, 256), 'float32')]


def kernel(**inputs):
    import numpy as _np
    import concourse.bacc as _bacc
    from concourse import mybir as _mybir
    from concourse.bass_utils import run_bass_kernel_spmd as _run

    nc = _bacc.Bacc("TRN2", target_bir_lowering=False, num_devices=1)
    arrays, args = {}, []
    for name in _INS:
        a = _np.ascontiguousarray(inputs[name]).reshape(_np.shape(inputs[name]) or (1,))
        arrays[f"in_{name}_dram"] = a
        args.append(nc.dram_tensor(f"in_{name}_dram", a.shape, _mybir.dt.from_np(a.dtype), kind="ExternalInput").ap())
    for i, (shape, dtype) in enumerate(_OUTS):
        dt = _mybir.dt.from_np(_np.dtype(dtype))
        args.append(nc.dram_tensor(f"out_{i}_dram", shape, dt, kind="ExternalOutput").ap())
    gnn(nc, *args)
    r = _run(nc, [arrays], core_ids=[0])
    got = tuple(r.results[0][f"out_{i}_dram"] for i in range(len(_OUTS)))
    return got[0]
```
